# Optimizing a Trainium2 kernel written in Bass

```python
import numpy as np
import jax
import jax.numpy as jnp

def _softmax(x, axis=-1):
    return jax.nn.softmax(x, axis=axis)

def _gelu(x):
    return jax.nn.gelu(x, approximate=True)

def _silu(x):
    return jax.nn.silu(x)

def _sigmoid(x):
    return jax.nn.sigmoid(x)

def _layernorm(x, axis=-1, eps=1e-05):
    m = jnp.mean(x, axis=axis, keepdims=True)
    v = jnp.var(x, axis=axis, keepdims=True)
    return (x - m) / jnp.sqrt(v + eps)

def _scatter_add(tgt, idx, src, axis=0):
    return tgt.at[idx].add(src)

def _segment_sum(src, seg, n):
    return jax.ops.segment_sum(src, seg, n)
kernel_name = 'mk_sandwich_d1_jaxref_r8_8942dd'

def setup_inputs(seed: int=0):
    np.random.seed(seed)
    _w = jnp.asarray

    def _L0_attn_setup():
        import jax, jax.numpy as jnp
        import numpy as np
        import math
        HIDDEN = 128
        HEADS = 16
        HEAD_DIM = HIDDEN // HEADS
        NUM_FEATURES = 64
        B, N = (4, 512)

        def _feature_map(x, rf):
            proj = jnp.einsum('bhnd,fd->bhnf', x, rf) / jnp.sqrt(jnp.float32(NUM_FEATURES))
            norm = jnp.linalg.norm(x, axis=-1, keepdims=True)
            return jnp.exp(proj - norm)
        key = jax.random.key(seed)
        ks = jax.random.split(key, 5)
        x = jax.random.normal(ks[0], (B, N, HIDDEN), dtype=jnp.float32)
        w_qkv = jax.random.normal(ks[1], (3 * HIDDEN, HIDDEN), dtype=jnp.float32) / math.sqrt(HIDDEN)
        w_out = jax.random.normal(ks[2], (HIDDEN, HIDDEN), dtype=jnp.float32) / math.sqrt(HIDDEN)
        b_out = jnp.zeros((HIDDEN,), dtype=jnp.float32)
        random_features = jax.random.normal(ks[3], (NUM_FEATURES, HEAD_DIM), dtype=jnp.float32)
        return {'x': x, 'w_qkv': w_qkv, 'w_out': w_out, 'b_out': b_out, 'random_features': random_features}
    _L0_attn_in = _L0_attn_setup()

    def _L0_ffn_setup():
        import jax, jax.numpy as jnp
        import numpy as np
        DIM = 128
        DEPTH = 2
        HEADS = 8
        DIM_HEAD = 64
        WINDOW = 64
        INNER = HEADS * DIM_HEAD
        HID = int(DIM * 4 * 2 / 3)
        B, N = (2, 1024)
        QK_SCALE = 8.0

        def shift_token(t):
            t1, t2 = jnp.split(t, 2, axis=-1)
            t2 = jnp.pad(t2, ((0, 0), (1, 0), (0, 0)))[:, :-1]
            return jnp.concatenate([t1, t2], axis=-1)

        def l2norm(t):
            return t / jnp.clip(jnp.linalg.norm(t, axis=-1, keepdims=True), 1e-12)

        def rotate_half(x):
            x1, x2 = jnp.split(x, 2, axis=-1)
            return jnp.concatenate([-x2, x1], axis=-1)

        def rotary_xpos(q, k):
            n = q.shape[-2]
            half_idx = jnp.arange(0, DIM_HEAD, 2, dtype=jnp.float32)
            inv_freq = 1.0 / 10000.0 ** (half_idx / DIM_HEAD)
            t = jnp.arange(n, dtype=jnp.float32)
            freqs = t[:, None] * inv_freq[None, :]
            freqs = jnp.concatenate([freqs, freqs], axis=-1)
            base = (half_idx + 0.4 * DIM_HEAD) / (1.4 * DIM_HEAD)
            power = (t - n // 2) / float(WINDOW // 2)
            scale = base[None, :] ** power[:, None]
            scale = jnp.concatenate([scale, scale], axis=-1)
            cos, sin = (jnp.cos(freqs), jnp.sin(freqs))
            q = q * cos * scale + rotate_half(q) * sin * scale
            k = k * cos / scale + rotate_half(k) * sin / scale
            return (q, k)

        def local_attention(q, k, v):
            b, h, n, d = q.shape
            w = n // WINDOW
            bq = q.reshape(b, h, w, WINDOW, d) * QK_SCALE
            bk = k.reshape(b, h, w, WINDOW, d)
            bv = v.reshape(b, h, w, WINDOW, d)

            def look_around(t):
                p = jnp.pad(t, ((0, 0), (0, 0), (1, 0), (0, 0), (0, 0)))
                return jnp.concatenate([p[:, :, :w], p[:, :, 1:]], axis=3)
            bk, bv = (look_around(bk), look_around(bv))
            bt = jnp.arange(n).reshape(w, WINDOW)
            btp = jnp.pad(bt, ((1, 0), (0, 0)), constant_values=-1)
            btk = jnp.concatenate([btp[:w], btp[1:]], axis=1)
            sim = jnp.einsum('bhwid,bhwjd->bhwij', bq, bk)
            i = bt[:, :, None]
            j = btk[:, None, :]
            mask = (i < j) | (i > j + WINDOW) | (j == -1)
            sim = jnp.where(mask, -jnp.finfo(sim.dtype).max, sim)
            attn = jax.nn.softmax(sim, axis=-1)
            out = jnp.einsum('bhwij,bhwjd->bhwid', attn, bv)
            return out.reshape(b, h, n, d)

        def _layer(x, wqkv, qs, ksc, wo, lg, lb, w1, b1, w2, b2):
            b, n, _ = x.shape
            h = shift_token(x)
            qkv = h @ wqkv
            q, k, v = jnp.split(qkv, 3, axis=-1)
            to_heads = lambda t: t.reshape(b, n, HEADS, DIM_HEAD).transpose(0, 2, 1, 3)
            q, k, v = (to_heads(q), to_heads(k), to_heads(v))
            q = l2norm(q) * qs
            k = l2norm(k) * ksc
            q, k = rotary_xpos(q, k)
            o = local_attention(q, k, v)
            o = o.transpose(0, 2, 1, 3).reshape(b, n, INNER)
            x = x + o @ wo
            h = shift_token(x)
            mu = h.mean(-1, keepdims=True)
            var = h.var(-1, keepdims=True)
            h = (h - mu) / jnp.sqrt(var + 1e-05) * lg + lb
            h = h @ w1 + b1
            a, g = jnp.split(h, 2, axis=-1)
            h = a * jax.nn.gelu(g, approximate=False)
            x = x + h @ w2 + b2
            return x
        key = jax.random.key(seed)
        ks = jax.random.split(key, 6)
        return {'x': jax.random.normal(ks[0], (B, N, DIM), jnp.float32), 'wqkv': jax.random.normal(ks[1], (DEPTH, DIM, 3 * INNER), jnp.float32) * 0.02, 'q_scale': jnp.ones((DEPTH, DIM_HEAD), jnp.float32), 'k_scale': jnp.ones((DEPTH, DIM_HEAD), jnp.float32), 'wo': jax.random.normal(ks[2], (DEPTH, INNER, DIM), jnp.float32) * 0.02, 'ln_g': jnp.ones((DEPTH, DIM), jnp.float32), 'ln_b': jnp.zeros((DEPTH, DIM), jnp.float32), 'w1': jax.random.normal(ks[3], (DEPTH, DIM, 2 * HID), jnp.float32) * 0.02, 'b1': jnp.zeros((DEPTH, 2 * HID), jnp.float32), 'w2': jax.random.normal(ks[4], (DEPTH, HID, DIM), jnp.float32) * 0.02, 'b2': jnp.zeros((DEPTH, DIM), jnp.float32)}
    _L0_ffn_in = _L0_ffn_setup()
    _d = {'L0_attn_x': _L0_attn_in['x'], 'L0_attn_w_qkv': _L0_attn_in['w_qkv'], 'L0_attn_w_out': _L0_attn_in['w_out'], 'L0_attn_b_out': _L0_attn_in['b_out'], 'L0_attn_random_features': _L0_attn_in['random_features'], 'L0_ffn_wqkv': _L0_ffn_in['wqkv'], 'L0_ffn_q_scale': _L0_ffn_in['q_scale'], 'L0_ffn_k_scale': _L0_ffn_in['k_scale'], 'L0_ffn_wo': _L0_ffn_in['wo'], 'L0_ffn_ln_g': _L0_ffn_in['ln_g'], 'L0_ffn_ln_b': _L0_ffn_in['ln_b'], 'L0_ffn_w1': _L0_ffn_in['w1'], 'L0_ffn_b1': _L0_ffn_in['b1'], 'L0_ffn_w2': _L0_ffn_in['w2'], 'L0_ffn_b2': _L0_ffn_in['b2']}
    _x0 = _d['L0_attn_x']
    _d['L0_attn_x'] = jax.random.normal(jax.random.fold_in(jax.random.key(seed), 1), (32, 256, 128), dtype=_x0.dtype)
    del _x0
    return _d

def reference(L0_attn_x, L0_attn_w_qkv, L0_attn_w_out, L0_attn_b_out, L0_attn_random_features, L0_ffn_wqkv, L0_ffn_q_scale, L0_ffn_k_scale, L0_ffn_wo, L0_ffn_ln_g, L0_ffn_ln_b, L0_ffn_w1, L0_ffn_b1, L0_ffn_w2, L0_ffn_b2):

    def _L0_attn_ref(x, w_qkv, w_out, b_out, random_features):
        import jax, jax.numpy as jnp
        import numpy as np
        import math
        HIDDEN = 128
        HEADS = 16
        HEAD_DIM = HIDDEN // HEADS
        NUM_FEATURES = 64
        B, N = (4, 512)

        def _feature_map(x, rf):
            proj = jnp.einsum('bhnd,fd->bhnf', x, rf) / jnp.sqrt(jnp.float32(NUM_FEATURES))
            norm = jnp.linalg.norm(x, axis=-1, keepdims=True)
            return jnp.exp(proj - norm)
        b, n, _ = x.shape
        qkv = jnp.einsum('bnh,oh->bno', x, w_qkv)
        qkv = qkv.reshape(b, n, 3, HEADS, HEAD_DIM)
        qkv = jnp.transpose(qkv, (2, 0, 3, 1, 4))
        q, k, v = (qkv[0], qkv[1], qkv[2])
        q_prime = _feature_map(q, random_features)
        k_prime = _feature_map(k, random_features)
        kv = jnp.einsum('bhnf,bhnd->bhfd', k_prime, v)
        normalizer = jnp.einsum('bhnf,bhf->bhn', q_prime, k_prime.sum(axis=2))
        out = jnp.einsum('bhnf,bhfd->bhnd', q_prime, kv)
        out = out / (normalizer[..., None] + 1e-06)
        out = jnp.transpose(out, (0, 2, 1, 3)).reshape(b, n, HIDDEN)
        return jnp.einsum('bnh,oh->bno', out, w_out) + b_out

    def _L0_ffn_ref(x, wqkv, q_scale, k_scale, wo, ln_g, ln_b, w1, b1, w2, b2):
        import jax, jax.numpy as jnp
        import numpy as np
        DIM = 128
        DEPTH = 2
        HEADS = 8
        DIM_HEAD = 64
        WINDOW = 64
        INNER = HEADS * DIM_HEAD
        HID = int(DIM * 4 * 2 / 3)
        B, N = (2, 1024)
        QK_SCALE = 8.0

        def shift_token(t):
            t1, t2 = jnp.split(t, 2, axis=-1)
            t2 = jnp.pad(t2, ((0, 0), (1, 0), (0, 0)))[:, :-1]
            return jnp.concatenate([t1, t2], axis=-1)

        def l2norm(t):
            return t / jnp.clip(jnp.linalg.norm(t, axis=-1, keepdims=True), 1e-12)

        def rotate_half(x):
            x1, x2 = jnp.split(x, 2, axis=-1)
            return jnp.concatenate([-x2, x1], axis=-1)

        def rotary_xpos(q, k):
            n = q.shape[-2]
            half_idx = jnp.arange(0, DIM_HEAD, 2, dtype=jnp.float32)
            inv_freq = 1.0 / 10000.0 ** (half_idx / DIM_HEAD)
            t = jnp.arange(n, dtype=jnp.float32)
            freqs = t[:, None] * inv_freq[None, :]
            freqs = jnp.concatenate([freqs, freqs], axis=-1)
            base = (half_idx + 0.4 * DIM_HEAD) / (1.4 * DIM_HEAD)
            power = (t - n // 2) / float(WINDOW // 2)
            scale = base[None, :] ** power[:, None]
            scale = jnp.concatenate([scale, scale], axis=-1)
            cos, sin = (jnp.cos(freqs), jnp.sin(freqs))
            q = q * cos * scale + rotate_half(q) * sin * scale
            k = k * cos / scale + rotate_half(k) * sin / scale
            return (q, k)

        def local_attention(q, k, v):
            b, h, n, d = q.shape
            w = n // WINDOW
            bq = q.reshape(b, h, w, WINDOW, d) * QK_SCALE
            bk = k.reshape(b, h, w, WINDOW, d)
            bv = v.reshape(b, h, w, WINDOW, d)

            def look_around(t):
                p = jnp.pad(t, ((0, 0), (0, 0), (1, 0), (0, 0), (0, 0)))
                return jnp.concatenate([p[:, :, :w], p[:, :, 1:]], axis=3)
            bk, bv = (look_around(bk), look_around(bv))
            bt = jnp.arange(n).reshape(w, WINDOW)
            btp = jnp.pad(bt, ((1, 0), (0, 0)), constant_values=-1)
            btk = jnp.concatenate([btp[:w], btp[1:]], axis=1)
            sim = jnp.einsum('bhwid,bhwjd->bhwij', bq, bk)
            i = bt[:, :, None]
            j = btk[:, None, :]
            mask = (i < j) | (i > j + WINDOW) | (j == -1)
            sim = jnp.where(mask, -jnp.finfo(sim.dtype).max, sim)
            attn = jax.nn.softmax(sim, axis=-1)
            out = jnp.einsum('bhwij,bhwjd->bhwid', attn, bv)
            return out.reshape(b, h, n, d)

        def _layer(x, wqkv, qs, ksc, wo, lg, lb, w1, b1, w2, b2):
            b, n, _ = x.shape
            h = shift_token(x)
            qkv = h @ wqkv
            q, k, v = jnp.split(qkv, 3, axis=-1)
            to_heads = lambda t: t.reshape(b, n, HEADS, DIM_HEAD).transpose(0, 2, 1, 3)
            q, k, v = (to_heads(q), to_heads(k), to_heads(v))
            q = l2norm(q) * qs
            k = l2norm(k) * ksc
            q, k = rotary_xpos(q, k)
            o = local_attention(q, k, v)
            o = o.transpose(0, 2, 1, 3).reshape(b, n, INNER)
            x = x + o @ wo
            h = shift_token(x)
            mu = h.mean(-1, keepdims=True)
            var = h.var(-1, keepdims=True)
            h = (h - mu) / jnp.sqrt(var + 1e-05) * lg + lb
            h = h @ w1 + b1
            a, g = jnp.split(h, 2, axis=-1)
            h = a * jax.nn.gelu(g, approximate=False)
            x = x + h @ w2 + b2
            return x
        for l in range(DEPTH):
            x = _layer(x, wqkv[l], q_scale[l], k_scale[l], wo[l], ln_g[l], ln_b[l], w1[l], b1[l], w2[l], b2[l])
        return x
    x = L0_attn_x
    x = x + _layernorm(_L0_attn_ref(_layernorm(x, axis=-1), L0_attn_w_qkv, L0_attn_w_out, L0_attn_b_out, L0_attn_random_features), axis=-1)
    x = x + _layernorm(_L0_ffn_ref(_layernorm(x, axis=-1), L0_ffn_wqkv, L0_ffn_q_scale, L0_ffn_k_scale, L0_ffn_wo, L0_ffn_ln_g, L0_ffn_ln_b, L0_ffn_w1, L0_ffn_b1, L0_ffn_w2, L0_ffn_b2), axis=-1)
    return x

_drawn_inputs = setup_inputs


def setup_inputs(seed=0):
    import zlib

    import numpy as np

    out = dict(_drawn_inputs(seed))
    spreads = {'L0_attn_b_out': (0.0, 0.1),
     'L0_ffn_q_scale': (1.0, 0.6),
     'L0_ffn_k_scale': (1.0, 0.6),
     'L0_ffn_ln_g': (1.0, 0.6),
     'L0_ffn_ln_b': (0.0, 0.8),
     'L0_ffn_b1': (0.0, 0.8),
     'L0_ffn_b2': (0.0, 0.8)}
    factors = {'L0_attn_random_features': 2.945, 'L0_ffn_w1': 7.457, 'L0_ffn_w2': 7.292}
    for name, (base, spread) in spreads.items():
        noise = np.random.default_rng([zlib.crc32(name.encode()), seed]).standard_normal(out[name].shape)
        drawn = base * np.exp(spread * noise) if base else spread * noise
        out[name] = jnp.asarray(drawn.astype(out[name].dtype))
    for name, factor in factors.items():
        out[name] = (out[name] * factor).astype(out[name].dtype)
    return out
```

```python
from contextlib import ExitStack

import numpy as np

import concourse.bass as bass
from concourse import mybir

F32 = mybir.dt.float32
BF16 = mybir.dt.bfloat16
ALU = mybir.AluOpType
ACT = mybir.ActivationFunctionType
AX = mybir.AxisListType

P = 128
TPB = 2
ROWS = 257
HEADS_A, DIM_A, FEAT = 16, 8, 64
GH = 8
HEADS, DH, WIN = 8, 64, 64
UH = 4
EPS_LN, EPS_A = 1e-5, 1e-6
MASKED = -2.0 ** 100


def rotary_tables(tokens):
    half = np.arange(0, DH, 2, dtype=np.float32)
    inv = (1.0 / np.power(np.float32(10000.0), half / np.float32(DH))).astype(np.float32)
    t = np.arange(tokens, dtype=np.float32)
    fr = t[:, None] * inv[None, :]
    fr = np.concatenate([fr, fr], -1).astype(np.float64)
    base = (half + np.float32(0.4 * DH)) / np.float32(1.4 * DH)
    power = (t - tokens // 2) / np.float32(WIN // 2)
    sc = np.power(base[None, :].astype(np.float64), power[:, None].astype(np.float64))
    sc = np.concatenate([sc, sc], -1)
    sign = np.concatenate([-np.ones(DH // 2), np.ones(DH // 2)])[None, :]
    tabs = [np.cos(fr) * sc * 8.0, sign * np.sin(fr) * sc * 8.0, np.cos(fr) / sc, sign * np.sin(fr) / sc]
    out = np.stack(tabs).astype(np.float32)
    return np.ascontiguousarray(out.reshape(4, tokens // P, P, DH).transpose(2, 0, 1, 3).reshape(P, -1))


def window_masks():
    i = np.arange(WIN)[:, None]
    j = np.arange(WIN)[None, :]
    own = np.where(i < j, MASKED, 0.0)
    before = np.where(i > j, MASKED, 0.0)
    odd = np.concatenate([before, own], 1)
    even = np.concatenate([own, before], 1)
    first = np.concatenate([own, np.full((WIN, WIN), MASKED)], 1)
    both = [np.concatenate([first, odd], 0), np.concatenate([even, odd], 0)]
    return np.ascontiguousarray(np.stack([np.tile(m, (1, UH)) for m in both], 1).astype(np.float32).reshape(P, -1))


def norm_rows():
    neg = np.zeros((72, GH * FEAT), np.float32)
    ones = np.zeros((64, GH), np.float32)
    for h in range(GH):
        neg[64 + h, h * FEAT:(h + 1) * FEAT] = -1.0
        ones[h * DIM_A:(h + 1) * DIM_A, h] = 1.0
    return neg, ones


def build(nc, x, w_qkv, w_out, b_out, rf, wqkv, q_scale, k_scale, wo, ln_g, ln_b, w1, b1, w2, b2, out,
          upto=5):
    B, N, D = x.shape
    assert N == TPB * P and D == P
    L, _, QKV = wqkv.shape
    INNER = QKV // 3
    HID = w2.shape[1]
    HC = (HID + P - 1) // P
    HW = [min(P, HID - c * P) for c in range(HC)]

    tabs_np = rotary_tables(N)
    mask_np = window_masks()
    neg_np, ones_np = norm_rows()
    tabs_c = nc.inline_tensor(tabs_np, name="rotary_tables")
    mask_c = nc.inline_tensor(mask_np, name="window_masks")
    neg_c = nc.inline_tensor(neg_np, name="norm_rows")
    ones_c = nc.inline_tensor(ones_np, name="head_ones")

    with ExitStack() as ctx:
        def sb(name, shape, dt=F32):
            return ctx.enter_context(nc.sbuf_tensor(name, shape, dt))

        def sem(name):
            return ctx.enter_context(nc.semaphore(name))

        x1_d = nc.dram_tensor("x1_d", [B, N, D], F32, kind="Internal").ap()
        y_d = [nc.dram_tensor(f"y{n}_d", [B, ROWS, D], F32, kind="Internal").ap() for n in range(2 * L)]

        ident = sb("ident", [P, P])
        ident_b = sb("ident_b", [P, P], BF16)
        zrow = sb("zrow", [B, D])
        half_neg = sb("half_neg", [P, 16])
        half_pos = sb("half_pos", [P, 1024])
        tabs = sb("tabs", [P, 4, TPB, DH])
        masks_f = sb("masks_f", [P, TPB, UH * P])
        masks = sb("masks", [P, TPB, UH * P], BF16)
        rfa = sb("rfa", [72, GH * FEAT])
        rfb = sb("rfb", [72, GH * FEAT])
        rfn = sb("rfn", [72, GH * FEAT])
        hones = sb("hones", [64, GH])
        wq_raw = sb("wq_raw", [P, 4, P])
        wT = sb("wT", [P, 4, P])
        bout = sb("bout", [P, D])
        wqkv_s = sb("wqkv_s", [P, L, QKV])
        wo_s = sb("wo_s", [P, L, INNER // P, D])
        w1_s = sb("w1_s", [P, L, 2 * HID])
        w2_s = sb("w2_s", [P, L, HC, D])
        scales = sb("scales", [P, 2 * L, 2, DH])
        ltab = sb("ltab", [P, L, 4, TPB, DH])
        lngb = sb("lngb", [P, L, 2])
        b1_s = sb("b1_s", [P, L, 2, HC])
        b2_s = sb("b2_s", [P, L, D])

        pairs = [ctx.enter_context(nc.psum_tensor(f"banks{2 * n}", [P, 1024], F32)) for n in range(4)]
        psA = [pairs[0][:, :], pairs[1][:, :]]
        bank = [pairs[n // 2][:, 512 * (n % 2):512 * (n % 2) + 512] for n in range(8)]

        phase_end = sem("phase_end")
        w_in = sem("w_in")
        set_id = sem("set_id")
        zero_out = sem("zero_out")
        set_ps = sem("set_ps")
        set_done = sem("set_done")
        set_c = sem("set_c")
        passed = sem("passed")

        n_w = [0]

        def load(eng, dst, src):
            eng.dma_start(dst, src).then_inc(w_in, 16)
            n_w[0] += 16

        block = ctx.enter_context(nc.Block())

        def setup_sync(sp):
            sp.wait_ge(set_id, 1)
            for h in range(GH):
                with nc.allow_non_contiguous_dma(reason="a 64x8 matrix, once"):
                    load(sp, rfb[h * DIM_A:(h + 1) * DIM_A, h * FEAT:(h + 1) * FEAT], rf.rearrange("f d -> d f"))
            load(sp, wq_raw[:, 0:3, :], w_qkv.rearrange("(c p) i -> p c i", p=P))
            load(sp, wq_raw[:, 3, :], w_out)
            load(sp, rfn[:, :], neg_c.ap() if hasattr(neg_c, "ap") else neg_c)
            load(sp, hones[:, :], ones_c.ap() if hasattr(ones_c, "ap") else ones_c)
            load(sp, bout[:, :], b_out.rearrange("(a d) -> a d", a=1).broadcast_to([P, D]))
            load(sp, tabs[:].rearrange("p a t d -> p (a t d)"), tabs_c.ap() if hasattr(tabs_c, "ap") else tabs_c)
            load(sp, masks_f[:].rearrange("p t d -> p (t d)"), mask_c.ap() if hasattr(mask_c, "ap") else mask_c)
            load(sp, wqkv_s[:], wqkv.rearrange("l p n -> p l n"))
            load(sp, w1_s[:], w1.rearrange("l p n -> p l n"))
            for l in range(L):
                load(sp, wo_s[:, l], wo[l].rearrange("(c p) d -> p c d", p=P))
                for c in range(HC):
                    load(sp, w2_s[0:HW[c], l, c, :], w2[l, c * P:c * P + HW[c], :])
                    for g in range(2):
                        with nc.allow_non_contiguous_dma(reason="a bias, once"):
                            load(sp, b1_s[0:HW[c], l, g, c:c + 1],
                                 b1[l, g * HID + c * P:g * HID + c * P + HW[c]].rearrange("(p a) -> p a", a=1))
                with nc.allow_non_contiguous_dma(reason="a gain and a bias, once"):
                    load(sp, lngb[:, l, 0:1], ln_g[l].rearrange("(p a) -> p a", a=1))
                    load(sp, lngb[:, l, 1:2], ln_b[l].rearrange("(p a) -> p a", a=1))
                load(sp, b2_s[:, l, :], b2[l:l + 1, :].broadcast_to([P, D]))
                for s, src in enumerate((q_scale, k_scale)):
                    load(sp, scales[:, 2 * l + s, 0, :], src[l:l + 1, :].broadcast_to([P, DH]))
                    load(sp, scales[:, 2 * l + s, 1, 0:DH // 2], src[l:l + 1, DH // 2:DH].broadcast_to([P, DH // 2]))
                    load(sp, scales[:, 2 * l + s, 1, DH // 2:DH], src[l:l + 1, 0:DH // 2].broadcast_to([P, DH // 2]))
            for n in range(2 * L):
                sp.dma_start(y_d[n][:, 0, :], zrow[:, :]).then_inc(zero_out, 16)

        def setup_gpsimd(pool):
            nc.gpsimd.memset(ident[:], 0.0).then_inc(set_c, 1)
            pool.wait_ge(set_c, 1)
            nc.gpsimd.affine_select(out=ident[:], in_=ident[:], compare_op=ALU.not_equal, fill=1.0, base=0,
                                    pattern=[[-1, P]], channel_multiplier=1).then_inc(set_c, 1)
            nc.gpsimd.memset(half_neg[:], -0.5)
            nc.gpsimd.memset(half_pos[:], 0.5).then_inc(set_c, 1)

        def setup_vector(dve):
            nc.vector.memset(zrow[:], 0.0)
            nc.vector.memset(rfb[:], 0.0).then_inc(set_id, 1)
            dve.wait_ge(set_c, 2)
            nc.vector.tensor_copy(ident_b[:], ident[:]).then_inc(set_done, 1)
            dve.wait_ge(w_in, n_w[0])
            nc.vector.scalar_tensor_tensor(out=rfa[:], in0=rfb[:], scalar=FEAT ** -0.5, in1=rfn[:],
                                           op0=ALU.mult, op1=ALU.add)
            nc.vector.tensor_copy(masks[:], masks_f[:])
            for l in range(L):
                for a in range(4):
                    s = scales[:, 2 * l + a // 2, a % 2, :].unsqueeze(1).broadcast_to([P, TPB, DH])
                    nc.vector.tensor_tensor(ltab[:, l, a], tabs[:, a], s, ALU.mult).then_inc(set_done, 1)
            for c in range(4):
                dve.wait_ge(set_ps, c + 1)
                nc.vector.tensor_copy(wT[:, c, :], bank[c][:, 0:P]).then_inc(set_done, 1)
            nc.vector.memset(kvb[:], 0.0).then_inc(set_done, 1)
            nc.vector.memset(vaug[:], 1.0).then_inc(set_done, 1)
            nc.vector.memset(vt[:], 1.0).then_inc(set_done, 1)
            nc.vector.memset(ve[:], 1.0).then_inc(set_done, 1)

        N_SET = 1 + 4 * L + 4 + 4

        def setup_tensor(pe):
            pe.wait_ge(set_c, 2)
            pe.wait_ge(w_in, n_w[0])
            for c in range(4):
                nc.tensor.transpose(bank[c][:, 0:P], wq_raw[:, c, :], ident[:]).then_inc(set_ps, 1)

        def setup_done(eng):
            eng.wait_ge(set_done, N_SET)
            eng.wait_ge(set_c, 3)
            eng.wait_ge(w_in, n_w[0])

        kvb = sb("kvb", [P, GH, 18])
        vaug = sb("vaug", [P, 2, TPB, HEADS_A, 9])
        only_a = ctx.enter_context(ExitStack())

        def sa(name, shape, dt=F32):
            return only_a.enter_context(nc.sbuf_tensor(name, shape, dt))

        xa = sa("xa", [P, 2, TPB, D])
        a_st = sa("a_st", [P, TPB, 6])
        a_mv = sa("a_mv", [P, TPB, 2])
        a_ve = sa("a_ve", [P, TPB])
        a_rs = sa("a_rs", [P, TPB])
        a_xn = sa("a_xn", [P, TPB, D])
        a_xT = sa("a_xT", [P, N])
        aug = sa("aug", [72, 2, 4, N])
        a_sq = sa("a_sq", [64, 4, N])
        a_ss = sa("a_ss", [72, 4 * N])
        kf = sa("kf", [P, TPB, 2, GH * FEAT])
        qf = sa("qf", [P, GH, N])
        a_rd = sa("a_rd", [P, TPB, HEADS_A])
        a_o = sa("a_o", [P, TPB, D])
        a_oT = sa("a_oT", [P, N])
        a_y = sa("a_y", [P, TPB, D])
        xr = sa("xr", [P, 2, TPB, D])
        a_y2 = sa("a_y2", [P, TPB, D])
        a_rr = sa("a_rr", [P, TPB * HEADS_A])
        a_st2, a_st3 = (sa(f"a_st{k}", [P, TPB, 6]) for k in (2, 3))
        a_mv2, a_mv3 = (sa(f"a_mv{k}", [P, TPB, 2]) for k in (2, 3))
        a_ve2, a_ve3, a_rs2, a_rs3 = (sa(k, [P, TPB]) for k in ("a_ve2", "a_ve3", "a_rs2", "a_rs3"))
        a_x1 = sa("a_x1", [P, 2, TPB, D])
        a_yo = sa("a_yo", [P, 2, TPB, D])

        A = {k: sem("A_" + k) for k in (
            "x_in0", "x_in1", "st", "mv", "ve", "rs", "xn", "xT_ps", "xT", "qk_ps", "v_ps", "sq", "v", "ss_ps",
            "ss", "nrm", "kf_ps", "kf", "qf_ps", "qf", "kv_ps", "kv", "o_ps", "rd", "o", "oT_ps", "oT", "w_ps",
            "y", "xr_in0", "xr_in1", "rs_xn", "mv2", "mv3", "st2", "ve2", "rs2", "yn", "x1", "st3", "ve3", "rs3", "yo", "out0", "out1")}

        only_a.close()

        FT = 2 * TPB
        f_h = sb("f_h", [P, 2, FT, D])
        f_y = sb("f_y", [P, 2, FT, D])
        f_x1 = sb("f_x1", [P, 2, FT, D])
        f_st = sb("f_st", [P, FT, 6])
        f_mv = sb("f_mv", [P, FT, 2])
        f_ve = sb("f_ve", [P, FT])
        f_rs = sb("f_rs", [P, FT])
        f_xn = sb("f_xn", [P, FT, D])
        f_hT = sb("f_hT", [P, 2, FT * P])
        f_g = sb("f_g", [P, 2, FT * P])
        f_u = sb("f_u", [P, 2, HC, FT * P])
        f_yb = sb("f_yb", [P, 2, FT, D])
        f_yn = sb("f_yn", [P, 2, FT, D])
        f_st2 = sb("f_st2", [P, FT, 6])
        f_mv2 = sb("f_mv2", [P, FT, 2])
        f_ve2 = sb("f_ve2", [P, FT])
        f_rs2 = sb("f_rs2", [P, FT])
        f_ln = sb("f_ln", [P, FT, D])
        f_o = sb("f_o", [P, 2, FT, D])

        hs = sb("hs", [P, 2, TPB, D])
        yt = sb("yt", [P, 2, TPB, D])
        hT = sb("hT", [P, N])
        qraw = sb("qraw", [P, TPB, INNER])
        kraw = sb("kraw", [P, TPB, INNER])
        sq = sb("sq", [P, 2 * INNER])
        ss = sb("ss", [P, 2, TPB, 2 * HEADS])
        rr = sb("rr", [P, 2, TPB, 2 * HEADS])
        kn = sb("kn", [P, INNER])
        m1k = sb("m1k", [P, INNER])
        m2k = sb("m2k", [P, INNER])
        m1q = sb("m1q", [P, INNER])
        m2q = sb("m2q", [P, INNER])
        qrot = sb("qrot", [P, TPB, INNER])
        krot = sb("krot", [P, TPB, INNER])
        qT = sb("qT", [P, TPB, 4, P])
        kT = sb("kT", [P, 4, TPB, P])
        vt = sb("vt", [P, 2, TPB, HEADS, DH + 1])
        ve = sb("ve", [P, 2, HEADS, DH + 1])
        mx = sb("mx", [P, 2, UH])
        nb = sb("nb", [P, 2, UH])
        pr = sb("pr", [P, 2, UH, P])
        pT = sb("pT", [P, 2, UH, P])
        rl = sb("rl", [P, 2, UH])
        ot = sb("ot", [P, TPB, INNER])
        oT = sb("oT", [P, TPB, 4, P])
        yn = sb("yn", [P, TPB, D])

        T = {k: sem("T_" + k) for k in (
            "h_in0", "h_in1", "y_in0", "y_in1", "hT_ps", "hT", "q_ps", "k_ps", "v_ps", "q", "k", "v", "ss", "rr",
            "kn", "km", "krot", "qm", "qrot", "qT_ps", "qT", "kT_ps", "kT", "s_ps", "mx", "nb", "p", "pT_ps", "pTa",
            "pTb", "o_ps", "rl", "o", "oT_ps", "oT", "w_ps", "yn", "out", "ssm")}

        G = {k: sem("F_" + k) for k in (
            "in0", "in1", "st", "mv", "ve", "rs", "xn", "hT_ps", "hT", "g_ps", "a_ps", "g", "u", "yb", "w_ps", "yn",
            "st2", "mv2", "ve2", "rs2", "ln", "o", "out0", "out1")}

        def until(eng, s, v):
            if isinstance(v, int) and v <= 0:
                return
            eng.wait_ge(s, v)

        def apart(eng):
            eng.sem_inc(passed, 1)

        def inv_std(pool, ve, rs, mv, stats_ready, v, ve_sem, rs_sem):
            until(pool, stats_ready, v)
            apart(pool)
            nc.gpsimd.tensor_scalar(ve, mv, EPS_LN, None, ALU.add).then_inc(ve_sem, 1)
            pool.wait_ge(ve_sem, v)
            nc.gpsimd.tensor_tensor(rs, ve, half_neg[:, 0:ve.shape[-1]], ALU.pow).then_inc(rs_sem, 1)

        def stats(dve, src, st, mv, tiles, st_sem, v, mv_sem):
            for t in range(tiles):
                nc.vector.bn_stats(st[:, t, :], src[:, t, :]).then_inc(st_sem, 1)
            dve.wait_ge(st_sem, v)
            apart(dve)
            for t in range(tiles):
                i = nc.vector.bn_aggr(mv[:, t, :], st[:, t, :])
            i.then_inc(mv_sem, 1)

        def normal(dst, src, mv, rs, t):
            return nc.vector.tensor_scalar(dst[:, t, :], src[:, t, :], mv[:, t, 0:1], rs[:, t:t + 1],
                                           ALU.subtract, ALU.mult)

        def steps(eng, step):
            step(-1, True, False, False)
            step(0, True, True, False)
            step(1, True, True, True)
            step(2, True, True, True)
            with eng.Fori(3, B - 2, 2) as i:
                step(i, True, True, True)
                step(i + 1, True, True, True, odd=False)
            step(B - 1, False, True, True)
            step(B, False, False, True)

        def par_of(i, odd):
            return i % 2 if isinstance(i, int) else int(odd)

        def a_sync(sp, i, ahead, now, behind, odd=True):
            p = par_of(i, odd)
            if ahead:
                until(sp, A["xn"], i)
                sp.dma_start(xa[:, 1 - p], x[bass.ds(i + 1, 1)].rearrange("b (t p) d -> p (b t) d", p=P)
                             ).then_inc(A[f"x_in{1 - p}"], 16)
            if behind:
                n = i - 1
                until(sp, A["x1"], n - 1)
                sp.dma_start(xr[:, 1 - p], x[bass.ds(n, 1)].rearrange("b (t p) d -> p (b t) d", p=P)
                             ).then_inc(A[f"xr_in{1 - p}"], 16)
                sp.wait_ge(A["x1"], n + 1)
                sp.dma_start(x1_d[bass.ds(n, 1)].rearrange("b (t p) d -> p (b t) d", p=P), a_x1[:, 1 - p]
                             ).then_inc(A[f"out{1 - p}"], 16)
                sp.wait_ge(A["yo"], n + 1)
                sp.dma_start(y_d[0][bass.ds(n, 1), 1:ROWS, :].rearrange("b (t p) d -> p (b t) d", p=P), a_yo[:, 1 - p]
                             ).then_inc(A[f"out{1 - p}"], 16)

        def a_pool(pool, i, ahead, now, behind, odd=True):
            p = par_of(i, odd)
            if ahead:
                inv_std(pool, a_ve[:], a_rs[:], a_mv[:, :, 1], A["mv"], i + 2, A["ve"], A["rs"])
            if now:
                pool.wait_ge(A["ss"], 2 * (i + 1))
                until(pool, A["qf_ps"], 2 * (i - 1))
                pool.wait_ge(A["rs"], i + 2 if ahead else i + 1)
                if not ahead:
                    pool.wait_ge(A["rs3"], i - 1)
                nc.gpsimd.tensor_tensor(aug[64:72, p].rearrange("p a n -> p (a n)"), a_ss[64:72, :],
                                        half_pos[64:72, :], ALU.pow).then_inc(A["nrm"], 1)
                pool.wait_ge(A["nrm"], i + 1)
            if behind:
                n = i - 1
                inv_std(pool, a_ve2[:], a_rs2[:], a_mv2[:, :, 1], A["mv2"], n + 1, A["ve2"], A["rs2"])
                pool.wait_ge(A["yn"], n + 1)
                pool.wait_ge(A[f"xr_in{1 - p}"], 16 * half_count(n))
                until(pool, A[f"out{1 - p}"], 32 * (half_count(n) - 1))
                nc.gpsimd.tensor_tensor(a_x1[:, 1 - p], a_y2[:], xr[:, 1 - p], ALU.add).then_inc(A["x1"], 1)
                inv_std(pool, a_ve3[:], a_rs3[:], a_mv3[:, :, 1], A["mv3"], n + 1, A["ve3"], A["rs3"])

        def a_act(act, i, ahead, now, behind, odd=True):
            p = par_of(i, odd)
            if behind:
                n = i - 1
                until(act, A["kv_ps"], n)
                for t in range(TPB):
                    act.wait_ge(A["kf_ps"], 2 * n + t + 1)
                    nc.scalar.activation(kf[:, t].rearrange("p g n -> p (g n)"), psA[t], ACT.Exp
                                         ).then_inc(A["kf"], 1)
            if now:
                act.wait_ge(A["xT_ps"], i + 1)
                nc.scalar.copy(a_xT[:], bank[6][:, 0:N]).then_inc(A["xT"], 1)
            if behind:
                until(act, A["o_ps"], n)
                act.wait_ge(A["qf_ps"], 2 * n + 1)
                nc.scalar.activation(qf[:, 0:4].rearrange("p j n -> p (j n)"), psA[0], ACT.Exp).then_inc(A["qf"], 1)
            if now:
                for c in range(2):
                    act.wait_ge(A["qk_ps"], 2 * i + c + 1)
                    nc.scalar.activation(a_sq[:, 2 * c:2 * c + 2, :].rearrange("p g n -> p (g n)"),
                                         bank[4 + c][0:64, :], ACT.Square)
                    if c == 0:
                        until(act, A["qf_ps"], 2 * (i - 1))
                    nc.scalar.copy(aug[0:64, p, 2 * c:2 * c + 2, :].rearrange("p g n -> p (g n)"),
                                   bank[4 + c][0:64, :]).then_inc(A["sq"], 1)
            if behind:
                act.wait_ge(A["qf_ps"], 2 * n + 2)
                nc.scalar.activation(qf[:, 4:8].rearrange("p j n -> p (j n)"), psA[1], ACT.Exp).then_inc(A["qf"], 1)
            if now:
                act.wait_ge(A["v_ps"], i + 1)
                until(act, A["kv_ps"], i - 1)
                nc.scalar.copy(vaug[:, p, :, :, 0:DIM_A].rearrange("p t h d -> p (t h) d"),
                               bank[6][:, N:2 * N].rearrange("p (h d) -> p h d", d=DIM_A)).then_inc(A["v"], 1)
            if behind:
                act.wait_ge(A["oT_ps"], n + 1)
                nc.scalar.copy(a_oT[:], bank[6][:, 0:N]).then_inc(A["oT"], 1)

        def a_pe(pe, i, ahead, now, behind, odd=True):
            p = par_of(i, odd)
            n = i - 1
            if behind:
                pe.wait_ge(A["nrm"], n + 1)
                for t in range(TPB):
                    until(pe, A["qf"], 2 * n - 1 + t)
                    for g in range(2):
                        m = nc.tensor.matmul(bank[2 * t + g][:], aug[:, 1 - p, 2 + g, t * P:(t + 1) * P], rfa[:],
                                             start=True, stop=True)
                    m.then_inc(A["kf_ps"], 1)
            if now:
                pe.wait_ge(A["rs_xn"], i + 1)
                until(pe, A["y"], i - 1)
                until(pe, A["v"], i)
                for t in range(TPB):
                    m = nc.tensor.transpose(bank[6][:, t * P:(t + 1) * P], a_xn[:, t, :], ident[:])
                m.then_inc(A["xT_ps"], 1)
            if behind:
                for g in range(2):
                    pe.wait_ge(A["kf"], 2 * n + 1 + g)
                    for j in range(4):
                        m = nc.tensor.matmul(bank[2 * g + j // 2][:, (j % 2) * N:(j % 2 + 1) * N],
                                             rfa[:, j * P:(j + 1) * P], aug[:, 1 - p, g, :], start=True, stop=True)
                    m.then_inc(A["qf_ps"], 1)
                    if g == 0 and now:
                        pe.wait_ge(A["xT"], i + 1)
                        until(pe, A["ss"], 2 * i)
                        a_qk(pe)
            if now:
                if not behind:
                    pe.wait_ge(A["xT"], i + 1)
                    until(pe, A["ss"], 2 * i)
                    a_qk(pe)
                for t in range(TPB):
                    m = nc.tensor.matmul(bank[6][:, N + t * P:N + (t + 1) * P], a_xT[:, t * P:(t + 1) * P],
                                         wT[:, 2, :], start=True, stop=True)
                m.then_inc(A["v_ps"], 1)
            if behind:
                pe.wait_ge(A["kf"], 2 * n + 2)
                pe.wait_ge(A["v"], n + 1)
                until(pe, A["o"], n)
                for j in range(GH):
                    for t in range(TPB):
                        m = nc.tensor.matmul(bank[7][:, 18 * j:18 * j + 18],
                                             kf[:, t, j // 4, (j % 4) * P:(j % 4 + 1) * P],
                                             vaug[:, 1 - p, t, 2 * j:2 * j + 2, :].rearrange("p h d -> p (h d)"),
                                             start=(t == 0), stop=(t == TPB - 1))
                m.then_inc(A["kv_ps"], 1)
            if now:
                pe.wait_ge(A["sq"], 2 * i + 2)
                apart(pe)
                for c in range(2):
                    nc.tensor.matmul(bank[4 + c][64:72, :], hones[:], a_sq[:, 2 * c:2 * c + 2, :].rearrange(
                        "p g n -> p (g n)"), start=True, stop=True).then_inc(A["ss_ps"], 1)
            if behind:
                pe.wait_ge(A["kv"], n + 1)
                pe.wait_ge(A["qf"], 2 * n + 2)
                for t in range(TPB):
                    for j in range(GH):
                        m = nc.tensor.matmul(bank[7][:, 160 + 144 * t + 18 * j:160 + 144 * t + 18 * j + 18],
                                             qf[:, j, t * P:(t + 1) * P], kvb[:, j, :], start=True, stop=True)
                m.then_inc(A["o_ps"], 1)
                pe.wait_ge(A["o"], n + 1)
                pe.wait_ge(A["v"], i + 1 if now else i)
                for t in range(TPB):
                    m = nc.tensor.transpose(bank[6][:, t * P:(t + 1) * P], a_o[:, t, :], ident[:])
                m.then_inc(A["oT_ps"], 1)
                pe.wait_ge(A["oT"], n + 1)
                for t in range(TPB):
                    m = nc.tensor.matmul(bank[6][:, N + t * P:N + (t + 1) * P], a_oT[:, t * P:(t + 1) * P],
                                         wT[:, 3, :], start=True, stop=True)
                m.then_inc(A["w_ps"], 1)

        def a_qk(pe):
            for c in range(2):
                for g in range(2):
                    m = nc.tensor.matmul(bank[4 + c][0:64, g * N:(g + 1) * N], wT[:, c, 64 * g:64 * g + 64], a_xT[:],
                                         start=True, stop=True)
                m.then_inc(A["qk_ps"], 1)

        def a_dve(dve, i, ahead, now, behind, odd=True):
            p = par_of(i, odd)
            n = i - 1
            if ahead:
                dve.wait_ge(A[f"x_in{1 - p}"], 16 * half_count(i + 1))
                until(dve, A["rs"], i + 1)
                stats(dve, xa[:, 1 - p], a_st, a_mv, TPB, A["st"], 2 * (i + 2), A["mv"])
            if behind:
                dve.wait_ge(A["kv_ps"], n + 1)
                until(dve, A["o_ps"], n)
                for r in range(2):
                    j = nc.vector.tensor_copy(
                        kvb[64 * r:64 * r + 64, :, 9 * r:9 * r + 9],
                        bank[7][64 * r:64 * r + 64, 0:144].rearrange("p (j c) -> p j c", c=18)[:, :, 9 * r:9 * r + 9])
                j.then_inc(A["kv"], 1)
            if now:
                until(dve, A["nrm"], i)
                for c in range(2):
                    dve.wait_ge(A["ss_ps"], 2 * i + c + 1)
                    nc.vector.tensor_copy(a_ss[64:72, 512 * c:512 * c + 512], bank[4 + c][64:72, :]
                                          ).then_inc(A["ss"], 1)
            if ahead:
                dve.wait_ge(A["rs"], i + 2)
                until(dve, A["xT_ps"], i + 1)
                for t in range(TPB):
                    j = normal(a_xn, xa[:, 1 - p], a_mv, a_rs, t)
                    if t == TPB - 1:
                        j.then_inc(A["rs_xn"], 1)
                dve.wait_ge(A["rs_xn"], i + 2)
                dve.sem_inc(A["xn"], 1)
            if behind:
                o = bank[7][:, 160:448].rearrange("p (h c) -> p h c", c=9)
                rd = a_rd[:].rearrange("p t h -> p (t h)")
                dve.wait_ge(A["o_ps"], n + 1)
                nc.vector.tensor_scalar(rd, o[:, :, 8], EPS_A, None, ALU.add).then_inc(A["rd"], 1)
                dve.wait_ge(A["rd"], 2 * n + 1)
                nc.vector.reciprocal(a_rr[:], rd).then_inc(A["rd"], 1)
                dve.wait_ge(A["rd"], 2 * n + 2)
                until(dve, A["oT_ps"], n)
                nc.vector.tensor_tensor(a_o[:].rearrange("p t (h d) -> p (t h) d", d=DIM_A), o[:, :, 0:8],
                                        a_rr[:].unsqueeze(2).broadcast_to([P, 2 * HEADS_A, DIM_A]), ALU.mult
                                        ).then_inc(A["o"], 1)
                dve.wait_ge(A["w_ps"], n + 1)
                nc.vector.tensor_tensor(a_y[:], bank[6][:, N:2 * N].rearrange("p (t d) -> p t d", d=D),
                                        bout[:].unsqueeze(1).broadcast_to([P, TPB, D]), ALU.add).then_inc(A["y"], 1)
                dve.wait_ge(A["y"], n + 1)
                stats(dve, a_y, a_st2, a_mv2, TPB, A["st2"], 2 * (n + 1), A["mv2"])
                dve.wait_ge(A["rs2"], n + 1)
                until(dve, A["x1"], n)
                for t in range(TPB):
                    j = normal(a_y2, a_y, a_mv2, a_rs2, t)
                j.then_inc(A["yn"], 1)
                dve.wait_ge(A["x1"], n + 1)
                stats(dve, a_x1[:, 1 - p], a_st3, a_mv3, TPB, A["st3"], 2 * (n + 1), A["mv3"])
                dve.wait_ge(A["rs3"], n + 1)
                until(dve, A[f"out{1 - p}"], 32 * (half_count(n) - 1))
                for t in range(TPB):
                    j = normal(a_yo[:, 1 - p], a_x1[:, 1 - p], a_mv3, a_rs3, t)
                j.then_inc(A["yo"], 1)

        def half_count(n):
            return n // 2 + 1

        MASK_FIRST = True

        def t_sync(sp, l, i, now, behind, odd=True):
            p = par_of(i, odd)
            if now:
                n = l * B + i
                until(sp, T["hT_ps"], 2 * (n - 1))
                for c, row in ((0, 1), (1, 0)):
                    sp.dma_start(hs[:, p, :, 64 * c:64 * c + 64],
                                 y_d[2 * l][bass.ds(i, 1), row:row + N, 64 * c:64 * c + 64].rearrange(
                                     "b (t p) d -> p (b t) d", p=P)).then_inc(T[f"h_in{p}"], 16)
            if behind:
                b = i - 1
                n = l * B + b
                until(sp, T["yn"], 2 * (n - 1))
                sp.dma_start(yt[:, 1 - p], y_d[2 * l][bass.ds(b, 1), 1:ROWS, :].rearrange(
                    "b (t p) d -> p (b t) d", p=P)).then_inc(T[f"y_in{1 - p}"], 16)

        def t_store(sp, l, i, odd=True):
            b = i - 1
            n = l * B + b
            sp.wait_ge(T["yn"], 2 * (n + 1))
            sp.dma_start(y_d[2 * l + 1][bass.ds(b, 1), 1:ROWS, :].rearrange("b (t p) d -> p (b t) d", p=P), yn[:]
                         ).then_inc(T["out"], 16)

        def t_pool(pool, l, i, now, behind, odd=True):
            p = par_of(i, odd)
            if now:
                n = l * B + i
                for t in range(TPB):
                    pool.wait_ge(T["ss"], 2 * n + t + 1)
                    apart(pool)
                    nc.gpsimd.tensor_scalar(ss[:, p, t, :], ss[:, p, t, :], 1e-24, None, ALU.max
                                            ).then_inc(T["ssm"], 1)
                    pool.wait_ge(T["ssm"], 2 * n + t + 1)
                    until(pool, T["p"], 4 * (n - 1))
                    nc.gpsimd.tensor_tensor(rr[:, p, t, :], ss[:, p, t, :], half_neg[:], ALU.pow
                                            ).then_inc(T["rr"], 1)
                    pool.wait_ge(T["q"], 2 * n + t + 1)
                    rotary(nc.gpsimd, pool, qraw[:, t, :], m1q, m2q, qrot[:, t, :], l, 0, t, T["qm"],
                           2 * (2 * n + t + 1), T["qT_ps"], 2 * (n - 1) + t + 1 if not isinstance(n, int) or n else 0,
                           T["qrot"])

        def rotary(on, eng, src, m1, m2, dst, l, a, t, m_sem, m_count, read_sem, read_count, done):
            s3 = src.rearrange("p (h d) -> p h d", d=DH)
            s4 = src.rearrange("p (h c d) -> p h c d", c=2, d=DH // 2)
            d4 = m2[:].rearrange("p (h c d) -> p h c d", c=2, d=DH // 2)
            cos = ltab[:, l, a, t, :].unsqueeze(1).broadcast_to([P, HEADS, DH])
            on.tensor_tensor(m1[:].rearrange("p (h d) -> p h d", d=DH), s3, cos, ALU.mult)
            for c in range(2):
                sin = ltab[:, l, a + 1, t, 32 * c:32 * c + 32].unsqueeze(1).broadcast_to([P, HEADS, DH // 2])
                on.tensor_tensor(d4[:, :, c, :], s4[:, :, 1 - c, :], sin, ALU.mult).then_inc(m_sem, 1)
            eng.wait_ge(m_sem, m_count)
            until(eng, read_sem, read_count)
            on.tensor_tensor(dst, m1[:], m2[:], ALU.add).then_inc(done, 1)

        def t_act(act, l, i, now, behind, odd=True):
            p = par_of(i, odd)
            n1 = l * B + i
            n = n1 - 1

            def exps(u):
                act.wait_ge(T["nb"], 4 * n + u + 1)
                until(act, T["pT_ps"], 4 * n + u - 1)
                for j in range(UH):
                    h = 2 * j + u % 2
                    e = nc.scalar.activation(pr[:, u % 2, j, :], bank[u % 2][:, j * P:(j + 1) * P], ACT.Exp,
                                             bias=nb[:, u % 2, j:j + 1], scale=rr[:, 1 - p, u // 2, h:h + 1])
                e.then_inc(T["p"], 1)

            def qk_in(t):
                act.wait_ge(T["q_ps"], 2 * n1 + t + 1)
                until(act, T["qrot"], 2 * (n1 - 1) + t + 1 if not isinstance(n1, int) or n1 else 0)
                nc.scalar.copy(qraw[:, t, :], bank[6 + t][:])
                until(act, T["ss"], 2 * n1 + t)
                nc.scalar.activation(sq[:, 0:INNER], bank[6 + t][:], ACT.Square).then_inc(T["q"], 1)
                act.wait_ge(T["k_ps"], 2 * n1 + t + 1)
                until(act, T["kn"], 2 * (n1 - 1) + t + 1 if not isinstance(n1, int) or n1 else 0)
                nc.scalar.copy(kraw[:, t, :], bank[7 - t][:])
                nc.scalar.activation(sq[:, INNER:], bank[7 - t][:], ACT.Square).then_inc(T["k"], 1)

            def v_in(t):
                act.wait_ge(T["v_ps"], 2 * n1 + t + 1)
                until(act, T["o_ps"], 4 * (n1 - 1))
                v = bank[6 + t][:].rearrange("p (h d) -> p h d", d=DH)
                nc.scalar.copy(vt[:, p, t, :, 0:DH], v)
                r = 64 * (1 - t)
                nc.scalar.copy(ve[r:r + 64, p, :, 0:DH], v[r:r + 64]).then_inc(T["v"], 1)

            if behind:
                for t in range(TPB):
                    act.wait_ge(T["qT_ps"], 2 * n + t + 1)
                    nc.scalar.copy(qT[:, t].rearrange("p j n -> p (j n)"), bank[2][:]).then_inc(T["qT"], 1)
            if now:
                for t in range(TPB):
                    act.wait_ge(T["hT_ps"], 2 * n1 + t + 1)
                    until(act, T["v_ps"], 2 * n1 - 1 + t)
                    nc.scalar.copy(hT[:, t * P:(t + 1) * P], bank[2 + t][:, 0:P]).then_inc(T["hT"], 1)
            if behind:
                exps(0)
            if now:
                qk_in(0)
            if behind:
                exps(1)
            if now:
                v_in(0)
            if behind:
                exps(2)
                act.wait_ge(T["pT_ps"], 4 * n + 2)
                until(act, T["o_ps"], 4 * n)
                nc.scalar.copy(pT[:, 1].rearrange("p j n -> p (j n)"), bank[3][:]).then_inc(T["pTb"], 1)
            if now:
                qk_in(1)
            if behind:
                exps(3)
            if now:
                v_in(1)
            if behind:
                act.wait_ge(T["oT_ps"], 2 * n + 1)
                nc.scalar.copy(oT[:, 0].rearrange("p j n -> p (j n)"), bank[3][:]).then_inc(T["oT"], 1)
                act.wait_ge(T["pT_ps"], 4 * n + 4)
                act.wait_ge(T["o_ps"], 4 * n + 2)
                nc.scalar.copy(pT[:, 1].rearrange("p j n -> p (j n)"), bank[2][:]).then_inc(T["pTb"], 1)
                act.wait_ge(T["oT_ps"], 2 * n + 2)
                nc.scalar.copy(oT[:, 1].rearrange("p j n -> p (j n)"), bank[2][:]).then_inc(T["oT"], 1)

        def t_dve(dve, l, i, now, behind, odd=True):
            p = par_of(i, odd)
            n1 = l * B + i
            n = n1 - 1

            def peak(u):
                dve.wait_ge(T["s_ps"], 4 * n + u + 1)
                nc.vector.tensor_reduce(mx[:, u % 2, :], bank[u % 2][:].rearrange("p (j k) -> p j k", k=P), AX.X,
                                        ALU.max).then_inc(T["mx"], 1)
                dve.wait_ge(T["mx"], 4 * n + u + 1)
                until(dve, T["p"], 4 * n + u - 1)
                nc.vector.scalar_tensor_tensor(out=nb[:, u % 2, :], in0=mx[:, u % 2, :], scalar=-1.0,
                                               in1=rr[:, 1 - p, u // 2, u % 2:HEADS:2], op0=ALU.mult, op1=ALU.mult
                                               ).then_inc(T["nb"], 1)

            def turned(u):
                dve.wait_ge(T["pT_ps"], 4 * n + u + 1)
                until(dve, T["o_ps"], 4 * n + u - 1)
                nc.vector.tensor_copy(pT[:, 0].rearrange("p j n -> p (j n)"), bank[2][:]).then_inc(T["pTa"], 1)

            def divide(u):
                o = bank[4 + u % 2][:, 0:UH * (DH + 1)].rearrange("p (j d) -> p j d", d=DH + 1)
                dve.wait_ge(T["o_ps"], 4 * n + u + 1)
                nc.vector.reciprocal(rl[:, u % 2, :], o[:, :, DH]).then_inc(T["rl"], 1)
                dve.wait_ge(T["rl"], 4 * n + u + 1)
                until(dve, T["oT_ps"], 2 * (n - 1) + u // 2 + 1)
                nc.vector.tensor_tensor(ot[:, u // 2].rearrange("p (j c d) -> p j c d", c=2, d=DH)[:, :, u % 2, :],
                                        o[:, :, 0:DH], rl[:, u % 2, :].unsqueeze(2).broadcast_to([P, UH, DH]),
                                        ALU.mult).then_inc(T["o"], 1)

            def squares(t):
                dve.wait_ge(T["k"], 2 * n1 + t + 1)
                nc.vector.tensor_reduce(ss[:, p, t, :], sq[:].rearrange("p (h d) -> p h d", d=DH), AX.X, ALU.add
                                        ).then_inc(T["ss"], 1)

            def keys(t):
                dve.wait_ge(T["rr"], 2 * n1 + t + 1)
                until(dve, T["krot"], 2 * n1 + t)
                nc.vector.tensor_tensor(kn[:].rearrange("p (h d) -> p h d", d=DH),
                                        kraw[:, t, :].rearrange("p (h d) -> p h d", d=DH),
                                        rr[:, p, t, HEADS:].unsqueeze(2).broadcast_to([P, HEADS, DH]), ALU.mult
                                        ).then_inc(T["kn"], 1)
                dve.wait_ge(T["kn"], 2 * n1 + t + 1)
                rotary(nc.vector, dve, kn[:], m1k, m2k, krot[:, t, :], l, 2, t, T["km"], 2 * (2 * n1 + t + 1),
                       T["kT_ps"], 2 * (n1 - 1) + t + 1 if not isinstance(n1, int) or n1 else 0, T["krot"])

            def residual(t):
                if t == 0:
                    dve.wait_ge(T[f"y_in{1 - p}"], 16 * half_count(n))
                    until(dve, T["out"], 16 * n)
                dve.wait_ge(T["w_ps"], 2 * n + t + 1)
                nc.vector.tensor_tensor(yn[:, t, :], yt[:, 1 - p, t, :], bank[3][:, 0:D], ALU.add
                                        ).then_inc(T["yn"], 1)

            if behind:
                for t in range(TPB):
                    dve.wait_ge(T["kT_ps"], 2 * n + t + 1)
                    nc.vector.tensor_copy(kT[:, :, 1 - t, :], bank[3][:].rearrange("p (j n) -> p j n", n=P)
                                          ).then_inc(T["kT"], 1)
                peak(0)
                peak(1)
                turned(0)
            if now:
                squares(0)
            if behind:
                peak(2)
            if now:
                keys(0)
            if behind:
                divide(0)
                peak(3)
                turned(2)
                divide(1)
            if now:
                squares(1)
            if behind:
                divide(2)
                residual(0)
            if now:
                keys(1)
            if behind:
                divide(3)
                residual(1)

        def t_pe(pe, l, i, now, behind, odd=True):
            p = par_of(i, odd)
            n1 = l * B + i
            n = n1 - 1

            def turn(src, t, b, into):
                for j in range(4):
                    m = nc.tensor.transpose(bank[b][:, j * P:(j + 1) * P], src[:, t, j * P:(j + 1) * P], ident[:])
                m.then_inc(into, 1)

            def project(t):
                pe.wait_ge(T["hT"], 2 * n1 + t + 1)
                if t == 0:
                    until(pe, T["k"], 2 * n1)
                else:
                    pe.wait_ge(T["k"], 2 * n1 + 1)
                nc.tensor.matmul(bank[6 + t][:], hT[:, t * P:(t + 1) * P], wqkv_s[:, l, 0:INNER],
                                 start=True, stop=True).then_inc(T["q_ps"], 1)
                until(pe, T["v"], 2 * n1 + t)
                nc.tensor.matmul(bank[7 - t][:], hT[:, t * P:(t + 1) * P], wqkv_s[:, l, INNER:2 * INNER],
                                 start=True, stop=True).then_inc(T["k_ps"], 1)
                pe.wait_ge(T["q"], 2 * n1 + t + 1)
                nc.tensor.matmul(bank[6 + t][:], hT[:, t * P:(t + 1) * P], wqkv_s[:, l, 2 * INNER:],
                                 start=True, stop=True).then_inc(T["v_ps"], 1)

            def scores(u):
                t, b = u // 2, bank[u % 2]
                pe.wait_ge(T["qT"], 2 * n + t + 1)
                pe.wait_ge(T["kT"], 2 * n + t + 1)
                until(pe, T["p"], 4 * n + u - 1)
                nc.tensor.matmul(b[:], ident_b[:], masks[:, t, :], start=True, stop=False, skip_group_check=True)
                for j in range(UH):
                    r, c = 64 * (u % 2), j
                    own = kT[r:r + 64, c, 1 - t, :]
                    for w in range(2):
                        q = qT[r:r + 64, t, c, 64 * w:64 * w + 64]
                        o = b[64 * w:64 * w + 64, j * P:(j + 1) * P]
                        if w == 1:
                            m = nc.tensor.matmul(o, q, own, start=False, stop=True, skip_group_check=True)
                        elif t == 0:
                            nc.tensor.matmul(o[:, 0:64], q, own[:, 0:64], start=False, stop=True,
                                             skip_group_check=True)
                        else:
                            both = kT[r:r + 64, c, :, :].rearrange("p t (w k) -> p (t w) k", k=64)[:, 0:4:3, :]
                            nc.tensor.matmul(o, q, both, start=False, stop=True, skip_group_check=True)
                m.then_inc(T["s_ps"], 1)

            def turn_p(u):
                pe.wait_ge(T["p"], 4 * n + u + 1)
                b = (2, 3, 2, 2)[u]
                if u == 0:
                    pe.wait_ge(T["hT"], 2 * n1 + 1 if now else 2 * n1)
                elif u == 1:
                    pe.wait_ge(T["hT"], 2 * n1 + 2 if now else 2 * n1)
                elif u == 2:
                    pe.wait_ge(T["pTa"], 2 * n + 1)
                else:
                    pe.wait_ge(T["pTa"], 2 * n + 2)
                for j in range(UH):
                    m = nc.tensor.transpose(bank[b][:, j * P:(j + 1) * P], pr[:, u % 2, j, :], ident[:])
                m.then_inc(T["pT_ps"], 1)

            def weigh(u):
                t, b = u // 2, bank[4 + u % 2]
                pe.wait_ge(T["pTb" if u % 2 else "pTa"], 2 * n + u // 2 + 1)
                pe.wait_ge(T["v"], 2 * n + 2)
                until(pe, T["o"], 4 * n + u - 1)
                apart(pe)
                for j in range(UH):
                    h = 2 * j + u % 2
                    o = b[:, j * (DH + 1):(j + 1) * (DH + 1)]
                    if t == 0:
                        nc.tensor.matmul(o[0:64], pT[0:64, u % 2, j, 0:64], vt[0:64, 1 - p, 0, h, :],
                                         start=True, stop=True)
                    else:
                        nc.tensor.matmul(o[0:64], pT[:, u % 2, j, 0:64], ve[:, 1 - p, h, :], start=True, stop=True)
                    m = nc.tensor.matmul(o[64:128], pT[:, u % 2, j, 64:128], vt[:, 1 - p, t, h, :],
                                         start=True, stop=True)
                m.then_inc(T["o_ps"], 1)

            def turn_o(t):
                pe.wait_ge(T["o"], 4 * n + 2 * t + 2)
                if t == 0:
                    pe.wait_ge(T["pTb"], 2 * n + 1)
                else:
                    pe.wait_ge(T["pTb"], 2 * n + 2)
                turn(ot, t, 3 - t, T["oT_ps"])

            def out_project(t):
                pe.wait_ge(T["oT"], 2 * n + t + 1)
                if t == 1:
                    pe.wait_ge(T["yn"], 2 * n + 1)
                for c in range(4):
                    m = nc.tensor.matmul(bank[3][:, 0:D], oT[:, t, c, :], wo_s[:, l, c, :],
                                         start=(c == 0), stop=(c == 3))
                m.then_inc(T["w_ps"], 1)

            if behind:
                for t in range(TPB):
                    pe.wait_ge(T["qrot"], 2 * n + t + 1)
                    if t == 0:
                        until(pe, T["oT"], 2 * n)
                    else:
                        pe.wait_ge(T["qT"], 2 * n + 1)
                    turn(qrot, t, 2, T["qT_ps"])
                    pe.wait_ge(T["krot"], 2 * n + t + 1)
                    if t == 0:
                        until(pe, T["yn"], 2 * n)
                    else:
                        pe.wait_ge(T["kT"], 2 * n + 1)
                    turn(krot, t, 3, T["kT_ps"])
            if now:
                pe.wait_ge(T[f"h_in{p}"], 32 * half_count(n1))
                for t in range(TPB):
                    if t == 0:
                        until(pe, T["qT"], 2 * n1)
                    else:
                        until(pe, T["kT"], 2 * n1)
                    nc.tensor.transpose(bank[2 + t][:, 0:P], hs[:, p, t, :], ident[:]).then_inc(T["hT_ps"], 1)
            if behind:
                scores(0)
            if now:
                project(0)
            if behind:
                scores(1)
                turn_p(0)
                scores(2)
                turn_p(1)
                weigh(0)
            if now:
                project(1)
            if behind:
                scores(3)
                turn_p(2)
                weigh(1)
                turn_o(0)
                turn_p(3)
                weigh(2)
                out_project(0)
                weigh(3)
                turn_o(1)
                out_project(1)

        def t_steps(eng, step):
            step(0, True, False)
            step(1, True, True)
            step(2, True, True)
            with eng.Fori(3, B - 2, 2) as i:
                step(i, True, True)
                step(i + 1, True, True, odd=False)
            step(B - 1, True, True)
            step(B, False, True)

        M = B // 2

        def f_sync(sp, l, i, odd=False, load_next=True):
            p = par_of(i, odd)
            m = l * M + i
            until(sp, G["xn"], 1 * (m - 1))
            until(sp, G["yb"], 1 * (m - 1))
            if l == L - 1:
                until(sp, G["o"], i - 1)
            for k in range(2):
                b = 2 * i + k
                tt = slice(TPB * k, TPB * k + TPB)
                for c, row in ((0, 1), (1, 0)):
                    sp.dma_start(f_h[:, p, tt, 64 * c:64 * c + 64],
                                 y_d[2 * l + 1][bass.ds(b, 1), row:row + N, 64 * c:64 * c + 64].rearrange(
                                     "b (t p) d -> p (b t) d", p=P)).then_inc(G[f"in{p}"], 16)
                sp.dma_start(f_y[:, p, tt, :], y_d[2 * l + 1][bass.ds(b, 1), 1:ROWS, :].rearrange(
                    "b (t p) d -> p (b t) d", p=P)).then_inc(G[f"in{p}"], 16)
                if l == L - 1:
                    sp.dma_start(f_x1[:, p, tt, :], x1_d[bass.ds(b, 1)].rearrange("b (t p) d -> p (b t) d", p=P)
                                 ).then_inc(G[f"in{p}"], 16)

        def f_in_count(l, i):
            return 96 * (M // 2 * l) + (96 if l < L - 1 else 128) * half_count(i)

        def f_store(sp, l, i, odd=False):
            p = par_of(i, odd)
            m = l * M + i
            src, ready = (f_o, "o") if l == L - 1 else (f_yn, "yn")
            until(sp, G[ready], i + 1 if l == L - 1 else m + 1)
            for k in range(2):
                tt = slice(TPB * k, TPB * k + TPB)
                if l == L - 1:
                    dst = out[bass.ds(2 * i + k, 1)]
                else:
                    dst = y_d[2 * l + 2][bass.ds(2 * i + k, 1), 1:ROWS, :]
                sp.dma_start(dst.rearrange("b (t p) d -> p (b t) d", p=P), src[:, p, tt, :]
                             ).then_inc(G[f"out{p}"], 16)

        def f_pool(pool, l, i, odd=False):
            p = par_of(i, odd)
            m = l * M + i
            inv_std(pool, f_ve[:], f_rs[:], f_mv[:, :, 1], G["mv"], m + 1, G["ve"], G["rs"])
            until(pool, G["yn"], m - 1)
            nc.gpsimd.tensor_tensor(f_yb[:, p], f_y[:, p], b2_s[:, l, :].unsqueeze(1).broadcast_to([P, FT, D]),
                                    ALU.add).then_inc(G["yb"], 1)

        def f_pool_end(pool, l, i, odd=False):
            if l == L - 1:
                p = par_of(i, odd)
                inv_std(pool, f_ve2[:], f_rs2[:], f_mv2[:, :, 1], G["mv2"], i + 1, G["ve2"], G["rs2"])
                pool.wait_ge(G["ln"], i + 1)
                until(pool, G[f"out{p}"], 32 * (M // 2 * l) + 32 * (half_count(i) - 1))
                nc.gpsimd.tensor_tensor(f_o[:, p], f_ln[:], f_x1[:, p], ALU.add).then_inc(G["o"], 1)

        def f_act(act, l, i, odd=False):
            m = l * M + i
            for c in range(HC):
                w = HW[c]
                act.wait_ge(G["g_ps"], HC * m + c + 1)
                until(act, G["u"], HC * m + c - 1)
                nc.scalar.activation(f_g[0:w, c % 2, :], bank[2 + c % 2][0:w, :], ACT.Gelu,
                                     bias=b1_s[0:w, l, 1, c:c + 1]).then_inc(G["g"], 1)

        def f_dve_in(dve, l, i, odd=False):
            p = par_of(i, odd)
            m = l * M + i
            dve.wait_ge(G[f"in{p}"], f_in_count(l, i))
            until(dve, G["rs"], m)
            stats(dve, f_h[:, p], f_st, f_mv, FT, G["st"], FT * (m + 1), G["mv"])
            dve.wait_ge(G["rs"], m + 1)
            until(dve, G["hT_ps"], m)
            for t in range(FT):
                j = normal(f_xn, f_h[:, p], f_mv, f_rs, t)
            j.then_inc(G["xn"], 1)

        def f_dve_turned(dve, l, i, odd=False):
            p = par_of(i, odd)
            m = l * M + i
            dve.wait_ge(G["hT_ps"], m + 1)
            until(dve, G["a_ps"], HC * (m - 1))
            nc.vector.tensor_scalar(f_hT[:, p, :], bank[0][:], lngb[:, l, 0:1], lngb[:, l, 1:2], ALU.mult, ALU.add
                                    ).then_inc(G["hT"], 1)

        def f_dve_gate(dve, l, i, odd=False):
            p = par_of(i, odd)
            m = l * M + i
            until(dve, G["w_ps"], m - 1)
            for c in range(HC):
                w = HW[c]
                dve.wait_ge(G["g"], HC * m + c + 1)
                dve.wait_ge(G["a_ps"], HC * m + c + 1)
                nc.vector.scalar_tensor_tensor(out=f_u[0:w, p, c, :], in0=bank[4 + c % 2][0:w, :],
                                               scalar=b1_s[0:w, l, 0, c:c + 1], in1=f_g[0:w, c % 2, :],
                                               op0=ALU.add, op1=ALU.mult).then_inc(G["u"], 1)

        def f_dve_out(dve, l, i, odd=False):
            p = par_of(i, odd)
            m = l * M + i
            dve.wait_ge(G["yb"], m + 1)
            dve.wait_ge(G["w_ps"], m + 1)
            if l < L - 1:
                until(dve, G[f"out{p}"], 32 * (half_count(i) - 1) + 32 * (M // 2 * l))
            elif isinstance(i, int) and i < 2:
                until(dve, G[f"out{p}"], 32 * (M // 2 * l))
            nc.vector.tensor_tensor(f_yn[:, p].rearrange("p t d -> p (t d)"), f_yb[:, p].rearrange("p t d -> p (t d)"),
                                    bank[6 + p][:], ALU.add).then_inc(G["yn"], 1)
            if l == L - 1:
                dve.wait_ge(G["yn"], m + 1)
                until(dve, G["rs2"], i)
                stats(dve, f_yn[:, p], f_st2, f_mv2, FT, G["st2"], FT * (i + 1), G["mv2"])
                dve.wait_ge(G["rs2"], i + 1)
                until(dve, G["o"], i)
                for t in range(FT):
                    j = normal(f_ln, f_yn[:, p], f_mv2, f_rs2, t)
                j.then_inc(G["ln"], 1)

        def f_pe_turn(pe, l, i, odd=False):
            m = l * M + i
            pe.wait_ge(G["xn"], m + 1)
            until(pe, G["hT"], m)
            for t in range(FT):
                j = nc.tensor.transpose(bank[0][:, t * P:(t + 1) * P], f_xn[:, t, :], ident[:])
            j.then_inc(G["hT_ps"], 1)

        def f_pe_up(pe, l, i, odd=False):
            p = par_of(i, odd)
            m = l * M + i
            pe.wait_ge(G["hT"], m + 1)
            for c in range(HC):
                w = HW[c]
                k = HC * m + c
                until(pe, G["g"], k - 1 if c else k)
                nc.tensor.matmul(bank[2 + c % 2][0:w, :], w1_s[:, l, HID + c * P:HID + c * P + w], f_hT[:, p, :],
                                 start=True, stop=True).then_inc(G["g_ps"], 1)
                until(pe, G["u"], k - 1 if c else k)
                nc.tensor.matmul(bank[4 + c % 2][0:w, :], w1_s[:, l, c * P:c * P + w], f_hT[:, p, :],
                                 start=True, stop=True).then_inc(G["a_ps"], 1)

        def f_pe_down(pe, l, i, odd=False):
            p = par_of(i, odd)
            m = l * M + i
            pe.wait_ge(G["u"], HC * (m + 1))
            until(pe, G["yn"], m - 1)
            for t in range(FT):
                for c in range(HC):
                    j = nc.tensor.matmul(bank[6 + p][:, t * P:(t + 1) * P], f_u[0:HW[c], p, c, t * P:(t + 1) * P],
                                         w2_s[0:HW[c], l, c, :], start=(c == 0), stop=(c == HC - 1))
            j.then_inc(G["w_ps"], 1)

        def in_loop(eng, first, body, last):
            first()
            body(1, True)
            body(2, False)
            with eng.Fori(3, M - 2, 2) as i:
                body(i, True)
                body(i + 1, False)
            last()

        def phase(eng, k):
            eng.wait_ge(phase_end, k)

        @block.sync
        def _(sp):
            setup_sync(sp)
            steps(sp, lambda *a, **k: a_sync(sp, *a, **k))
            for p in range(2):
                sp.wait_ge(A[f"out{p}"], 16 * B)
            sp.wait_ge(zero_out, 16 * 2 * L)
            sp.sem_inc(phase_end, 1)
            for l in range(L):
                phase(sp, 2 * l + 1)

                def t_step(i, now, behind, odd=True):
                    t_sync(sp, l, i, now, behind, odd)
                    if behind:
                        t_store(sp, l, i, odd)
                t_steps(sp, t_step)
                sp.wait_ge(T["out"], 16 * B * (l + 1))
                sp.sem_inc(phase_end, 1)
                phase(sp, 2 * l + 2)

                def both(i, odd=False):
                    f_sync(sp, l, i + 1, not odd)
                    f_store(sp, l, i, odd)
                in_loop(sp, lambda: (f_sync(sp, l, 0), f_sync(sp, l, 1), f_store(sp, l, 0)), both,
                        lambda: f_store(sp, l, M - 1))
                for p in range(2):
                    sp.wait_ge(G[f"out{p}"], 32 * (M // 2) * (l + 1))
                sp.sem_inc(phase_end, 1)

        @block.gpsimd
        def _(pool):
            setup_gpsimd(pool)
            setup_done(pool)
            steps(pool, lambda *a, **k: a_pool(pool, *a, **k))
            for l in range(L):
                phase(pool, 2 * l + 1)
                t_steps(pool, lambda *a, **k: t_pool(pool, l, *a, **k))
                phase(pool, 2 * l + 2)

                def both(i, odd=False):
                    f_pool(pool, l, i + 1, not odd)
                    f_pool_end(pool, l, i, odd)
                in_loop(pool, lambda: (f_pool(pool, l, 0), f_pool(pool, l, 1), f_pool_end(pool, l, 0)), both,
                        lambda: f_pool_end(pool, l, M - 1))

        @block.scalar
        def _(act):
            setup_done(act)
            steps(act, lambda *a, **k: a_act(act, *a, **k))
            for l in range(L):
                phase(act, 2 * l + 1)
                t_steps(act, lambda *a, **k: t_act(act, l, *a, **k))
                phase(act, 2 * l + 2)
                in_loop(act, lambda: f_act(act, l, 0), lambda i, odd: f_act(act, l, i, odd),
                        lambda: f_act(act, l, M - 1))

        @block.vector
        def _(dve):
            setup_vector(dve)
            setup_done(dve)
            steps(dve, lambda *a, **k: a_dve(dve, *a, **k))
            for l in range(L):
                phase(dve, 2 * l + 1)
                t_steps(dve, lambda *a, **k: t_dve(dve, l, *a, **k))
                phase(dve, 2 * l + 2)

                def both(i, odd=False, ahead=True):
                    if ahead:
                        f_dve_in(dve, l, i + 1, not odd)
                    f_dve_gate(dve, l, i, odd)
                    if ahead:
                        f_dve_turned(dve, l, i + 1, not odd)
                    f_dve_out(dve, l, i, odd)
                in_loop(dve, lambda: (f_dve_in(dve, l, 0), f_dve_turned(dve, l, 0), both(0)), both,
                        lambda: both(M - 1, True, ahead=False))

        @block.tensor
        def _(pe):
            setup_tensor(pe)
            setup_done(pe)
            steps(pe, lambda *a, **k: a_pe(pe, *a, **k))
            for l in range(L):
                phase(pe, 2 * l + 1)
                t_steps(pe, lambda *a, **k: t_pe(pe, l, *a, **k))
                phase(pe, 2 * l + 2)

                def both(i, odd=False, ahead=True):
                    f_pe_up(pe, l, i, odd)
                    if ahead:
                        f_pe_turn(pe, l, i + 1, not odd)
                    f_pe_down(pe, l, i, odd)
                in_loop(pe, lambda: (f_pe_turn(pe, l, 0), both(0)), both, lambda: both(M - 1, True, ahead=False))


_INS = ["L0_attn_x", "L0_attn_w_qkv", "L0_attn_w_out", "L0_attn_b_out", "L0_attn_random_features", "L0_ffn_wqkv",
        "L0_ffn_q_scale", "L0_ffn_k_scale", "L0_ffn_wo", "L0_ffn_ln_g", "L0_ffn_ln_b", "L0_ffn_w1", "L0_ffn_b1",
        "L0_ffn_w2", "L0_ffn_b2"]


def kernel(**inputs):
    import numpy as _np
    import concourse.bacc as _bacc
    from concourse import mybir as _mybir
    from concourse.bass_utils import run_bass_kernel_spmd as _run

    nc = _bacc.Bacc("TRN2", target_bir_lowering=False, num_devices=1)
    arrays, args = {}, []
    for name in _INS:
        a = _np.ascontiguousarray(inputs[name])
        arrays[f"in_{name}"] = a
        args.append(nc.dram_tensor(f"in_{name}", a.shape, _mybir.dt.from_np(a.dtype), kind="ExternalInput").ap())
    shape = inputs["L0_attn_x"].shape
    args.append(nc.dram_tensor("out_0", shape, _mybir.dt.float32, kind="ExternalOutput").ap())
    build(nc, *args)
    r = _run(nc, [arrays], core_ids=[0])
    return r.results[0]["out_0"]
```

```python
from contextlib import ExitStack

import numpy as np

import concourse.bass as bass
from concourse import mybir

F32 = mybir.dt.float32
BF16 = mybir.dt.bfloat16
ALU = mybir.AluOpType
ACT = mybir.ActivationFunctionType
AX = mybir.AxisListType

P = 128
TPB = 2
ROWS = 257
HEADS_A, DIM_A, FEAT = 16, 8, 64
GH = 8
HEADS, DH, WIN = 8, 64, 64
UH = 4
EPS_LN, EPS_A = 1e-5, 1e-6
MASKED = -2.0 ** 100


def rotary_tables(tokens):
    half = np.arange(0, DH, 2, dtype=np.float32)
    inv = (1.0 / np.power(np.float32(10000.0), half / np.float32(DH))).astype(np.float32)
    t = np.arange(tokens, dtype=np.float32)
    fr = t[:, None] * inv[None, :]
    fr = np.concatenate([fr, fr], -1).astype(np.float64)
    base = (half + np.float32(0.4 * DH)) / np.float32(1.4 * DH)
    power = (t - tokens // 2) / np.float32(WIN // 2)
    sc = np.power(base[None, :].astype(np.float64), power[:, None].astype(np.float64))
    sc = np.concatenate([sc, sc], -1)
    sign = np.concatenate([-np.ones(DH // 2), np.ones(DH // 2)])[None, :]
    tabs = [np.cos(fr) * sc * 8.0, sign * np.sin(fr) * sc * 8.0, np.cos(fr) / sc, sign * np.sin(fr) / sc]
    out = np.stack(tabs).astype(np.float32)
    return np.ascontiguousarray(out.reshape(4, tokens // P, P, DH).transpose(2, 0, 1, 3).reshape(P, -1))


def window_masks():
    i = np.arange(WIN)[:, None]
    j = np.arange(WIN)[None, :]
    own = np.where(i < j, MASKED, 0.0)
    before = np.where(i > j, MASKED, 0.0)
    odd = np.concatenate([before, own], 1)
    even = np.concatenate([own, before], 1)
    first = np.concatenate([own, np.full((WIN, WIN), MASKED)], 1)
    both = [np.concatenate([first, odd], 0), np.concatenate([even, odd], 0)]
    return np.ascontiguousarray(np.stack([np.tile(m, (1, UH)) for m in both], 1).astype(np.float32).reshape(P, -1))


def norm_rows():
    neg = np.zeros((72, GH * FEAT), np.float32)
    ones = np.zeros((64, GH), np.float32)
    for h in range(GH):
        neg[64 + h, h * FEAT:(h + 1) * FEAT] = -1.0
        ones[h * DIM_A:(h + 1) * DIM_A, h] = 1.0
    return neg, ones


def build(nc, x, w_qkv, w_out, b_out, rf, wqkv, q_scale, k_scale, wo, ln_g, ln_b, w1, b1, w2, b2, out,
          upto=5):
    B, N, D = x.shape
    assert N == TPB * P and D == P
    L, _, QKV = wqkv.shape
    INNER = QKV // 3
    HID = w2.shape[1]
    HC = (HID + P - 1) // P
    HW = [min(P, HID - c * P) for c in range(HC)]

    tabs_np = rotary_tables(N)
    mask_np = window_masks()
    neg_np, ones_np = norm_rows()
    tabs_c = nc.inline_tensor(tabs_np, name="rotary_tables")
    mask_c = nc.inline_tensor(mask_np, name="window_masks")
    neg_c = nc.inline_tensor(neg_np, name="norm_rows")
    ones_c = nc.inline_tensor(ones_np, name="head_ones")

    with ExitStack() as ctx:
        def sb(name, shape, dt=F32):
            return ctx.enter_context(nc.sbuf_tensor(name, shape, dt))

        def sem(name):
            return ctx.enter_context(nc.semaphore(name))

        x1_d = nc.dram_tensor("x1_d", [B, N, D], F32, kind="Internal").ap()
        y_d = [nc.dram_tensor(f"y{n}_d", [B, ROWS, D], F32, kind="Internal").ap() for n in range(2 * L)]

        ident = sb("ident", [P, P])
        ident_b = sb("ident_b", [P, P], BF16)
        zrow = sb("zrow", [B, D])
        half_neg = sb("half_neg", [P, 16])
        tabs = sb("tabs", [P, 4, TPB, DH])
        masks_f = sb("masks_f", [P, TPB, UH * P])
        masks = sb("masks", [P, TPB, UH * P], BF16)
        rfa = sb("rfa", [72, GH * FEAT])
        rfb = sb("rfb", [72, GH * FEAT])
        rfn = sb("rfn", [72, GH * FEAT])
        hones = sb("hones", [64, GH])
        wq_raw = sb("wq_raw", [P, 4, P])
        wT = sb("wT", [P, 4, P])
        bout = sb("bout", [P, D])
        wqkv_s = sb("wqkv_s", [P, L, QKV])
        wo_s = sb("wo_s", [P, L, INNER // P, D])
        w1_s = sb("w1_s", [P, L, 2 * HID])
        w2_s = sb("w2_s", [P, L, HC, D])
        scales = sb("scales", [P, 2 * L, 2, DH])
        ltab = sb("ltab", [P, L, 4, TPB, DH])
        lngb = sb("lngb", [P, L, 2])
        b1_s = sb("b1_s", [P, L, 2, HC])
        b2_s = sb("b2_s", [P, L, D])

        pairs = [ctx.enter_context(nc.psum_tensor(f"banks{2 * n}", [P, 1024], F32)) for n in range(4)]
        psA = [pairs[0][:, :], pairs[1][:, :]]
        bank = [pairs[n // 2][:, 512 * (n % 2):512 * (n % 2) + 512] for n in range(8)]

        phase_end = sem("phase_end")
        w_in = sem("w_in")
        set_id = sem("set_id")
        zero_out = sem("zero_out")
        set_ps = sem("set_ps")
        set_done = sem("set_done")
        set_c = sem("set_c")
        passed = sem("passed")

        n_w = [0]

        def load(eng, dst, src):
            eng.dma_start(dst, src).then_inc(w_in, 16)
            n_w[0] += 16

        block = ctx.enter_context(nc.Block())

        def setup_sync(sp):
            sp.wait_ge(set_id, 1)
            for h in range(GH):
                with nc.allow_non_contiguous_dma(reason="a 64x8 matrix, once"):
                    load(sp, rfb[h * DIM_A:(h + 1) * DIM_A, h * FEAT:(h + 1) * FEAT], rf.rearrange("f d -> d f"))
            load(sp, wq_raw[:, 0:3, :], w_qkv.rearrange("(c p) i -> p c i", p=P))
            load(sp, wq_raw[:, 3, :], w_out)
            load(sp, rfn[:, :], neg_c.ap() if hasattr(neg_c, "ap") else neg_c)
            load(sp, hones[:, :], ones_c.ap() if hasattr(ones_c, "ap") else ones_c)
            load(sp, bout[:, :], b_out.rearrange("(a d) -> a d", a=1).broadcast_to([P, D]))
            load(sp, tabs[:].rearrange("p a t d -> p (a t d)"), tabs_c.ap() if hasattr(tabs_c, "ap") else tabs_c)
            load(sp, masks_f[:].rearrange("p t d -> p (t d)"), mask_c.ap() if hasattr(mask_c, "ap") else mask_c)
            load(sp, wqkv_s[:], wqkv.rearrange("l p n -> p l n"))
            load(sp, w1_s[:], w1.rearrange("l p n -> p l n"))
            for l in range(L):
                load(sp, wo_s[:, l], wo[l].rearrange("(c p) d -> p c d", p=P))
                for c in range(HC):
                    load(sp, w2_s[0:HW[c], l, c, :], w2[l, c * P:c * P + HW[c], :])
                    for g in range(2):
                        with nc.allow_non_contiguous_dma(reason="a bias, once"):
                            load(sp, b1_s[0:HW[c], l, g, c:c + 1],
                                 b1[l, g * HID + c * P:g * HID + c * P + HW[c]].rearrange("(p a) -> p a", a=1))
                with nc.allow_non_contiguous_dma(reason="a gain and a bias, once"):
                    load(sp, lngb[:, l, 0:1], ln_g[l].rearrange("(p a) -> p a", a=1))
                    load(sp, lngb[:, l, 1:2], ln_b[l].rearrange("(p a) -> p a", a=1))
                load(sp, b2_s[:, l, :], b2[l:l + 1, :].broadcast_to([P, D]))
                for s, src in enumerate((q_scale, k_scale)):
                    load(sp, scales[:, 2 * l + s, 0, :], src[l:l + 1, :].broadcast_to([P, DH]))
                    load(sp, scales[:, 2 * l + s, 1, 0:DH // 2], src[l:l + 1, DH // 2:DH].broadcast_to([P, DH // 2]))
                    load(sp, scales[:, 2 * l + s, 1, DH // 2:DH], src[l:l + 1, 0:DH // 2].broadcast_to([P, DH // 2]))
            for n in range(2 * L):
                sp.dma_start(y_d[n][:, 0, :], zrow[:, :]).then_inc(zero_out, 16)

        def setup_gpsimd(pool):
            nc.gpsimd.memset(ident[:], 0.0).then_inc(set_c, 1)
            pool.wait_ge(set_c, 1)
            nc.gpsimd.affine_select(out=ident[:], in_=ident[:], compare_op=ALU.not_equal, fill=1.0, base=0,
                                    pattern=[[-1, P]], channel_multiplier=1).then_inc(set_c, 1)
            nc.gpsimd.memset(half_neg[:], -0.5).then_inc(set_c, 1)

        def setup_vector(dve):
            nc.vector.memset(zrow[:], 0.0)
            nc.vector.memset(rfb[:], 0.0).then_inc(set_id, 1)
            dve.wait_ge(set_c, 2)
            nc.vector.tensor_copy(ident_b[:], ident[:]).then_inc(set_done, 1)
            dve.wait_ge(w_in, n_w[0])
            nc.vector.scalar_tensor_tensor(out=rfa[:], in0=rfb[:], scalar=FEAT ** -0.5, in1=rfn[:],
                                           op0=ALU.mult, op1=ALU.add)
            nc.vector.tensor_copy(masks[:], masks_f[:])
            for l in range(L):
                for a in range(4):
                    s = scales[:, 2 * l + a // 2, a % 2, :].unsqueeze(1).broadcast_to([P, TPB, DH])
                    nc.vector.tensor_tensor(ltab[:, l, a], tabs[:, a], s, ALU.mult).then_inc(set_done, 1)
            for c in range(4):
                dve.wait_ge(set_ps, c + 1)
                nc.vector.tensor_copy(wT[:, c, :], bank[c][:, 0:P]).then_inc(set_done, 1)
            nc.vector.memset(kvb[:], 0.0).then_inc(set_done, 1)
            nc.vector.memset(vaug[:], 1.0).then_inc(set_done, 1)
            nc.vector.memset(vt[:], 1.0).then_inc(set_done, 1)
            nc.vector.memset(ve[:], 1.0).then_inc(set_done, 1)

        N_SET = 1 + 4 * L + 4 + 4

        def setup_tensor(pe):
            pe.wait_ge(set_c, 2)
            pe.wait_ge(w_in, n_w[0])
            for c in range(4):
                nc.tensor.transpose(bank[c][:, 0:P], wq_raw[:, c, :], ident[:]).then_inc(set_ps, 1)

        def setup_done(eng):
            eng.wait_ge(set_done, N_SET)
            eng.wait_ge(set_c, 3)
            eng.wait_ge(w_in, n_w[0])

        kvb = sb("kvb", [P, GH, 18])
        vaug = sb("vaug", [P, 2, TPB, HEADS_A, 9])
        only_a = ctx.enter_context(ExitStack())

        def sa(name, shape, dt=F32):
            return only_a.enter_context(nc.sbuf_tensor(name, shape, dt))

        xa = sa("xa", [P, 2, TPB, D])
        a_st = sa("a_st", [P, TPB, 6])
        a_mv = sa("a_mv", [P, TPB, 2])
        a_ve = sa("a_ve", [P, TPB])
        a_rs = sa("a_rs", [P, TPB])
        a_xn = sa("a_xn", [P, TPB, D])
        a_xT = sa("a_xT", [P, N])
        aug = sa("aug", [72, 2, 4, N])
        a_sq = sa("a_sq", [64, 4, N])
        kf = sa("kf", [P, TPB, 2, GH * FEAT])
        qf = sa("qf", [P, GH, N])
        a_rd = sa("a_rd", [P, TPB, HEADS_A])
        a_o = sa("a_o", [P, TPB, D])
        a_oT = sa("a_oT", [P, N])
        a_y = sa("a_y", [P, TPB, D])
        xr = sa("xr", [P, 2, TPB, D])
        a_y2 = sa("a_y2", [P, TPB, D])
        a_rr = sa("a_rr", [P, TPB * HEADS_A])
        a_st2, a_st3 = (sa(f"a_st{k}", [P, TPB, 6]) for k in (2, 3))
        a_mv2, a_mv3 = (sa(f"a_mv{k}", [P, TPB, 2]) for k in (2, 3))
        a_ve2, a_ve3, a_rs2, a_rs3 = (sa(k, [P, TPB]) for k in ("a_ve2", "a_ve3", "a_rs2", "a_rs3"))
        a_x1 = sa("a_x1", [P, 2, TPB, D])
        a_yo = sa("a_yo", [P, 2, TPB, D])

        A = {k: sem("A_" + k) for k in (
            "x_in0", "x_in1", "st", "mv", "ve", "rs", "xn", "xT_ps", "xT", "qk_ps", "v_ps", "sq", "v", "ss_ps",
            "ss", "nrm", "kf_ps", "kf", "qf_ps", "qf", "kv_ps", "kv", "o_ps", "rd", "o", "oT_ps", "oT", "w_ps",
            "y", "xr_in0", "xr_in1", "rs_xn", "mv2", "mv3", "st2", "ve2", "rs2", "yn", "x1", "st3", "ve3", "rs3", "yo", "out0", "out1")}

        only_a.close()

        FT = 2 * TPB
        f_h = sb("f_h", [P, 2, FT, D])
        f_y = sb("f_y", [P, 2, FT, D])
        f_x1 = sb("f_x1", [P, 2, FT, D])
        f_st = sb("f_st", [P, FT, 6])
        f_mv = sb("f_mv", [P, FT, 2])
        f_ve = sb("f_ve", [P, FT])
        f_rs = sb("f_rs", [P, FT])
        f_xn = sb("f_xn", [P, FT, D])
        f_hT = sb("f_hT", [P, 2, FT * P])
        f_g = sb("f_g", [P, 2, FT * P])
        f_u = sb("f_u", [P, 2, HC, FT * P])
        f_yb = sb("f_yb", [P, 2, FT, D])
        f_yn = sb("f_yn", [P, 2, FT, D])
        f_st2 = sb("f_st2", [P, FT, 6])
        f_mv2 = sb("f_mv2", [P, FT, 2])
        f_ve2 = sb("f_ve2", [P, FT])
        f_rs2 = sb("f_rs2", [P, FT])
        f_ln = sb("f_ln", [P, FT, D])
        f_o = sb("f_o", [P, 2, FT, D])

        hs = sb("hs", [P, 2, TPB, D])
        yt = sb("yt", [P, 2, TPB, D])
        hT = sb("hT", [P, N])
        qraw = sb("qraw", [P, TPB, INNER])
        kraw = sb("kraw", [P, TPB, INNER])
        sq = sb("sq", [P, 2 * INNER])
        ss = sb("ss", [P, 2, TPB, 2 * HEADS])
        rr = sb("rr", [P, 2, TPB, 2 * HEADS])
        kn = sb("kn", [P, INNER])
        m1k = sb("m1k", [P, INNER])
        m2k = sb("m2k", [P, INNER])
        m1q = sb("m1q", [P, INNER])
        m2q = sb("m2q", [P, INNER])
        qrot = sb("qrot", [P, TPB, INNER])
        krot = sb("krot", [P, TPB, INNER])
        qT = sb("qT", [P, TPB, 4, P])
        kT = sb("kT", [P, 4, TPB, P])
        vt = sb("vt", [P, 2, TPB, HEADS, DH + 1])
        ve = sb("ve", [P, 2, HEADS, DH + 1])
        mx = sb("mx", [P, 2, UH])
        nb = sb("nb", [P, 2, UH])
        pr = sb("pr", [P, 2, UH, P])
        pT = sb("pT", [P, 2, UH, P])
        rl = sb("rl", [P, 2, UH])
        ot = sb("ot", [P, TPB, INNER])
        oT = sb("oT", [P, TPB, 4, P])
        yn = sb("yn", [P, 2, TPB, D])

        T = {k: sem("T_" + k) for k in (
            "h_in0", "h_in1", "y_in0", "y_in1", "hT_ps", "hT", "q_ps", "k_ps", "v_ps", "q", "k", "v", "ss", "rr",
            "kn", "km", "krot", "qm", "qrot", "qT_ps", "qT", "kT_ps", "kT", "s_ps", "mx", "nb", "p", "pT_ps", "pTa",
            "pTb", "o_ps", "rl", "o", "oT_ps", "oT", "w_ps", "yn", "out0", "out1", "ssm")}

        G = {k: sem("F_" + k) for k in (
            "in0", "in1", "x1_in0", "x1_in1", "st", "mv", "ve", "rs", "xn", "hT_ps", "hT", "g_ps", "a_ps", "g", "u", "yb", "w_ps", "yn",
            "st2", "mv2", "ve2", "rs2", "ln", "o", "out0", "out1")}

        def until(eng, s, v):
            if isinstance(v, int) and v <= 0:
                return
            eng.wait_ge(s, v)

        def apart(eng):
            eng.sem_inc(passed, 1)

        def inv_std(pool, ve, rs, mv, stats_ready, v, ve_sem, rs_sem):
            until(pool, stats_ready, v)
            apart(pool)
            nc.gpsimd.tensor_scalar(ve, mv, EPS_LN, None, ALU.add).then_inc(ve_sem, 1)
            pool.wait_ge(ve_sem, v)
            nc.gpsimd.tensor_tensor(rs, ve, half_neg[:, 0:ve.shape[-1]], ALU.pow).then_inc(rs_sem, 1)

        def stats(dve, src, st, mv, tiles, st_sem, v, mv_sem):
            for t in range(tiles):
                nc.vector.bn_stats(st[:, t, :], src[:, t, :]).then_inc(st_sem, 1)
            dve.wait_ge(st_sem, v)
            apart(dve)
            for t in range(tiles):
                i = nc.vector.bn_aggr(mv[:, t, :], st[:, t, :])
            i.then_inc(mv_sem, 1)

        def normal(dst, src, mv, rs, t):
            return nc.vector.tensor_scalar(dst[:, t, :], src[:, t, :], mv[:, t, 0:1], rs[:, t:t + 1],
                                           ALU.subtract, ALU.mult)

        def steps(eng, step):
            step(-1, True, False, False)
            step(0, True, True, False)
            step(1, True, True, True)
            step(2, True, True, True)
            with eng.Fori(3, B - 2, 2) as i:
                step(i, True, True, True)
                step(i + 1, True, True, True, odd=False)
            step(B - 1, False, True, True)
            step(B, False, False, True)

        def par_of(i, odd):
            return i % 2 if isinstance(i, int) else int(odd)

        def a_sync(sp, i, ahead, now, behind, odd=True):
            p = par_of(i, odd)
            if ahead:
                until(sp, A["xn"], i)
                sp.dma_start(xa[:, 1 - p], x[bass.ds(i + 1, 1)].rearrange("b (t p) d -> p (b t) d", p=P)
                             ).then_inc(A[f"x_in{1 - p}"], 16)
            if behind:
                n = i - 1
                until(sp, A["x1"], n - 1)
                sp.dma_start(xr[:, 1 - p], x[bass.ds(n, 1)].rearrange("b (t p) d -> p (b t) d", p=P)
                             ).then_inc(A[f"xr_in{1 - p}"], 16)
                sp.wait_ge(A["x1"], n + 1)
                sp.dma_start(x1_d[bass.ds(n, 1)].rearrange("b (t p) d -> p (b t) d", p=P), a_x1[:, 1 - p]
                             ).then_inc(A[f"out{1 - p}"], 16)
                sp.wait_ge(A["yo"], n + 1)
                sp.dma_start(y_d[0][bass.ds(n, 1), 1:ROWS, :].rearrange("b (t p) d -> p (b t) d", p=P), a_yo[:, 1 - p]
                             ).then_inc(A[f"out{1 - p}"], 16)

        def a_pool(pool, i, ahead, now, behind, odd=True):
            p = par_of(i, odd)
            if ahead:
                inv_std(pool, a_ve[:], a_rs[:], a_mv[:, :, 1], A["mv"], i + 2, A["ve"], A["rs"])
            if behind:
                n = i - 1
                inv_std(pool, a_ve2[:], a_rs2[:], a_mv2[:, :, 1], A["mv2"], n + 1, A["ve2"], A["rs2"])
                pool.wait_ge(A["yn"], n + 1)
                pool.wait_ge(A[f"xr_in{1 - p}"], 16 * half_count(n))
                until(pool, A[f"out{1 - p}"], 32 * (half_count(n) - 1))
                nc.gpsimd.tensor_tensor(a_x1[:, 1 - p], a_y2[:], xr[:, 1 - p], ALU.add).then_inc(A["x1"], 1)
                inv_std(pool, a_ve3[:], a_rs3[:], a_mv3[:, :, 1], A["mv3"], n + 1, A["ve3"], A["rs3"])

        def a_act(act, i, ahead, now, behind, odd=True):
            p = par_of(i, odd)
            if behind:
                n = i - 1
                until(act, A["kv_ps"], n)
                for t in range(TPB):
                    act.wait_ge(A["kf_ps"], 2 * n + t + 1)
                    nc.scalar.activation(kf[:, t].rearrange("p g n -> p (g n)"), psA[t], ACT.Exp
                                         ).then_inc(A["kf"], 1)
            if now:
                act.wait_ge(A["xT_ps"], i + 1)
                nc.scalar.copy(a_xT[:], bank[6][:, 0:N]).then_inc(A["xT"], 1)
            if behind:
                until(act, A["o_ps"], n)
                act.wait_ge(A["qf_ps"], 2 * n + 1)
                nc.scalar.activation(qf[:, 0:4].rearrange("p j n -> p (j n)"), psA[0], ACT.Exp).then_inc(A["qf"], 1)
            if now:
                for c in range(2):
                    act.wait_ge(A["qk_ps"], 2 * i + c + 1)
                    nc.scalar.activation(a_sq[:, 2 * c:2 * c + 2, :].rearrange("p g n -> p (g n)"),
                                         bank[4 + c][0:64, :], ACT.Square)
                    if c == 0:
                        until(act, A["qf_ps"], 2 * (i - 1))
                    nc.scalar.copy(aug[0:64, p, 2 * c:2 * c + 2, :].rearrange("p g n -> p (g n)"),
                                   bank[4 + c][0:64, :]).then_inc(A["sq"], 1)
            if behind:
                act.wait_ge(A["qf_ps"], 2 * n + 2)
                nc.scalar.activation(qf[:, 4:8].rearrange("p j n -> p (j n)"), psA[1], ACT.Exp).then_inc(A["qf"], 1)
            if now:
                act.wait_ge(A["v_ps"], i + 1)
                until(act, A["kv_ps"], i - 1)
                nc.scalar.copy(vaug[:, p, :, :, 0:DIM_A].rearrange("p t h d -> p (t h) d"),
                               bank[6][:, N:2 * N].rearrange("p (h d) -> p h d", d=DIM_A)).then_inc(A["v"], 1)
            if behind:
                act.wait_ge(A["oT_ps"], n + 1)
                nc.scalar.copy(a_oT[:], bank[6][:, 0:N]).then_inc(A["oT"], 1)
            if now:
                for c in range(2):
                    act.wait_ge(A["ss_ps"], 2 * i + c + 1)
                    nc.scalar.activation(aug[64:72, p, 2 * c:2 * c + 2, :].rearrange("p g n -> p (g n)"),
                                         bank[4 + c][64:72, :], ACT.Sqrt).then_inc(A["nrm"], 1)

        def a_pe(pe, i, ahead, now, behind, odd=True):
            p = par_of(i, odd)
            n = i - 1
            if behind:
                pe.wait_ge(A["nrm"], 2 * (n + 1))
                for t in range(TPB):
                    until(pe, A["qf"], 2 * n - 1 + t)
                    for g in range(2):
                        m = nc.tensor.matmul(bank[2 * t + g][:], aug[:, 1 - p, 2 + g, t * P:(t + 1) * P], rfa[:],
                                             start=True, stop=True)
                    m.then_inc(A["kf_ps"], 1)
            if now:
                pe.wait_ge(A["rs_xn"], i + 1)
                until(pe, A["y"], i - 1)
                until(pe, A["v"], i)
                for t in range(TPB):
                    m = nc.tensor.transpose(bank[6][:, t * P:(t + 1) * P], a_xn[:, t, :], ident[:])
                m.then_inc(A["xT_ps"], 1)
            if behind:
                for g in range(2):
                    pe.wait_ge(A["kf"], 2 * n + 1 + g)
                    for j in range(4):
                        m = nc.tensor.matmul(bank[2 * g + j // 2][:, (j % 2) * N:(j % 2 + 1) * N],
                                             rfa[:, j * P:(j + 1) * P], aug[:, 1 - p, g, :], start=True, stop=True)
                    m.then_inc(A["qf_ps"], 1)
                    if g == 0 and now:
                        pe.wait_ge(A["xT"], i + 1)
                        until(pe, A["nrm"], 2 * i)
                        a_qk(pe)
            if now:
                if not behind:
                    pe.wait_ge(A["xT"], i + 1)
                    until(pe, A["nrm"], 2 * i)
                    a_qk(pe)
                for t in range(TPB):
                    m = nc.tensor.matmul(bank[6][:, N + t * P:N + (t + 1) * P], a_xT[:, t * P:(t + 1) * P],
                                         wT[:, 2, :], start=True, stop=True)
                m.then_inc(A["v_ps"], 1)
            if behind:
                pe.wait_ge(A["kf"], 2 * n + 2)
                pe.wait_ge(A["v"], n + 1)
                until(pe, A["o"], n)
                for j in range(GH):
                    for t in range(TPB):
                        m = nc.tensor.matmul(bank[7][:, 18 * j:18 * j + 18],
                                             kf[:, t, j // 4, (j % 4) * P:(j % 4 + 1) * P],
                                             vaug[:, 1 - p, t, 2 * j:2 * j + 2, :].rearrange("p h d -> p (h d)"),
                                             start=(t == 0), stop=(t == TPB - 1))
                m.then_inc(A["kv_ps"], 1)
            if now:
                pe.wait_ge(A["sq"], 2 * i + 2)
                apart(pe)
                for c in range(2):
                    nc.tensor.matmul(bank[4 + c][64:72, :], hones[:], a_sq[:, 2 * c:2 * c + 2, :].rearrange(
                        "p g n -> p (g n)"), start=True, stop=True).then_inc(A["ss_ps"], 1)
            if behind:
                pe.wait_ge(A["kv"], n + 1)
                pe.wait_ge(A["qf"], 2 * n + 2)
                for t in range(TPB):
                    for j in range(GH):
                        m = nc.tensor.matmul(bank[7][:, 160 + 144 * t + 18 * j:160 + 144 * t + 18 * j + 18],
                                             qf[:, j, t * P:(t + 1) * P], kvb[:, j, :], start=True, stop=True)
                m.then_inc(A["o_ps"], 1)
                pe.wait_ge(A["o"], n + 1)
                pe.wait_ge(A["v"], i + 1 if now else i)
                for t in range(TPB):
                    m = nc.tensor.transpose(bank[6][:, t * P:(t + 1) * P], a_o[:, t, :], ident[:])
                m.then_inc(A["oT_ps"], 1)
                pe.wait_ge(A["oT"], n + 1)
                for t in range(TPB):
                    m = nc.tensor.matmul(bank[6][:, N + t * P:N + (t + 1) * P], a_oT[:, t * P:(t + 1) * P],
                                         wT[:, 3, :], start=True, stop=True)
                m.then_inc(A["w_ps"], 1)

        def a_qk(pe):
            for c in range(2):
                for g in range(2):
                    m = nc.tensor.matmul(bank[4 + c][0:64, g * N:(g + 1) * N], wT[:, c, 64 * g:64 * g + 64], a_xT[:],
                                         start=True, stop=True)
                m.then_inc(A["qk_ps"], 1)

        def a_dve(dve, i, ahead, now, behind, odd=True):
            p = par_of(i, odd)
            n = i - 1
            if ahead:
                dve.wait_ge(A[f"x_in{1 - p}"], 16 * half_count(i + 1))
                until(dve, A["rs"], i + 1)
                stats(dve, xa[:, 1 - p], a_st, a_mv, TPB, A["st"], 2 * (i + 2), A["mv"])
            if behind:
                dve.wait_ge(A["kv_ps"], n + 1)
                until(dve, A["o_ps"], n)
                for r in range(2):
                    j = nc.vector.tensor_copy(
                        kvb[64 * r:64 * r + 64, :, 9 * r:9 * r + 9],
                        bank[7][64 * r:64 * r + 64, 0:144].rearrange("p (j c) -> p j c", c=18)[:, :, 9 * r:9 * r + 9])
                j.then_inc(A["kv"], 1)
            if ahead:
                dve.wait_ge(A["rs"], i + 2)
                until(dve, A["xT_ps"], i + 1)
                for t in range(TPB):
                    j = normal(a_xn, xa[:, 1 - p], a_mv, a_rs, t)
                    if t == TPB - 1:
                        j.then_inc(A["rs_xn"], 1)
                dve.wait_ge(A["rs_xn"], i + 2)
                dve.sem_inc(A["xn"], 1)
            if behind:
                o = bank[7][:, 160:448].rearrange("p (h c) -> p h c", c=9)
                rd = a_rd[:].rearrange("p t h -> p (t h)")
                dve.wait_ge(A["o_ps"], n + 1)
                nc.vector.tensor_scalar(rd, o[:, :, 8], EPS_A, None, ALU.add).then_inc(A["rd"], 1)
                dve.wait_ge(A["rd"], 2 * n + 1)
                nc.vector.reciprocal(a_rr[:], rd).then_inc(A["rd"], 1)
                dve.wait_ge(A["rd"], 2 * n + 2)
                until(dve, A["oT_ps"], n)
                nc.vector.tensor_tensor(a_o[:].rearrange("p t (h d) -> p (t h) d", d=DIM_A), o[:, :, 0:8],
                                        a_rr[:].unsqueeze(2).broadcast_to([P, 2 * HEADS_A, DIM_A]), ALU.mult
                                        ).then_inc(A["o"], 1)
                dve.wait_ge(A["w_ps"], n + 1)
                nc.vector.tensor_tensor(a_y[:], bank[6][:, N:2 * N].rearrange("p (t d) -> p t d", d=D),
                                        bout[:].unsqueeze(1).broadcast_to([P, TPB, D]), ALU.add).then_inc(A["y"], 1)
                dve.wait_ge(A["y"], n + 1)
                stats(dve, a_y, a_st2, a_mv2, TPB, A["st2"], 2 * (n + 1), A["mv2"])
                dve.wait_ge(A["rs2"], n + 1)
                until(dve, A["x1"], n)
                for t in range(TPB):
                    j = normal(a_y2, a_y, a_mv2, a_rs2, t)
                j.then_inc(A["yn"], 1)
                dve.wait_ge(A["x1"], n + 1)
                stats(dve, a_x1[:, 1 - p], a_st3, a_mv3, TPB, A["st3"], 2 * (n + 1), A["mv3"])
                dve.wait_ge(A["rs3"], n + 1)
                until(dve, A[f"out{1 - p}"], 32 * (half_count(n) - 1))
                for t in range(TPB):
                    j = normal(a_yo[:, 1 - p], a_x1[:, 1 - p], a_mv3, a_rs3, t)
                j.then_inc(A["yo"], 1)

        def half_count(n):
            return n // 2 + 1

        MASK_FIRST = True

        def t_sync(sp, l, i, now, behind, tail, odd=True):
            p = par_of(i, odd)
            if now:
                n = l * B + i
                until(sp, T["hT_ps"], 2 * (n - 1))
                for c, row in ((0, 1), (1, 0)):
                    sp.dma_start(hs[:, p, :, 64 * c:64 * c + 64],
                                 y_d[2 * l][bass.ds(i, 1), row:row + N, 64 * c:64 * c + 64].rearrange(
                                     "b (t p) d -> p (b t) d", p=P)).then_inc(T[f"h_in{p}"], 16)
            if behind:
                b = i - 1
                n = l * B + b
                until(sp, T["yn"], 2 * (n - 1))
                sp.dma_start(yt[:, 1 - p], y_d[2 * l][bass.ds(b, 1), 1:ROWS, :].rearrange(
                    "b (t p) d -> p (b t) d", p=P)).then_inc(T[f"y_in{1 - p}"], 16)
            if tail:
                b = i - 2
                n = l * B + b
                sp.wait_ge(T["yn"], 2 * (n + 1))
                sp.dma_start(y_d[2 * l + 1][bass.ds(b, 1), 1:ROWS, :].rearrange("b (t p) d -> p (b t) d", p=P),
                             yn[:, p]).then_inc(T[f"out{p}"], 16)

        def t_pool(pool, l, i, now, behind, tail, odd=True):
            p = par_of(i, odd)
            if now:
                n = l * B + i
                for t in range(TPB):
                    pool.wait_ge(T["ss"], 2 * n + t + 1)
                    apart(pool)
                    nc.gpsimd.tensor_scalar(ss[:, p, t, :], ss[:, p, t, :], 1e-24, None, ALU.max
                                            ).then_inc(T["ssm"], 1)
                    pool.wait_ge(T["ssm"], 2 * n + t + 1)
                    until(pool, T["p"], 4 * (n - 1))
                    nc.gpsimd.tensor_tensor(rr[:, p, t, :], ss[:, p, t, :], half_neg[:], ALU.pow
                                            ).then_inc(T["rr"], 1)
                    pool.wait_ge(T["q"], 2 * n + t + 1)
                    rotary(nc.gpsimd, pool, qraw[:, t, :], m1q, m2q, qrot[:, t, :], l, 0, t, T["qm"],
                           2 * (2 * n + t + 1), T["qT_ps"], 2 * (n - 1) + t + 1 if not isinstance(n, int) or n else 0,
                           T["qrot"])

        def rotary(on, eng, src, m1, m2, dst, l, a, t, m_sem, m_count, read_sem, read_count, done):
            s3 = src.rearrange("p (h d) -> p h d", d=DH)
            s4 = src.rearrange("p (h c d) -> p h c d", c=2, d=DH // 2)
            d4 = m2[:].rearrange("p (h c d) -> p h c d", c=2, d=DH // 2)
            cos = ltab[:, l, a, t, :].unsqueeze(1).broadcast_to([P, HEADS, DH])
            on.tensor_tensor(m1[:].rearrange("p (h d) -> p h d", d=DH), s3, cos, ALU.mult)
            for c in range(2):
                sin = ltab[:, l, a + 1, t, 32 * c:32 * c + 32].unsqueeze(1).broadcast_to([P, HEADS, DH // 2])
                on.tensor_tensor(d4[:, :, c, :], s4[:, :, 1 - c, :], sin, ALU.mult).then_inc(m_sem, 1)
            eng.wait_ge(m_sem, m_count)
            until(eng, read_sem, read_count)
            on.tensor_tensor(dst, m1[:], m2[:], ALU.add).then_inc(done, 1)

        def t_act(act, l, i, now, behind, tail, odd=True):
            p = par_of(i, odd)
            n1 = l * B + i
            n = n1 - 1

            def exps(u):
                act.wait_ge(T["nb"], 4 * n + u + 1)
                until(act, T["pT_ps"], 4 * n + u - 1)
                for j in range(UH):
                    h = 2 * j + u % 2
                    e = nc.scalar.activation(pr[:, u % 2, j, :], bank[u % 2][:, j * P:(j + 1) * P], ACT.Exp,
                                             bias=nb[:, u % 2, j:j + 1], scale=rr[:, 1 - p, u // 2, h:h + 1])
                e.then_inc(T["p"], 1)

            def qk_in(t):
                act.wait_ge(T["q_ps"], 2 * n1 + t + 1)
                until(act, T["qrot"], 2 * (n1 - 1) + t + 1 if not isinstance(n1, int) or n1 else 0)
                nc.scalar.copy(qraw[:, t, :], bank[6 + t][:])
                until(act, T["ss"], 2 * n1 + t)
                nc.scalar.activation(sq[:, 0:INNER], bank[6 + t][:], ACT.Square).then_inc(T["q"], 1)
                act.wait_ge(T["k_ps"], 2 * n1 + t + 1)
                until(act, T["kn"], 2 * (n1 - 1) + t + 1 if not isinstance(n1, int) or n1 else 0)
                nc.scalar.copy(kraw[:, t, :], bank[7 - t][:])
                nc.scalar.activation(sq[:, INNER:], bank[7 - t][:], ACT.Square).then_inc(T["k"], 1)

            def v_in(t):
                act.wait_ge(T["v_ps"], 2 * n1 + t + 1)
                until(act, T["o_ps"], 4 * (n1 - 1))
                v = bank[6 + t][:].rearrange("p (h d) -> p h d", d=DH)
                nc.scalar.copy(vt[:, p, t, :, 0:DH], v)
                r = 64 * (1 - t)
                nc.scalar.copy(ve[r:r + 64, p, :, 0:DH], v[r:r + 64]).then_inc(T["v"], 1)

            def turned_q(t):
                act.wait_ge(T["qT_ps"], 2 * n + t + 1)
                nc.scalar.copy(qT[:, t].rearrange("p j n -> p (j n)"), bank[2][:]).then_inc(T["qT"], 1)

            def turned_p(u):
                act.wait_ge(T["pT_ps"], 4 * n + u + 1)
                until(act, T["o_ps"], 4 * n + u - 1)
                nc.scalar.copy(pT[:, 1].rearrange("p j n -> p (j n)"), bank[3][:]).then_inc(T["pTb"], 1)

            def turned_o(k, t):
                act.wait_ge(T["oT_ps"], 2 * k + t + 1)
                nc.scalar.copy(oT[:, t].rearrange("p j n -> p (j n)"), bank[2][:]).then_inc(T["oT"], 1)

            if now:
                for t in range(TPB):
                    act.wait_ge(T["hT_ps"], 2 * n1 + t + 1)
                    until(act, T["v_ps"], 2 * n1 - 1 + t)
                    nc.scalar.copy(hT[:, t * P:(t + 1) * P], bank[2 + t][:, 0:P]).then_inc(T["hT"], 1)
            if behind:
                turned_q(0)
            if now:
                qk_in(0)
                v_in(0)
            if tail:
                turned_o(n - 1, 1)
            if behind:
                exps(0)
                exps(1)
                turned_q(1)
            if now:
                qk_in(1)
            if behind:
                turned_p(1)
            if now:
                v_in(1)
            if behind:
                exps(2)
                turned_o(n, 0)
                exps(3)
                turned_p(3)

        def t_dve(dve, l, i, now, behind, tail, odd=True):
            p = par_of(i, odd)
            n1 = l * B + i
            n = n1 - 1

            def peak(u):
                dve.wait_ge(T["s_ps"], 4 * n + u + 1)
                nc.vector.tensor_reduce(mx[:, u % 2, :], bank[u % 2][:].rearrange("p (j k) -> p j k", k=P), AX.X,
                                        ALU.max).then_inc(T["mx"], 1)
                dve.wait_ge(T["mx"], 4 * n + u + 1)
                until(dve, T["p"], 4 * n + u - 1)
                nc.vector.scalar_tensor_tensor(out=nb[:, u % 2, :], in0=mx[:, u % 2, :], scalar=-1.0,
                                               in1=rr[:, 1 - p, u // 2, u % 2:HEADS:2], op0=ALU.mult, op1=ALU.mult
                                               ).then_inc(T["nb"], 1)

            def turned(u):
                dve.wait_ge(T["pT_ps"], 4 * n + u + 1)
                until(dve, T["o_ps"], 4 * n + u - 1)
                nc.vector.tensor_copy(pT[:, 0].rearrange("p j n -> p (j n)"), bank[2 + u // 2][:]
                                      ).then_inc(T["pTa"], 1)

            def divide(k, u):
                o = bank[4 + u % 2][:, 0:UH * (DH + 1)].rearrange("p (j d) -> p j d", d=DH + 1)
                dve.wait_ge(T["o_ps"], 4 * k + u + 1)
                nc.vector.reciprocal(rl[:, u % 2, :], o[:, :, DH]).then_inc(T["rl"], 1)
                dve.wait_ge(T["rl"], 4 * k + u + 1)
                until(dve, T["oT_ps"], 2 * (k - 1) + u // 2 + 1)
                nc.vector.tensor_tensor(ot[:, u // 2].rearrange("p (j c d) -> p j c d", c=2, d=DH)[:, :, u % 2, :],
                                        o[:, :, 0:DH], rl[:, u % 2, :].unsqueeze(2).broadcast_to([P, UH, DH]),
                                        ALU.mult).then_inc(T["o"], 1)

            def squares(t):
                dve.wait_ge(T["k"], 2 * n1 + t + 1)
                nc.vector.tensor_reduce(ss[:, p, t, :], sq[:].rearrange("p (h d) -> p h d", d=DH), AX.X, ALU.add
                                        ).then_inc(T["ss"], 1)

            def keys(t):
                dve.wait_ge(T["rr"], 2 * n1 + t + 1)
                until(dve, T["krot"], 2 * n1 + t)
                nc.vector.tensor_tensor(kn[:].rearrange("p (h d) -> p h d", d=DH),
                                        kraw[:, t, :].rearrange("p (h d) -> p h d", d=DH),
                                        rr[:, p, t, HEADS:].unsqueeze(2).broadcast_to([P, HEADS, DH]), ALU.mult
                                        ).then_inc(T["kn"], 1)
                dve.wait_ge(T["kn"], 2 * n1 + t + 1)
                rotary(nc.vector, dve, kn[:], m1k, m2k, krot[:, t, :], l, 2, t, T["km"], 2 * (2 * n1 + t + 1),
                       T["kT_ps"], 2 * (n1 - 1) + t + 1 if not isinstance(n1, int) or n1 else 0, T["krot"])

            def residual(k, t, q):
                if t == 0:
                    dve.wait_ge(T[f"y_in{q}"], 16 * half_count(k))
                    until(dve, T[f"out{q}"], 16 * (half_count(k) - 1))
                dve.wait_ge(T["w_ps"], 2 * k + t + 1)
                nc.vector.tensor_tensor(yn[:, q, t, :], yt[:, q, t, :], bank[2 + t][:, 0:D], ALU.add
                                        ).then_inc(T["yn"], 1)

            def turned_k(t):
                dve.wait_ge(T["kT_ps"], 2 * n + t + 1)
                nc.vector.tensor_copy(kT[:, :, 1 - t, :], bank[3][:].rearrange("p (j n) -> p j n", n=P)
                                      ).then_inc(T["kT"], 1)

            if tail:
                divide(n - 1, 3)
            if behind:
                turned_k(0)
                peak(0)
            if tail:
                residual(n - 1, 1, p)
            if now:
                squares(0)
            if behind:
                peak(1)
                turned_k(1)
                turned(0)
            if now:
                keys(0)
            if behind:
                divide(n, 0)
            if now:
                squares(1)
            if behind:
                peak(2)
                divide(n, 1)
                peak(3)
                turned(2)
                residual(n, 0, 1 - p)
                divide(n, 2)
            if now:
                keys(1)

        def t_pe(pe, l, i, now, behind, tail, odd=True):
            p = par_of(i, odd)
            n1 = l * B + i
            n = n1 - 1

            def turn(src, t, b, into):
                for j in range(4):
                    m = nc.tensor.transpose(bank[b][:, j * P:(j + 1) * P], src[:, t, j * P:(j + 1) * P], ident[:])
                m.then_inc(into, 1)

            def project(t):
                pe.wait_ge(T["hT"], 2 * n1 + t + 1)
                if t == 0:
                    until(pe, T["k"], 2 * n1)
                else:
                    pe.wait_ge(T["k"], 2 * n1 + 1)
                nc.tensor.matmul(bank[6 + t][:], hT[:, t * P:(t + 1) * P], wqkv_s[:, l, 0:INNER],
                                 start=True, stop=True).then_inc(T["q_ps"], 1)
                until(pe, T["v"], 2 * n1 + t)
                nc.tensor.matmul(bank[7 - t][:], hT[:, t * P:(t + 1) * P], wqkv_s[:, l, INNER:2 * INNER],
                                 start=True, stop=True).then_inc(T["k_ps"], 1)
                pe.wait_ge(T["q"], 2 * n1 + t + 1)
                nc.tensor.matmul(bank[6 + t][:], hT[:, t * P:(t + 1) * P], wqkv_s[:, l, 2 * INNER:],
                                 start=True, stop=True).then_inc(T["v_ps"], 1)

            def scores(u):
                t, b = u // 2, bank[u % 2]
                pe.wait_ge(T["qT"], 2 * n + t + 1)
                pe.wait_ge(T["kT"], 2 * n + t + 1)
                until(pe, T["p"], 4 * n + u - 1)
                nc.tensor.matmul(b[:], ident_b[:], masks[:, t, :], start=True, stop=False, skip_group_check=True)
                for j in range(UH):
                    r, c = 64 * (u % 2), j
                    own = kT[r:r + 64, c, 1 - t, :]
                    for w in range(2):
                        q = qT[r:r + 64, t, c, 64 * w:64 * w + 64]
                        o = b[64 * w:64 * w + 64, j * P:(j + 1) * P]
                        if w == 1:
                            m = nc.tensor.matmul(o, q, own, start=False, stop=True, skip_group_check=True)
                        elif t == 0:
                            nc.tensor.matmul(o[:, 0:64], q, own[:, 0:64], start=False, stop=True,
                                             skip_group_check=True)
                        else:
                            both = kT[r:r + 64, c, :, :].rearrange("p t (w k) -> p (t w) k", k=64)[:, 0:4:3, :]
                            nc.tensor.matmul(o, q, both, start=False, stop=True, skip_group_check=True)
                m.then_inc(T["s_ps"], 1)

            def turn_p(u):
                pe.wait_ge(T["p"], 4 * n + u + 1)
                if u == 0:
                    pe.wait_ge(T["qT"], 2 * n + 2)
                elif u == 1:
                    pe.wait_ge(T["kT"], 2 * n + 2)
                elif u == 2:
                    pe.wait_ge(T["pTb"], 2 * n + 1)
                else:
                    pe.wait_ge(T["pTa"], 2 * n + 2)
                for j in range(UH):
                    m = nc.tensor.transpose(bank[2 + (u > 0)][:, j * P:(j + 1) * P], pr[:, u % 2, j, :], ident[:])
                m.then_inc(T["pT_ps"], 1)

            def weigh(k, u, q):
                t, b = u // 2, bank[4 + u % 2]
                pe.wait_ge(T["pTb" if u % 2 else "pTa"], 2 * k + u // 2 + 1)
                pe.wait_ge(T["v"], 2 * k + 2)
                until(pe, T["o"], 4 * k + u - 1)
                apart(pe)
                for j in range(UH):
                    h = 2 * j + u % 2
                    o = b[:, j * (DH + 1):(j + 1) * (DH + 1)]
                    if t == 0:
                        nc.tensor.matmul(o[0:64], pT[0:64, u % 2, j, 0:64], vt[0:64, q, 0, h, :],
                                         start=True, stop=True)
                    else:
                        nc.tensor.matmul(o[0:64], pT[:, u % 2, j, 0:64], ve[:, q, h, :], start=True, stop=True)
                    m = nc.tensor.matmul(o[64:128], pT[:, u % 2, j, 64:128], vt[:, q, t, h, :],
                                         start=True, stop=True)
                m.then_inc(T["o_ps"], 1)

            def turn_o(k, t):
                pe.wait_ge(T["o"], 4 * k + 2 * t + 2)
                if t == 0:
                    pe.wait_ge(T["pTa"], 2 * k + 1)
                elif behind:
                    pe.wait_ge(T["qT"], 2 * n + 1)
                else:
                    pe.wait_ge(T["yn"], 2 * k + 1)
                turn(ot, t, 2, T["oT_ps"])

            def out_project(k, t):
                pe.wait_ge(T["oT"], 2 * k + t + 1)
                if t == 1:
                    if behind:
                        pe.wait_ge(T["kT"], 2 * n + 1)
                    else:
                        pe.wait_ge(T["pTb"], 2 * k + 2)
                for c in range(4):
                    m = nc.tensor.matmul(bank[2 + t][:, 0:D], oT[:, t, c, :], wo_s[:, l, c, :],
                                         start=(c == 0), stop=(c == 3))
                m.then_inc(T["w_ps"], 1)

            def turn_qk(t):
                pe.wait_ge(T["qrot"], 2 * n + t + 1)
                if t == 0 and now:
                    pe.wait_ge(T["hT"], 2 * n1 + 2)
                elif t == 0:
                    pe.wait_ge(T["yn"], 2 * n - 1)
                    pe.wait_ge(T["pTb"], 2 * n)
                elif tail:
                    pe.wait_ge(T["yn"], 2 * n)
                else:
                    pe.wait_ge(T["qT"], 2 * n + 1)
                    pe.wait_ge(T["kT"], 2 * n + 1)
                turn(qrot, t, 2, T["qT_ps"])
                pe.wait_ge(T["krot"], 2 * n + t + 1)
                turn(krot, t, 3, T["kT_ps"])

            if now:
                pe.wait_ge(T[f"h_in{p}"], 32 * half_count(n1))
                if behind:
                    until(pe, T["yn"], 2 * n - 1)
                    until(pe, T["pTb"], 2 * n)
                else:
                    until(pe, T["yn"], 2 * n1)
                for t in range(TPB):
                    nc.tensor.transpose(bank[2 + t][:, 0:P], hs[:, p, t, :], ident[:]).then_inc(T["hT_ps"], 1)
            if tail:
                weigh(n - 1, 3, p)
            if behind:
                turn_qk(0)
            if now:
                project(0)
            if tail:
                turn_o(n - 1, 1)
            if behind:
                scores(0)
            if tail:
                out_project(n - 1, 1)
            if behind:
                scores(1)
                turn_qk(1)
            if now:
                project(1)
            if behind:
                turn_p(0)
                turn_p(1)
                weigh(n, 0, 1 - p)
                scores(2)
                weigh(n, 1, 1 - p)
                turn_o(n, 0)
                scores(3)
                turn_p(2)
                out_project(n, 0)
                weigh(n, 2, 1 - p)
                turn_p(3)

        def t_steps(eng, step):
            step(0, True, False, False)
            step(1, True, True, False)
            step(2, True, True, True)
            with eng.Fori(3, B - 2, 2) as i:
                step(i, True, True, True)
                step(i + 1, True, True, True, odd=False)
            step(B - 1, True, True, True)
            step(B, False, True, True)
            step(B + 1, False, False, True)

        M = B // 2

        def f_sync(sp, l, i, odd=False, load_next=True):
            p = par_of(i, odd)
            m = l * M + i
            until(sp, G["xn"], 1 * (m - 1))
            if not isinstance(m, int):
                apart(sp)
            until(sp, G["yb"], 1 * (m - 1))
            if not isinstance(m, int):
                apart(sp)
            for k in range(2):
                b = 2 * i + k
                tt = slice(TPB * k, TPB * k + TPB)
                for c, row in ((0, 1), (1, 0)):
                    sp.dma_start(f_h[:, p, tt, 64 * c:64 * c + 64],
                                 y_d[2 * l + 1][bass.ds(b, 1), row:row + N, 64 * c:64 * c + 64].rearrange(
                                     "b (t p) d -> p (b t) d", p=P)).then_inc(G[f"in{p}"], 16)
                sp.dma_start(f_y[:, p, tt, :], y_d[2 * l + 1][bass.ds(b, 1), 1:ROWS, :].rearrange(
                    "b (t p) d -> p (b t) d", p=P)).then_inc(G[f"in{p}"], 16)
            if l == L - 1 and isinstance(i, int) and i < 2:
                f_x1_in(sp, i, odd)

        def f_x1_in(sp, i, odd):
            p = par_of(i, odd)
            for k in range(2):
                sp.dma_start(f_x1[:, p, TPB * k:TPB * k + TPB, :],
                             x1_d[bass.ds(2 * i + k, 1)].rearrange("b (t p) d -> p (b t) d", p=P)
                             ).then_inc(G[f"x1_in{p}"], 16)

        def f_in_count(l, i):
            return 96 * (M // 2 * l) + 96 * half_count(i)

        def f_store(sp, l, i, odd=False):
            p = par_of(i, odd)
            m = l * M + i
            src, ready = (f_o, "o") if l == L - 1 else (f_yn, "yn")
            until(sp, G[ready], i + 1 if l == L - 1 else m + 1)
            for k in range(2):
                tt = slice(TPB * k, TPB * k + TPB)
                if l == L - 1:
                    dst = out[bass.ds(2 * i + k, 1)]
                else:
                    dst = y_d[2 * l + 2][bass.ds(2 * i + k, 1), 1:ROWS, :]
                sp.dma_start(dst.rearrange("b (t p) d -> p (b t) d", p=P), src[:, p, tt, :]
                             ).then_inc(G[f"out{p}"], 16)
            if l == L - 1 and not (isinstance(i, int) and i + 2 >= M):
                f_x1_in(sp, i + 2, odd)

        def f_pool(pool, l, i, odd=False):
            p = par_of(i, odd)
            m = l * M + i
            inv_std(pool, f_ve[:], f_rs[:], f_mv[:, :, 1], G["mv"], m + 1, G["ve"], G["rs"])
            until(pool, G["yn"], m - 1)
            nc.gpsimd.tensor_tensor(f_yb[:, p], f_y[:, p], b2_s[:, l, :].unsqueeze(1).broadcast_to([P, FT, D]),
                                    ALU.add).then_inc(G["yb"], 1)

        def f_pool_end(pool, l, i, odd=False):
            if l == L - 1:
                p = par_of(i, odd)
                inv_std(pool, f_ve2[:], f_rs2[:], f_mv2[:, :, 1], G["mv2"], i + 1, G["ve2"], G["rs2"])
                pool.wait_ge(G["ln"], i + 1)
                pool.wait_ge(G[f"x1_in{p}"], 32 * half_count(i))
                until(pool, G[f"out{p}"], 32 * (M // 2 * l) + 32 * (half_count(i) - 1))
                nc.gpsimd.tensor_tensor(f_o[:, p], f_ln[:], f_x1[:, p], ALU.add).then_inc(G["o"], 1)

        def f_act(act, l, i, odd=False):
            m = l * M + i
            for c in range(HC):
                w = HW[c]
                act.wait_ge(G["g_ps"], HC * m + c + 1)
                until(act, G["u"], HC * m + c - 1)
                nc.scalar.activation(f_g[0:w, c % 2, :], bank[2 + c % 2][0:w, :], ACT.Gelu,
                                     bias=b1_s[0:w, l, 1, c:c + 1]).then_inc(G["g"], 1)

        def f_dve_in(dve, l, i, odd=False):
            p = par_of(i, odd)
            m = l * M + i
            dve.wait_ge(G[f"in{p}"], f_in_count(l, i))
            until(dve, G["rs"], m)
            stats(dve, f_h[:, p], f_st, f_mv, FT, G["st"], FT * (m + 1), G["mv"])
            dve.wait_ge(G["rs"], m + 1)
            until(dve, G["hT_ps"], m)
            for t in range(FT):
                j = normal(f_xn, f_h[:, p], f_mv, f_rs, t)
            j.then_inc(G["xn"], 1)

        def f_dve_turned(dve, l, i, odd=False):
            p = par_of(i, odd)
            m = l * M + i
            dve.wait_ge(G["hT_ps"], m + 1)
            until(dve, G["a_ps"], HC * (m - 1))
            nc.vector.tensor_scalar(f_hT[:, p, :], bank[0][:], lngb[:, l, 0:1], lngb[:, l, 1:2], ALU.mult, ALU.add
                                    ).then_inc(G["hT"], 1)

        def f_dve_gate(dve, l, i, odd=False):
            p = par_of(i, odd)
            m = l * M + i
            until(dve, G["w_ps"], m - 1)
            for c in range(HC):
                w = HW[c]
                dve.wait_ge(G["g"], HC * m + c + 1)
                dve.wait_ge(G["a_ps"], HC * m + c + 1)
                nc.vector.scalar_tensor_tensor(out=f_u[0:w, p, c, :], in0=bank[4 + c % 2][0:w, :],
                                               scalar=b1_s[0:w, l, 0, c:c + 1], in1=f_g[0:w, c % 2, :],
                                               op0=ALU.add, op1=ALU.mult).then_inc(G["u"], 1)

        def f_dve_out(dve, l, i, odd=False):
            p = par_of(i, odd)
            m = l * M + i
            dve.wait_ge(G["yb"], m + 1)
            dve.wait_ge(G["w_ps"], m + 1)
            if l < L - 1:
                until(dve, G[f"out{p}"], 32 * (half_count(i) - 1) + 32 * (M // 2 * l))
            elif isinstance(i, int) and i < 2:
                until(dve, G[f"out{p}"], 32 * (M // 2 * l))
            nc.vector.tensor_tensor(f_yn[:, p].rearrange("p t d -> p (t d)"), f_yb[:, p].rearrange("p t d -> p (t d)"),
                                    bank[6 + p][:], ALU.add).then_inc(G["yn"], 1)
            if l == L - 1:
                dve.wait_ge(G["yn"], m + 1)
                until(dve, G["rs2"], i)
                stats(dve, f_yn[:, p], f_st2, f_mv2, FT, G["st2"], FT * (i + 1), G["mv2"])
                dve.wait_ge(G["rs2"], i + 1)
                until(dve, G["o"], i)
                for t in range(FT):
                    j = normal(f_ln, f_yn[:, p], f_mv2, f_rs2, t)
                j.then_inc(G["ln"], 1)

        def f_pe_turn(pe, l, i, odd=False):
            m = l * M + i
            pe.wait_ge(G["xn"], m + 1)
            until(pe, G["hT"], m)
            for t in range(FT):
                j = nc.tensor.transpose(bank[0][:, t * P:(t + 1) * P], f_xn[:, t, :], ident[:])
            j.then_inc(G["hT_ps"], 1)

        def f_pe_up(pe, l, i, odd=False):
            p = par_of(i, odd)
            m = l * M + i
            pe.wait_ge(G["hT"], m + 1)
            for c in range(HC):
                w = HW[c]
                k = HC * m + c
                until(pe, G["g"], k - 1 if c else k)
                nc.tensor.matmul(bank[2 + c % 2][0:w, :], w1_s[:, l, HID + c * P:HID + c * P + w], f_hT[:, p, :],
                                 start=True, stop=True).then_inc(G["g_ps"], 1)
                until(pe, G["u"], k - 1 if c else k)
                nc.tensor.matmul(bank[4 + c % 2][0:w, :], w1_s[:, l, c * P:c * P + w], f_hT[:, p, :],
                                 start=True, stop=True).then_inc(G["a_ps"], 1)

        def f_pe_down(pe, l, i, odd=False):
            p = par_of(i, odd)
            m = l * M + i
            pe.wait_ge(G["u"], HC * (m + 1))
            until(pe, G["yn"], m - 1)
            for t in range(FT):
                for c in range(HC):
                    j = nc.tensor.matmul(bank[6 + p][:, t * P:(t + 1) * P], f_u[0:HW[c], p, c, t * P:(t + 1) * P],
                                         w2_s[0:HW[c], l, c, :], start=(c == 0), stop=(c == HC - 1))
            j.then_inc(G["w_ps"], 1)

        def f_steps(eng, load, up, turn, down, normalise=None):
            def step(i, odd):
                def part(f, d):
                    k = i + d
                    if f and not (isinstance(k, int) and not 0 <= k < M):
                        f(k, odd=odd ^ (d % 2 == 1))
                part(load, 3)
                part(up, 0)
                part(turn, 1)
                part(down, -1)
                part(normalise, 2)
            for i in range(-3, 3):
                step(i, i % 2 == 1)
            with eng.Fori(3, M - 4, 2) as i:
                step(i, True)
                step(i + 1, False)
            for i in range(M - 3, M + 1):
                step(i, i % 2 == 1)

        def phase(eng, k):
            eng.wait_ge(phase_end, k)

        @block.sync
        def _(sp):
            setup_sync(sp)
            steps(sp, lambda *a, **k: a_sync(sp, *a, **k))
            for p in range(2):
                sp.wait_ge(A[f"out{p}"], 16 * B)
            sp.wait_ge(zero_out, 16 * 2 * L)
            sp.sem_inc(phase_end, 1)
            for l in range(L):
                phase(sp, 2 * l + 1)

                t_steps(sp, lambda *a, **k: t_sync(sp, l, *a, **k))
                for p in range(2):
                    sp.wait_ge(T[f"out{p}"], 8 * B * (l + 1))
                sp.sem_inc(phase_end, 1)
                phase(sp, 2 * l + 2)

                f_steps(sp, lambda i, **k: f_sync(sp, l, i, **k), None, None, lambda i, **k: f_store(sp, l, i, **k))
                for p in range(2):
                    sp.wait_ge(G[f"out{p}"], 32 * (M // 2) * (l + 1))
                sp.sem_inc(phase_end, 1)

        @block.gpsimd
        def _(pool):
            setup_gpsimd(pool)
            setup_done(pool)
            steps(pool, lambda *a, **k: a_pool(pool, *a, **k))
            for l in range(L):
                phase(pool, 2 * l + 1)
                t_steps(pool, lambda *a, **k: t_pool(pool, l, *a, **k))
                phase(pool, 2 * l + 2)

                f_steps(pool, None, None, None, lambda i, **k: f_pool_end(pool, l, i, **k),
                        lambda i, **k: f_pool(pool, l, i, **k))

        @block.scalar
        def _(act):
            setup_done(act)
            steps(act, lambda *a, **k: a_act(act, *a, **k))
            for l in range(L):
                phase(act, 2 * l + 1)
                t_steps(act, lambda *a, **k: t_act(act, l, *a, **k))
                phase(act, 2 * l + 2)
                f_steps(act, None, lambda i, **k: f_act(act, l, i, **k), None, None)

        @block.vector
        def _(dve):
            setup_vector(dve)
            setup_done(dve)
            steps(dve, lambda *a, **k: a_dve(dve, *a, **k))
            for l in range(L):
                phase(dve, 2 * l + 1)
                t_steps(dve, lambda *a, **k: t_dve(dve, l, *a, **k))
                phase(dve, 2 * l + 2)

                f_steps(dve, None, lambda i, **k: f_dve_gate(dve, l, i, **k),
                        lambda i, **k: f_dve_turned(dve, l, i, **k), lambda i, **k: f_dve_out(dve, l, i, **k),
                        lambda i, **k: f_dve_in(dve, l, i, **k))

        @block.tensor
        def _(pe):
            setup_tensor(pe)
            setup_done(pe)
            steps(pe, lambda *a, **k: a_pe(pe, *a, **k))
            for l in range(L):
                phase(pe, 2 * l + 1)
                t_steps(pe, lambda *a, **k: t_pe(pe, l, *a, **k))
                phase(pe, 2 * l + 2)

                f_steps(pe, None, lambda i, **k: f_pe_up(pe, l, i, **k), lambda i, **k: f_pe_turn(pe, l, i, **k),
                        lambda i, **k: f_pe_down(pe, l, i, **k))


_INS = ["L0_attn_x", "L0_attn_w_qkv", "L0_attn_w_out", "L0_attn_b_out", "L0_attn_random_features", "L0_ffn_wqkv",
        "L0_ffn_q_scale", "L0_ffn_k_scale", "L0_ffn_wo", "L0_ffn_ln_g", "L0_ffn_ln_b", "L0_ffn_w1", "L0_ffn_b1",
        "L0_ffn_w2", "L0_ffn_b2"]


def kernel(**inputs):
    import numpy as _np
    import concourse.bacc as _bacc
    from concourse import mybir as _mybir
    from concourse.bass_utils import run_bass_kernel_spmd as _run

    nc = _bacc.Bacc("TRN2", target_bir_lowering=False, num_devices=1)
    arrays, args = {}, []
    for name in _INS:
        a = _np.ascontiguousarray(inputs[name])
        arrays[f"in_{name}"] = a
        args.append(nc.dram_tensor(f"in_{name}", a.shape, _mybir.dt.from_np(a.dtype), kind="ExternalInput").ap())
    shape = inputs["L0_attn_x"].shape
    args.append(nc.dram_tensor("out_0", shape, _mybir.dt.float32, kind="ExternalOutput").ap())
    build(nc, *args)
    r = _run(nc, [arrays], core_ids=[0])
    return r.results[0]["out_0"]
```

```python
from contextlib import ExitStack

import numpy as np

import concourse.bass as bass
from concourse import mybir

F32 = mybir.dt.float32
BF16 = mybir.dt.bfloat16
ALU = mybir.AluOpType
ACT = mybir.ActivationFunctionType
AX = mybir.AxisListType

P = 128
TPB = 2
ROWS = 257
HEADS_A, DIM_A, FEAT = 16, 8, 64
GH = 8
HEADS, DH, WIN = 8, 64, 64
UH = 4
EPS_LN, EPS_A = 1e-5, 1e-6
MASKED = -2.0 ** 100


def rotary_tables(tokens):
    half = np.arange(0, DH, 2, dtype=np.float32)
    inv = (1.0 / np.power(np.float32(10000.0), half / np.float32(DH))).astype(np.float32)
    t = np.arange(tokens, dtype=np.float32)
    fr = t[:, None] * inv[None, :]
    fr = np.concatenate([fr, fr], -1).astype(np.float64)
    base = (half + np.float32(0.4 * DH)) / np.float32(1.4 * DH)
    power = (t - tokens // 2) / np.float32(WIN // 2)
    sc = np.power(base[None, :].astype(np.float64), power[:, None].astype(np.float64))
    sc = np.concatenate([sc, sc], -1)
    sign = np.concatenate([-np.ones(DH // 2), np.ones(DH // 2)])[None, :]
    tabs = [np.cos(fr) * sc * 8.0, sign * np.sin(fr) * sc * 8.0, np.cos(fr) / sc, sign * np.sin(fr) / sc]
    out = np.stack(tabs).astype(np.float32)
    return np.ascontiguousarray(out.reshape(4, tokens // P, P, DH).transpose(2, 0, 1, 3).reshape(P, -1))


def window_masks():
    i = np.arange(WIN)[:, None]
    j = np.arange(WIN)[None, :]
    own = np.where(i < j, MASKED, 0.0)
    before = np.where(i > j, MASKED, 0.0)
    odd = np.concatenate([before, own], 1)
    even = np.concatenate([own, before], 1)
    first = np.concatenate([own, np.full((WIN, WIN), MASKED)], 1)
    both = [np.concatenate([first, odd], 0), np.concatenate([even, odd], 0)]
    return np.ascontiguousarray(np.stack([np.tile(m, (1, UH)) for m in both], 1).astype(np.float32).reshape(P, -1))


def norm_rows():
    neg = np.zeros((P, 2, GH * FEAT), np.float32)
    ones = np.zeros((P, 72), np.float32)
    for h in range(GH):
        for g in range(2):
            row = 64 * (1 - g) + h
            neg[row, g, h * FEAT:(h + 1) * FEAT] = -1.0
            ones[64 * g + h * DIM_A:64 * g + (h + 1) * DIM_A, row] = 1.0
    return neg.reshape(P, -1), ones


def build(nc, x, w_qkv, w_out, b_out, rf, wqkv, q_scale, k_scale, wo, ln_g, ln_b, w1, b1, w2, b2, out,
          upto=5):
    B, N, D = x.shape
    assert N == TPB * P and D == P
    L, _, QKV = wqkv.shape
    INNER = QKV // 3
    HID = w2.shape[1]
    HC = (HID + P - 1) // P
    HW = [min(P, HID - c * P) for c in range(HC)]

    tabs_np = rotary_tables(N)
    mask_np = window_masks()
    neg_np, ones_np = norm_rows()
    tabs_c = nc.inline_tensor(tabs_np, name="rotary_tables")
    mask_c = nc.inline_tensor(mask_np, name="window_masks")
    neg_c = nc.inline_tensor(neg_np, name="norm_rows")
    ones_c = nc.inline_tensor(ones_np, name="head_ones")

    with ExitStack() as ctx:
        def sb(name, shape, dt=F32):
            return ctx.enter_context(nc.sbuf_tensor(name, shape, dt))

        def sem(name):
            return ctx.enter_context(nc.semaphore(name))

        x1_d = nc.dram_tensor("x1_d", [B, N, D], F32, kind="Internal").ap()
        y_d = [nc.dram_tensor(f"y{n}_d", [B, ROWS, D], F32, kind="Internal").ap() for n in range(2 * L)]

        ident = sb("ident", [P, P])
        ident_b = sb("ident_b", [P, P], BF16)
        zrow = sb("zrow", [B, D])
        half_neg = sb("half_neg", [P, 16])
        tabs = sb("tabs", [P, 4, TPB, DH])
        masks_f = sb("masks_f", [P, TPB, UH * P])
        masks = sb("masks", [P, TPB, UH * P], BF16)
        rfa = sb("rfa", [P, 2, GH * FEAT])
        rfb = sb("rfb", [P, 2, GH * FEAT])
        rfn = sb("rfn", [P, 2, GH * FEAT])
        hones = sb("hones", [P, 72])
        wq_raw = sb("wq_raw", [P, 4, P])
        wT = sb("wT", [P, 4, P])
        bout = sb("bout", [P, D])
        wqkv_s = sb("wqkv_s", [P, L, QKV])
        wo_s = sb("wo_s", [P, L, INNER // P, D])
        w1_s = sb("w1_s", [P, L, 2 * HID])
        w2_s = sb("w2_s", [P, L, HC, D])
        scales = sb("scales", [P, 2 * L, 2, DH])
        ltab = sb("ltab", [P, L, 4, TPB, DH])
        lngb = sb("lngb", [P, L, 2])
        b1_s = sb("b1_s", [P, L, 2, HC])
        b2_s = sb("b2_s", [P, L, D])

        pairs = [ctx.enter_context(nc.psum_tensor(f"banks{2 * n}", [P, 1024], F32)) for n in range(4)]
        psA = [pairs[0][:, :], pairs[1][:, :]]
        bank = [pairs[n // 2][:, 512 * (n % 2):512 * (n % 2) + 512] for n in range(8)]

        phase_end = sem("phase_end")
        w_in = sem("w_in")
        late_in = sem("late_in")
        set_id = sem("set_id")
        zero_out = sem("zero_out")
        set_ps = sem("set_ps")
        set_done = sem("set_done")
        set_c = sem("set_c")
        passed = sem("passed")

        n_w, n_late = [0], [0]

        def load(eng, dst, src):
            eng.dma_start(dst, src).then_inc(w_in, 16)
            n_w[0] += 16

        def load_late(eng, dst, src):
            eng.dma_start(dst, src).then_inc(late_in, 16)
            n_late[0] += 16

        block = ctx.enter_context(nc.Block())

        def setup_sync(sp):
            sp.wait_ge(set_id, 1)
            for h in range(GH):
                for g in range(2):
                    r = 64 * g + h * DIM_A
                    with nc.allow_non_contiguous_dma(reason="a 64x8 matrix, once"):
                        load(sp, rfb[r:r + DIM_A, g, h * FEAT:(h + 1) * FEAT], rf.rearrange("f d -> d f"))
            load(sp, wq_raw[:, 0:3, :], w_qkv.rearrange("(c p) i -> p c i", p=P))
            load(sp, wq_raw[:, 3, :], w_out)
            load(sp, rfn[:].rearrange("p g n -> p (g n)"), neg_c.ap() if hasattr(neg_c, "ap") else neg_c)
            load(sp, hones[:, :], ones_c.ap() if hasattr(ones_c, "ap") else ones_c)
            load(sp, bout[:, :], b_out.rearrange("(a d) -> a d", a=1).broadcast_to([P, D]))

        def late_loads(sp, part):
            if part == 0:
                for n in range(2 * L):
                    sp.dma_start(y_d[n][:, 0, :], zrow[:, :]).then_inc(zero_out, 16)
                load_late(sp, tabs[:].rearrange("p a t d -> p (a t d)"), tabs_c.ap() if hasattr(tabs_c, "ap") else tabs_c)
                load_late(sp, masks_f[:].rearrange("p t d -> p (t d)"), mask_c.ap() if hasattr(mask_c, "ap") else mask_c)
                load_late(sp, wqkv_s[:], wqkv.rearrange("l p n -> p l n"))
                load_late(sp, w1_s[:], w1.rearrange("l p n -> p l n"))
                return
            l = (part - 1) // 2
            if part % 2 == 1:
                load_late(sp, wo_s[:, l], wo[l].rearrange("(c p) d -> p c d", p=P))
                for c in range(HC):
                    load_late(sp, w2_s[0:HW[c], l, c, :], w2[l, c * P:c * P + HW[c], :])
                    for g in range(2):
                        with nc.allow_non_contiguous_dma(reason="a bias, once"):
                            load_late(sp, b1_s[0:HW[c], l, g, c:c + 1],
                                      b1[l, g * HID + c * P:g * HID + c * P + HW[c]].rearrange("(p a) -> p a", a=1))
            else:
                with nc.allow_non_contiguous_dma(reason="a gain and a bias, once"):
                    load_late(sp, lngb[:, l, 0:1], ln_g[l].rearrange("(p a) -> p a", a=1))
                    load_late(sp, lngb[:, l, 1:2], ln_b[l].rearrange("(p a) -> p a", a=1))
                load_late(sp, b2_s[:, l, :], b2[l:l + 1, :].broadcast_to([P, D]))
                for s, src in enumerate((q_scale, k_scale)):
                    load_late(sp, scales[:, 2 * l + s, 0, :], src[l:l + 1, :].broadcast_to([P, DH]))
                    load_late(sp, scales[:, 2 * l + s, 1, 0:DH // 2],
                              src[l:l + 1, DH // 2:DH].broadcast_to([P, DH // 2]))
                    load_late(sp, scales[:, 2 * l + s, 1, DH // 2:DH],
                              src[l:l + 1, 0:DH // 2].broadcast_to([P, DH // 2]))

        def setup_gpsimd(pool):
            nc.gpsimd.memset(ident[:], 0.0).then_inc(set_c, 1)
            pool.wait_ge(set_c, 1)
            nc.gpsimd.affine_select(out=ident[:], in_=ident[:], compare_op=ALU.not_equal, fill=1.0, base=0,
                                    pattern=[[-1, P]], channel_multiplier=1).then_inc(set_c, 1)
            nc.gpsimd.memset(half_neg[:], -0.5).then_inc(set_c, 1)

        def setup_vector(dve):
            nc.vector.memset(zrow[:], 0.0)
            nc.vector.memset(rfb[:], 0.0).then_inc(set_id, 1)
            nc.vector.memset(kvb[:], 0.0).then_inc(set_done, 1)
            nc.vector.memset(aug[:], 0.0).then_inc(set_done, 1)
            nc.vector.memset(vaug[:], 1.0).then_inc(set_done, 1)
            nc.vector.memset(vt[:], 1.0).then_inc(set_done, 1)
            nc.vector.memset(ve[:], 1.0).then_inc(set_done, 1)
            dve.wait_ge(set_c, 2)
            nc.vector.tensor_copy(ident_b[:], ident[:]).then_inc(set_done, 1)
            dve.wait_ge(w_in, n_w[0])
            nc.vector.scalar_tensor_tensor(out=rfa[:], in0=rfb[:], scalar=FEAT ** -0.5, in1=rfn[:],
                                           op0=ALU.mult, op1=ALU.add)
            for c in range(4):
                dve.wait_ge(set_ps, c + 1)
                nc.vector.tensor_copy(wT[:, c, :], bank[c][:, 0:P]).then_inc(set_done, 1)

        N_SET = 5 + 1 + 4
        N_LATE = N_SET + 1 + 4 * L

        def setup_late(dve):
            dve.wait_ge(late_in, n_late[0])
            nc.vector.tensor_copy(masks[:], masks_f[:]).then_inc(set_done, 1)
            for l in range(L):
                for a in range(4):
                    s = scales[:, 2 * l + a // 2, a % 2, :].unsqueeze(1).broadcast_to([P, TPB, DH])
                    nc.vector.tensor_tensor(ltab[:, l, a], tabs[:, a], s, ALU.mult).then_inc(set_done, 1)

        def late_done(eng):
            eng.wait_ge(set_done, N_LATE)
            eng.wait_ge(late_in, n_late[0])

        def setup_tensor(pe):
            pe.wait_ge(set_c, 2)
            pe.wait_ge(w_in, n_w[0])
            for c in range(4):
                nc.tensor.transpose(bank[c][:, 0:P], wq_raw[:, c, :], ident[:]).then_inc(set_ps, 1)

        def setup_done(eng):
            eng.wait_ge(set_done, N_SET)
            eng.wait_ge(set_c, 3)
            eng.wait_ge(w_in, n_w[0])

        kvb = sb("kvb", [P, 2, 4, 2, 32])
        vaug = sb("vaug", [P, 2, TPB, GH, 2, 16])
        only_a = ctx.enter_context(ExitStack())

        def sa(name, shape, dt=F32):
            return only_a.enter_context(nc.sbuf_tensor(name, shape, dt))

        xa = sa("xa", [P, 2, TPB, D])
        a_st = sa("a_st", [P, TPB, 6])
        a_mv = sa("a_mv", [P, TPB, 2])
        a_ve = sa("a_ve", [P, TPB])
        a_rs = sa("a_rs", [P, TPB])
        a_xn = sa("a_xn", [P, TPB, D])
        a_xT = sa("a_xT", [P, N])
        aug = sa("aug", [P, 2, 2, 2, N])
        a_sq = sa("a_sq", [P, 2 * N])
        kf = sa("kf", [P, TPB, 2, GH * FEAT])
        qf = sa("qf", [P, GH, N])
        a_rd = sa("a_rd", [P, N])
        a_oT = sa("a_oT", [P, N])
        a_exp = sa("a_exp", [P, 1])
        a_y = sa("a_y", [P, TPB, D])
        xr = sa("xr", [P, 2, TPB, D])
        a_y2 = sa("a_y2", [P, TPB, D])
        a_rr = sa("a_rr", [P, N])
        a_kvT = sa("a_kvT", [P, N])
        a_st2, a_st3 = (sa(f"a_st{k}", [P, TPB, 6]) for k in (2, 3))
        a_mv2, a_mv3 = (sa(f"a_mv{k}", [P, TPB, 2]) for k in (2, 3))
        a_ve2, a_ve3, a_rs2, a_rs3 = (sa(k, [P, TPB]) for k in ("a_ve2", "a_ve3", "a_rs2", "a_rs3"))
        a_x1 = sa("a_x1", [P, 2, TPB, D])
        a_yo = sa("a_yo", [P, 2, TPB, D])

        A = {k: sem("A_" + k) for k in (
            "x_in0", "x_in1", "st", "mv", "ve", "rs", "xn", "xT_ps", "xT", "qk_ps", "v_ps", "sq", "v", "ss_ps",
            "ss", "nrm", "kf_ps", "kf", "qf_ps", "qf", "kv_ps", "kv", "o_ps", "rd", "o", "oT_ps", "oT", "w_ps",
            "y", "xr_in0", "xr_in1", "kvT_ps", "kvT", "rs_xn", "mv2",
             "mv3", "st2", "ve2", "rs2", "yn", "x1", "st3", "ve3", "rs3", "yo", "out0", "out1")}

        only_a.close()

        FT = 2 * TPB
        f_h = sb("f_h", [P, 2, FT, D])
        f_y = sb("f_y", [P, 2, FT, D])
        f_x1 = sb("f_x1", [P, 2, FT, D])
        f_st = sb("f_st", [P, FT, 6])
        f_mv = sb("f_mv", [P, FT, 2])
        f_ve = sb("f_ve", [P, FT])
        f_rs = sb("f_rs", [P, FT])
        f_xn = sb("f_xn", [P, FT, D])
        f_hT = sb("f_hT", [P, 2, FT * P])
        f_g = sb("f_g", [P, HC, FT * P])
        f_u = sb("f_u", [P, 2, HC, FT * P])
        f_yb = sb("f_yb", [P, 2, FT, D])
        f_yn = sb("f_yn", [P, 2, FT, D])
        f_st2 = sb("f_st2", [P, FT, 6])
        f_mv2 = sb("f_mv2", [P, FT, 2])
        f_ve2 = sb("f_ve2", [P, FT])
        f_rs2 = sb("f_rs2", [P, FT])
        f_ln = sb("f_ln", [P, FT, D])
        f_o = sb("f_o", [P, 2, FT, D])

        hs = sb("hs", [P, 2, TPB, D])
        yt = sb("yt", [P, 2, TPB, D])
        hT = sb("hT", [P, N])
        qraw = sb("qraw", [P, TPB, INNER])
        kraw = sb("kraw", [P, TPB, INNER])
        sq = sb("sq", [P, 2 * INNER])
        ss = sb("ss", [P, 2, TPB, 2 * HEADS])
        rr = sb("rr", [P, 2, TPB, 2 * HEADS])
        kn = sb("kn", [P, INNER])
        m1k = sb("m1k", [P, INNER])
        m2k = sb("m2k", [P, INNER])
        m1q = sb("m1q", [P, INNER])
        m2q = sb("m2q", [P, INNER])
        qrot = sb("qrot", [P, TPB, INNER])
        krot = sb("krot", [P, TPB, INNER])
        qT = sb("qT", [P, TPB, 4, P])
        kT = sb("kT", [P, 4, TPB, P])
        vt = sb("vt", [P, 2, TPB, HEADS, DH + 1])
        ve = sb("ve", [P, 2, HEADS, DH + 1])
        mx = sb("mx", [P, 2, UH])
        nb = sb("nb", [P, 2, UH])
        pr = sb("pr", [P, 2, UH, P])
        pT = sb("pT", [P, 2, UH, P])
        rl = sb("rl", [P, 2, UH])
        ot = sb("ot", [P, TPB, INNER])
        oT = sb("oT", [P, TPB, 4, P])
        yn = sb("yn", [P, 2, TPB, D])

        T = {k: sem("T_" + k) for k in (
            "h_in0", "h_in1", "y_in0", "y_in1", "hT_ps", "hT", "q_ps", "k_ps", "v_ps", "q", "k", "v", "ss", "rr",
            "kn", "km", "krot", "qm", "qrot", "qT_ps", "qT", "kT_ps", "kT", "s_ps", "mx", "nb", "p", "pT_ps", "pTa",
            "pTb", "o_ps", "rl", "o", "oT_ps", "oT", "w_ps", "yn", "out0", "out1", "ssm")}

        G = {k: sem("F_" + k) for k in (
            "in0", "in1", "x1_in0", "x1_in1", "st", "mv", "ve", "rs", "xn", "hT_ps",
            "hT", "g_ps", "a_ps", "g", "u", "yb", "w_ps", "yn",
            "st2", "mv2", "ve2", "rs2", "ln", "o", "out0", "out1")}

        def until(eng, s, v):
            if isinstance(v, int) and v <= 0:
                return
            eng.wait_ge(s, v)

        def apart(eng):
            eng.sem_inc(passed, 1)

        def inv_std(pool, ve, rs, mv, stats_ready, v, ve_sem, rs_sem):
            until(pool, stats_ready, v)
            apart(pool)
            nc.gpsimd.tensor_scalar(ve, mv, EPS_LN, None, ALU.add).then_inc(ve_sem, 1)
            pool.wait_ge(ve_sem, v)
            nc.gpsimd.tensor_tensor(rs, ve, half_neg[:, 0:ve.shape[-1]], ALU.pow).then_inc(rs_sem, 1)

        def stats(dve, src, st, mv, tiles, st_sem, v, mv_sem):
            for t in range(tiles):
                nc.vector.bn_stats(st[:, t, :], src[:, t, :]).then_inc(st_sem, 1)
            dve.wait_ge(st_sem, v)
            apart(dve)
            for t in range(tiles):
                i = nc.vector.bn_aggr(mv[:, t, :], st[:, t, :])
            i.then_inc(mv_sem, 1)

        def normal(dst, src, mv, rs, t):
            return nc.vector.tensor_scalar(dst[:, t, :], src[:, t, :], mv[:, t, 0:1], rs[:, t:t + 1],
                                           ALU.subtract, ALU.mult)

        def steps(eng, step, between=None):
            step(-1, True, False, False, False)
            step(0, True, True, False, False)
            if between:
                between(0)
            step(1, True, True, True, False)
            if between:
                between(1)
            step(2, True, True, True, True)
            if between:
                between(2)
            with eng.Fori(3, B - 2, 2) as i:
                step(i, True, True, True, True)
                step(i + 1, True, True, True, True, odd=False)
            step(B - 1, False, True, True, True)
            if between:
                between(3)
            step(B, False, False, True, True)
            if between:
                between(4)
            step(B + 1, False, False, False, True)

        def par_of(i, odd):
            return i % 2 if isinstance(i, int) else int(odd)

        def a_sync(sp, i, ahead, now, behind, tail, odd=True):
            p = par_of(i, odd)
            if ahead:
                until(sp, A["xn"], i)
                sp.dma_start(xa[:, 1 - p], x[bass.ds(i + 1, 1)].rearrange("b (t p) d -> p (b t) d", p=P)
                             ).then_inc(A[f"x_in{1 - p}"], 16)
            if behind:
                n = i - 1
                until(sp, A["x1"], n - 1)
                sp.dma_start(xr[:, 1 - p], x[bass.ds(n, 1)].rearrange("b (t p) d -> p (b t) d", p=P)
                             ).then_inc(A[f"xr_in{1 - p}"], 16)
            if tail:
                n = i - 2
                sp.wait_ge(A["x1"], n + 1)
                sp.dma_start(x1_d[bass.ds(n, 1)].rearrange("b (t p) d -> p (b t) d", p=P), a_x1[:, p]
                             ).then_inc(A[f"out{p}"], 16)
                sp.wait_ge(A["yo"], n + 1)
                sp.dma_start(y_d[0][bass.ds(n, 1), 1:ROWS, :].rearrange("b (t p) d -> p (b t) d", p=P), a_yo[:, p]
                             ).then_inc(A[f"out{p}"], 16)

        def a_pool(pool, i, ahead, now, behind, tail, odd=True):
            p = par_of(i, odd)
            n = i - 2
            if tail:
                inv_std(pool, a_ve2[:], a_rs2[:], a_mv2[:, :, 1], A["mv2"], n + 1, A["ve2"], A["rs2"])
            if ahead:
                inv_std(pool, a_ve[:], a_rs[:], a_mv[:, :, 1], A["mv"], i + 2, A["ve"], A["rs"])
            if tail:
                pool.wait_ge(A["yn"], n + 1)
                pool.wait_ge(A[f"xr_in{p}"], 16 * half_count(n))
                until(pool, A[f"out{p}"], 32 * (half_count(n) - 1))
                nc.gpsimd.tensor_tensor(a_x1[:, p], a_y2[:], xr[:, p], ALU.add).then_inc(A["x1"], 1)
                inv_std(pool, a_ve3[:], a_rs3[:], a_mv3[:, :, 1], A["mv3"], n + 1, A["ve3"], A["rs3"])

        def a_act(act, i, ahead, now, behind, tail, odd=True):
            p = par_of(i, odd)
            n = i - 1
            if behind:
                until(act, A["kv_ps"], n)
                for t in range(TPB):
                    act.wait_ge(A["kf_ps"], 2 * n + t + 1)
                    nc.scalar.activation(kf[:, t].rearrange("p g n -> p (g n)"), psA[t], ACT.Exp
                                         ).then_inc(A["kf"], 1)
            if now:
                act.wait_ge(A["xT_ps"], i + 1)
                nc.scalar.copy(a_xT[:], bank[6][:, 0:N]).then_inc(A["xT"], 1)
            if behind:
                until(act, A["o_ps"], n)
                act.wait_ge(A["qf_ps"], 2 * n + 1)
                nc.scalar.activation(qf[:, 0:4].rearrange("p j n -> p (j n)"), psA[0], ACT.Exp).then_inc(A["qf"], 1)
            if now:
                act.wait_ge(A["qk_ps"], i + 1)
                nc.scalar.activation(a_sq[:], bank[4][:], ACT.Square)
                until(act, A["qf_ps"], 2 * (i - 1))
                nc.scalar.copy(aug[0:64, p, 0].rearrange("p a n -> p (a n)"), bank[4][0:64, :])
                nc.scalar.copy(aug[64:128, p, 1].rearrange("p a n -> p (a n)"), bank[4][64:128, :]
                               ).then_inc(A["sq"], 1)
            if behind:
                act.wait_ge(A["qf_ps"], 2 * n + 2)
                nc.scalar.activation(qf[:, 4:8].rearrange("p j n -> p (j n)"), psA[1], ACT.Exp).then_inc(A["qf"], 1)
            if now:
                act.wait_ge(A["v_ps"], i + 1)
                until(act, A["kv_ps"], i - 1)
                for t in range(TPB):
                    e = nc.scalar.copy(vaug[:, p, t, :, 0, :],
                                       bank[6][:, N + t * P:N + (t + 1) * P].rearrange("p (j e) -> p j e", e=16))
                e.then_inc(A["v"], 1)
                act.wait_ge(A["ss_ps"], i + 1)
                nc.scalar.activation(aug[64:72, p, 0].rearrange("p a n -> p (a n)"), bank[5][64:72, :], ACT.Sqrt)
                nc.scalar.activation(aug[0:8, p, 1].rearrange("p a n -> p (a n)"), bank[5][0:8, :], ACT.Sqrt
                                     ).then_inc(A["nrm"], 1)
                nc.scalar.activation(a_exp[:], half_neg[:, 0:1], ACT.Exp)

        def a_pe(pe, i, ahead, now, behind, tail, odd=True):
            p = par_of(i, odd)
            n = i - 1
            if behind:
                pe.wait_ge(A["nrm"], n + 1)
                for t in range(TPB):
                    until(pe, A["qf"], 2 * n - 1 + t)
                    for g in range(2):
                        m = nc.tensor.matmul(bank[2 * t + g][:], aug[:, 1 - p, g, 1, t * P:(t + 1) * P], rfa[:, g, :],
                                             start=True, stop=True)
                    m.then_inc(A["kf_ps"], 1)
            if now:
                pe.wait_ge(A["rs_xn"], i + 1)
                until(pe, A["v"], i)
                for t in range(TPB):
                    m = nc.tensor.transpose(bank[6][:, t * P:(t + 1) * P], a_xn[:, t, :], ident[:])
                m.then_inc(A["xT_ps"], 1)
            if tail:
                pe.wait_ge(A["o"], n)
                for t in range(TPB):
                    m = nc.tensor.matmul(bank[7][:, t * P:(t + 1) * P], a_oT[:, t * P:(t + 1) * P],
                                         wT[:, 3, :], start=True, stop=True)
                m.then_inc(A["w_ps"], 1)

            def q_features(g):
                pe.wait_ge(A["kf"], 2 * n + 1 + g)
                for j in range(4):
                    m = nc.tensor.matmul(bank[2 * g + j // 2][:, (j % 2) * N:(j % 2 + 1) * N],
                                         rfa[:, g, j * P:(j + 1) * P], aug[:, 1 - p, g, 0, :], start=True, stop=True)
                m.then_inc(A["qf_ps"], 1)

            if behind:
                q_features(0)
                pe.wait_ge(A["kf"], 2 * n + 2)
                pe.wait_ge(A["v"], n + 1)
                for r in range(2):
                    for t in range(TPB):
                        for c in range(4):
                            j = 2 * c + r
                            m = nc.tensor.matmul(bank[5][32 * c:32 * c + 32, r * P:(r + 1) * P],
                                                 vaug[:, 1 - p, t, j].rearrange("p a e -> p (a e)"),
                                                 kf[:, t, j // 4, (j % 4) * P:(j % 4 + 1) * P],
                                                 start=(t == 0), stop=(t == TPB - 1))
                m.then_inc(A["kvT_ps"], 1)
            if now:
                pe.wait_ge(A["xT"], i + 1)
                until(pe, A["sq"], i)
                until(pe, A["kv"], i - 1)
                for c in range(2):
                    m = nc.tensor.matmul(bank[4][:, c * N:(c + 1) * N], wT[:, c, :], a_xT[:], start=True, stop=True)
                m.then_inc(A["qk_ps"], 1)
            if behind:
                q_features(1)
            if now:
                for t in range(TPB):
                    m = nc.tensor.matmul(bank[6][:, N + t * P:N + (t + 1) * P], a_xT[:, t * P:(t + 1) * P],
                                         wT[:, 2, :], start=True, stop=True)
                m.then_inc(A["v_ps"], 1)
                pe.wait_ge(A["sq"], i + 1)
            if behind:
                pe.wait_ge(A["kvT"], n + 1)
                until(pe, A["kv"], n)
                for r in range(2):
                    m = nc.tensor.transpose(bank[4][:, r * P:(r + 1) * P], a_kvT[:, r * P:(r + 1) * P], ident[:])
                m.then_inc(A["kv_ps"], 1)
            if now:
                until(pe, A["nrm"], i)
                nc.tensor.matmul(bank[5][0:72, :], hones[:], a_sq[:], start=True, stop=True).then_inc(A["ss_ps"], 1)
            if behind:
                pe.wait_ge(A["qf"], 2 * n + 2)
                if tail:
                    pe.wait_ge(A["y"], n)
                pe.wait_ge(A["kv"], n + 1)
                for a in range(2):
                    for r in range(2):
                        for c in range(4):
                            m = nc.tensor.matmul(bank[7][32 * c:32 * c + 32, a * N:(a + 1) * N], kvb[:, a, c, r, :],
                                                 qf[:, 2 * c + r, :], start=(r == 0), stop=(r == 1))
                m.then_inc(A["o_ps"], 1)

        def a_dve(dve, i, ahead, now, behind, tail, odd=True):
            p = par_of(i, odd)
            n = i - 1
            k = i - 2
            if tail:
                dve.wait_ge(A["w_ps"], k + 1)
                nc.vector.tensor_tensor(a_y[:], bank[7][:, 0:N].rearrange("p (t d) -> p t d", d=D),
                                        bout[:].unsqueeze(1).broadcast_to([P, TPB, D]), ALU.add).then_inc(A["y"], 1)
                dve.wait_ge(A["y"], k + 1)
                stats(dve, a_y, a_st2, a_mv2, TPB, A["st2"], 2 * (k + 1), A["mv2"])
            if ahead:
                dve.wait_ge(A[f"x_in{1 - p}"], 16 * half_count(i + 1))
                until(dve, A["rs"], i + 1)
                stats(dve, xa[:, 1 - p], a_st, a_mv, TPB, A["st"], 2 * (i + 2), A["mv"])
            if behind:
                dve.wait_ge(A["kvT_ps"], n + 1)
                until(dve, A["kv_ps"], n)
                nc.vector.tensor_copy(a_kvT[:], bank[5][:, 0:N]).then_inc(A["kvT"], 1)
            if tail:
                dve.wait_ge(A["rs2"], k + 1)
                until(dve, A["x1"], k)
                for t in range(TPB):
                    j = normal(a_y2, a_y, a_mv2, a_rs2, t)
                j.then_inc(A["yn"], 1)
            if ahead:
                dve.wait_ge(A["rs"], i + 2)
                until(dve, A["xT_ps"], i + 1)
                for t in range(TPB):
                    j = normal(a_xn, xa[:, 1 - p], a_mv, a_rs, t)
                    if t == TPB - 1:
                        j.then_inc(A["rs_xn"], 1)
                dve.wait_ge(A["rs_xn"], i + 2)
                dve.sem_inc(A["xn"], 1)
            if tail:
                dve.wait_ge(A["x1"], k + 1)
                stats(dve, a_x1[:, p], a_st3, a_mv3, TPB, A["st3"], 2 * (k + 1), A["mv3"])
            if behind:
                dve.wait_ge(A["kv_ps"], n + 1)
                until(dve, A["o_ps"], n)
                kv = bank[4][:, 0:32 * GH].rearrange("p (r c a h e) -> p c r a h e", c=4, r=2, a=2, h=2)
                for h in range(2):
                    for r in range(2):
                        j = nc.vector.tensor_copy(
                            kvb[64 * h:64 * h + 64, :, :, r, 16 * r + 8 * h:16 * r + 8 * h + 8],
                            kv[64 * h:64 * h + 64, :, r, :, h, :].rearrange("p c a e -> p a c e"))
                j.then_inc(A["kv"], 1)
            if tail:
                dve.wait_ge(A["rs3"], k + 1)
                until(dve, A[f"out{p}"], 32 * (half_count(k) - 1))
                for t in range(TPB):
                    j = normal(a_yo[:, p], a_x1[:, p], a_mv3, a_rs3, t)
                j.then_inc(A["yo"], 1)
            if behind:
                dve.wait_ge(A["o_ps"], n + 1)
                nc.vector.tensor_scalar(a_rd[:], bank[7][:, N:2 * N], EPS_A, None, ALU.add).then_inc(A["rd"], 1)
                dve.wait_ge(A["rd"], 2 * n + 1)
                nc.vector.reciprocal(a_rr[:], a_rd[:]).then_inc(A["rd"], 1)
                dve.wait_ge(A["rd"], 2 * n + 2)
                until(dve, A["w_ps"], n)
                nc.vector.tensor_tensor(a_oT[:], bank[7][:, 0:N], a_rr[:], ALU.mult).then_inc(A["o"], 1)

        def half_count(n):
            return n // 2 + 1

        MASK_FIRST = True

        def t_sync(sp, l, i, now, behind, tail, odd=True):
            p = par_of(i, odd)
            if now:
                n = l * B + i
                until(sp, T["hT_ps"], n - 1)
                for c, row in ((0, 1), (1, 0)):
                    sp.dma_start(hs[:, p, :, 64 * c:64 * c + 64],
                                 y_d[2 * l][bass.ds(i, 1), row:row + N, 64 * c:64 * c + 64].rearrange(
                                     "b (t p) d -> p (b t) d", p=P)).then_inc(T[f"h_in{p}"], 16)
            if behind:
                b = i - 1
                n = l * B + b
                until(sp, T["yn"], 2 * (n - 1))
                sp.dma_start(yt[:, 1 - p], y_d[2 * l][bass.ds(b, 1), 1:ROWS, :].rearrange(
                    "b (t p) d -> p (b t) d", p=P)).then_inc(T[f"y_in{1 - p}"], 16)
            if tail:
                b = i - 2
                n = l * B + b
                sp.wait_ge(T["yn"], 2 * (n + 1))
                sp.dma_start(y_d[2 * l + 1][bass.ds(b, 1), 1:ROWS, :].rearrange("b (t p) d -> p (b t) d", p=P),
                             yn[:, p]).then_inc(T[f"out{p}"], 16)

        def t_pool(pool, l, i, now, behind, tail, odd=True):
            p = par_of(i, odd)
            if now:
                n = l * B + i
                for t in range(TPB):
                    pool.wait_ge(T["ss"], 2 * n + t + 1)
                    apart(pool)
                    nc.gpsimd.tensor_scalar(ss[:, p, t, :], ss[:, p, t, :], 1e-24, None, ALU.max
                                            ).then_inc(T["ssm"], 1)
                    pool.wait_ge(T["ssm"], 2 * n + t + 1)
                    until(pool, T["p"], 4 * (n - 1))
                    nc.gpsimd.tensor_tensor(rr[:, p, t, :], ss[:, p, t, :], half_neg[:], ALU.pow
                                            ).then_inc(T["rr"], 1)
                    pool.wait_ge(T["q"], 2 * n + t + 1)
                    rotary(nc.gpsimd, pool, qraw[:, t, :], m1q, m2q, qrot[:, t, :], l, 0, t, T["qm"],
                           2 * (2 * n + t + 1), T["qT_ps"], 2 * (n - 1) + t + 1 if not isinstance(n, int) or n else 0,
                           T["qrot"])

        def rotary(on, eng, src, m1, m2, dst, l, a, t, m_sem, m_count, read_sem, read_count, done):
            s3 = src.rearrange("p (h d) -> p h d", d=DH)
            s4 = src.rearrange("p (h c d) -> p h c d", c=2, d=DH // 2)
            d4 = m2[:].rearrange("p (h c d) -> p h c d", c=2, d=DH // 2)
            cos = ltab[:, l, a, t, :].unsqueeze(1).broadcast_to([P, HEADS, DH])
            on.tensor_tensor(m1[:].rearrange("p (h d) -> p h d", d=DH), s3, cos, ALU.mult)
            for c in range(2):
                sin = ltab[:, l, a + 1, t, 32 * c:32 * c + 32].unsqueeze(1).broadcast_to([P, HEADS, DH // 2])
                on.tensor_tensor(d4[:, :, c, :], s4[:, :, 1 - c, :], sin, ALU.mult).then_inc(m_sem, 1)
            eng.wait_ge(m_sem, m_count)
            until(eng, read_sem, read_count)
            on.tensor_tensor(dst, m1[:], m2[:], ALU.add).then_inc(done, 1)

        def t_act(act, l, i, now, behind, tail, odd=True):
            p = par_of(i, odd)
            n1 = l * B + i
            n = n1 - 1

            def exps(u):
                act.wait_ge(T["nb"], 4 * n + u + 1)
                until(act, T["pT_ps"], 4 * n + u - 1)
                for j in range(UH):
                    h = 2 * j + u % 2
                    e = nc.scalar.activation(pr[:, u % 2, j, :], bank[u % 2][:, j * P:(j + 1) * P], ACT.Exp,
                                             bias=nb[:, u % 2, j:j + 1], scale=rr[:, 1 - p, u // 2, h:h + 1])
                e.then_inc(T["p"], 1)

            def q_in(t):
                act.wait_ge(T["q_ps"], 2 * n1 + t + 1)
                until(act, T["qrot"], 2 * (n1 - 1) + t + 1 if not isinstance(n1, int) or n1 else 0)
                nc.scalar.copy(qraw[:, t, :], bank[6 + t][:])
                until(act, T["ss"], 2 * n1 + t)
                nc.scalar.activation(sq[:, 0:INNER], bank[6 + t][:], ACT.Square).then_inc(T["q"], 1)

            def k_in(t):
                act.wait_ge(T["k_ps"], 2 * n1 + t + 1)
                until(act, T["kn"], 2 * (n1 - 1) + t + 1 if not isinstance(n1, int) or n1 else 0)
                nc.scalar.copy(kraw[:, t, :], bank[7 - t][:])
                nc.scalar.activation(sq[:, INNER:], bank[7 - t][:], ACT.Square).then_inc(T["k"], 1)

            def v_in(t):
                act.wait_ge(T["v_ps"], 2 * n1 + t + 1)
                until(act, T["o_ps"], 4 * (n1 - 1))
                v = bank[6 + t][:].rearrange("p (h d) -> p h d", d=DH)
                nc.scalar.copy(vt[:, p, t, :, 0:DH], v)
                r = 64 * (1 - t)
                nc.scalar.copy(ve[r:r + 64, p, :, 0:DH], v[r:r + 64]).then_inc(T["v"], 1)

            def turned_q(t):
                act.wait_ge(T["qT_ps"], 2 * n + t + 1)
                nc.scalar.copy(qT[:, t].rearrange("p j n -> p (j n)"), bank[3][:]).then_inc(T["qT"], 1)

            def turned_p(k, u):
                act.wait_ge(T["pT_ps"], 4 * k + u + 1)
                until(act, T["o_ps"], 4 * k + u - 1)
                nc.scalar.copy(pT[:, 1].rearrange("p j n -> p (j n)"), bank[2 + u // 2][:]).then_inc(T["pTb"], 1)

            def turned_o(k, t):
                act.wait_ge(T["oT_ps"], 2 * k + t + 1)
                nc.scalar.copy(oT[:, t].rearrange("p j n -> p (j n)"), bank[3][:]).then_inc(T["oT"], 1)

            if now:
                act.wait_ge(T["hT_ps"], n1 + 1)
                until(act, T["v_ps"], 2 * n1)
                nc.scalar.copy(hT[:], bank[2][:, 0:N]).then_inc(T["hT"], 1)
            if tail:
                turned_p(n - 1, 3)
            if now:
                q_in(0)
            if behind:
                turned_q(0)
            if now:
                k_in(0)
            if tail:
                turned_o(n - 1, 1)
            if now:
                v_in(0)
            if behind:
                exps(0)
                turned_q(1)
            if now:
                q_in(1)
            if behind:
                exps(1)
            if now:
                k_in(1)
            if behind:
                turned_p(n, 1)
            if now:
                v_in(1)
            if behind:
                exps(2)
                turned_o(n, 0)
                exps(3)

        def t_dve(dve, l, i, now, behind, tail, odd=True):
            p = par_of(i, odd)
            n1 = l * B + i
            n = n1 - 1

            def peak(u):
                dve.wait_ge(T["s_ps"], 4 * n + u + 1)
                nc.vector.tensor_reduce(mx[:, u % 2, :], bank[u % 2][:].rearrange("p (j k) -> p j k", k=P), AX.X,
                                        ALU.max).then_inc(T["mx"], 1)
                dve.wait_ge(T["mx"], 4 * n + u + 1)
                until(dve, T["p"], 4 * n + u - 1)
                nc.vector.scalar_tensor_tensor(out=nb[:, u % 2, :], in0=mx[:, u % 2, :], scalar=-1.0,
                                               in1=rr[:, 1 - p, u // 2, u % 2:HEADS:2], op0=ALU.mult, op1=ALU.mult
                                               ).then_inc(T["nb"], 1)

            def turned(u):
                dve.wait_ge(T["pT_ps"], 4 * n + u + 1)
                until(dve, T["o_ps"], 4 * n + u - 1)
                nc.vector.tensor_copy(pT[:, 0].rearrange("p j n -> p (j n)"), bank[3 - u // 2][:]
                                      ).then_inc(T["pTa"], 1)

            def divide(k, u):
                o = bank[4 + u % 2][:, 0:UH * (DH + 1)].rearrange("p (j d) -> p j d", d=DH + 1)
                dve.wait_ge(T["o_ps"], 4 * k + u + 1)
                nc.vector.reciprocal(rl[:, u % 2, :], o[:, :, DH]).then_inc(T["rl"], 1)
                dve.wait_ge(T["rl"], 4 * k + u + 1)
                until(dve, T["oT_ps"], 2 * (k - 1) + u // 2 + 1)
                nc.vector.tensor_tensor(ot[:, u // 2].rearrange("p (j c d) -> p j c d", c=2, d=DH)[:, :, u % 2, :],
                                        o[:, :, 0:DH], rl[:, u % 2, :].unsqueeze(2).broadcast_to([P, UH, DH]),
                                        ALU.mult).then_inc(T["o"], 1)

            def squares(t):
                dve.wait_ge(T["k"], 2 * n1 + t + 1)
                nc.vector.tensor_reduce(ss[:, p, t, :], sq[:].rearrange("p (h d) -> p h d", d=DH), AX.X, ALU.add
                                        ).then_inc(T["ss"], 1)

            def keys(k, t, q):
                dve.wait_ge(T["rr"], 2 * k + t + 1)
                until(dve, T["krot"], 2 * k + t)
                nc.vector.tensor_tensor(kn[:].rearrange("p (h d) -> p h d", d=DH),
                                        kraw[:, t, :].rearrange("p (h d) -> p h d", d=DH),
                                        rr[:, q, t, HEADS:].unsqueeze(2).broadcast_to([P, HEADS, DH]), ALU.mult
                                        ).then_inc(T["kn"], 1)
                dve.wait_ge(T["kn"], 2 * k + t + 1)
                rotary(nc.vector, dve, kn[:], m1k, m2k, krot[:, t, :], l, 2, t, T["km"], 2 * (2 * k + t + 1),
                       T["kT_ps"], 2 * (k - 1) + t + 1 if not isinstance(k, int) or k else 0, T["krot"])

            def residual(k, t, q):
                if t == 0:
                    dve.wait_ge(T[f"y_in{q}"], 16 * half_count(k))
                    until(dve, T[f"out{q}"], 16 * (half_count(k) - 1))
                dve.wait_ge(T["w_ps"], 2 * k + t + 1)
                nc.vector.tensor_tensor(yn[:, q, t, :], yt[:, q, t, :], bank[3 - t][:, 0:D], ALU.add
                                        ).then_inc(T["yn"], 1)

            def turned_k(t):
                dve.wait_ge(T["kT_ps"], 2 * n + t + 1)
                nc.vector.tensor_copy(kT[:, :, 1 - t, :], bank[2][:].rearrange("p (j n) -> p j n", n=P)
                                      ).then_inc(T["kT"], 1)

            if tail:
                divide(n - 1, 2)
                divide(n - 1, 3)
            if behind:
                turned_k(0)
                keys(n, 1, 1 - p)
                peak(0)
            if tail:
                residual(n - 1, 1, p)
            if behind:
                peak(1)
            if now:
                squares(0)
            if behind:
                turned_k(1)
                turned(0)
            if now:
                squares(1)
            if behind:
                divide(n, 0)
                peak(2)
                divide(n, 1)
                peak(3)
                turned(2)
                residual(n, 0, 1 - p)
            if now:
                keys(n1, 0, p)

        def t_pe(pe, l, i, now, behind, tail, odd=True):
            p = par_of(i, odd)
            n1 = l * B + i
            n = n1 - 1

            def turn(src, t, b, into):
                for j in range(4):
                    m = nc.tensor.transpose(bank[b][:, j * P:(j + 1) * P], src[:, t, j * P:(j + 1) * P], ident[:])
                m.then_inc(into, 1)

            def project_q(t):
                pe.wait_ge(T["hT"], n1 + 1)
                if t == 0:
                    until(pe, T["k"], 2 * n1)
                else:
                    pe.wait_ge(T["k"], 2 * n1 + 1)
                nc.tensor.matmul(bank[6 + t][:], hT[:, t * P:(t + 1) * P], wqkv_s[:, l, 0:INNER],
                                 start=True, stop=True).then_inc(T["q_ps"], 1)

            def project_kv(t):
                until(pe, T["v"], 2 * n1 + t)
                nc.tensor.matmul(bank[7 - t][:], hT[:, t * P:(t + 1) * P], wqkv_s[:, l, INNER:2 * INNER],
                                 start=True, stop=True).then_inc(T["k_ps"], 1)
                pe.wait_ge(T["q"], 2 * n1 + t + 1)
                nc.tensor.matmul(bank[6 + t][:], hT[:, t * P:(t + 1) * P], wqkv_s[:, l, 2 * INNER:],
                                 start=True, stop=True).then_inc(T["v_ps"], 1)

            def scores(u):
                t, b = u // 2, bank[u % 2]
                pe.wait_ge(T["qT"], 2 * n + t + 1)
                pe.wait_ge(T["kT"], 2 * n + t + 1)
                until(pe, T["p"], 4 * n + u - 1)
                nc.tensor.matmul(b[:], ident_b[:], masks[:, t, :], start=True, stop=False, skip_group_check=True)
                for j in range(UH):
                    r, c = 64 * (u % 2), j
                    own = kT[r:r + 64, c, 1 - t, :]
                    for w in range(2):
                        q = qT[r:r + 64, t, c, 64 * w:64 * w + 64]
                        o = b[64 * w:64 * w + 64, j * P:(j + 1) * P]
                        if w == 1:
                            m = nc.tensor.matmul(o, q, own, start=False, stop=True, skip_group_check=True)
                        elif t == 0:
                            nc.tensor.matmul(o[:, 0:64], q, own[:, 0:64], start=False, stop=True,
                                             skip_group_check=True)
                        else:
                            both = kT[r:r + 64, c, :, :].rearrange("p t (w k) -> p (t w) k", k=64)[:, 0:4:3, :]
                            nc.tensor.matmul(o, q, both, start=False, stop=True, skip_group_check=True)
                m.then_inc(T["s_ps"], 1)

            def turn_p(k, u):
                pe.wait_ge(T["p"], 4 * k + u + 1)
                if u == 0:
                    pe.wait_ge(T["qT"], 2 * k + 2)
                elif u == 1:
                    pe.wait_ge(T["kT"], 2 * k + 2)
                elif u == 2:
                    pe.wait_ge(T["pTb"], 2 * k + 1)
                else:
                    pe.wait_ge(T["yn"], 2 * k + 1)
                b = bank[(3, 2, 2, 3)[u]]
                for j in range(UH):
                    m = nc.tensor.transpose(b[:, j * P:(j + 1) * P], pr[:, u % 2, j, :], ident[:])
                m.then_inc(T["pT_ps"], 1)

            def weigh(k, u, q):
                t, b = u // 2, bank[4 + u % 2]
                pe.wait_ge(T["pTb" if u % 2 else "pTa"], 2 * k + u // 2 + 1)
                pe.wait_ge(T["v"], 2 * k + 2)
                until(pe, T["o"], 4 * k + u - 1)
                apart(pe)
                for j in range(UH):
                    h = 2 * j + u % 2
                    o = b[:, j * (DH + 1):(j + 1) * (DH + 1)]
                    if t == 0:
                        nc.tensor.matmul(o[0:64], pT[0:64, u % 2, j, 0:64], vt[0:64, q, 0, h, :],
                                         start=True, stop=True)
                    else:
                        nc.tensor.matmul(o[0:64], pT[:, u % 2, j, 0:64], ve[:, q, h, :], start=True, stop=True)
                    m = nc.tensor.matmul(o[64:128], pT[:, u % 2, j, 64:128], vt[:, q, t, h, :],
                                         start=True, stop=True)
                m.then_inc(T["o_ps"], 1)

            def turn_o(k, t):
                pe.wait_ge(T["o"], 4 * k + 2 * t + 2)
                if t == 0:
                    pe.wait_ge(T["pTa"], 2 * k + 1)
                elif behind:
                    pe.wait_ge(T["qT"], 2 * n + 1)
                else:
                    pe.wait_ge(T["pTb"], 2 * k + 2)
                turn(ot, t, 3, T["oT_ps"])

            def out_project(k, t):
                pe.wait_ge(T["oT"], 2 * k + t + 1)
                if t == 1:
                    if behind:
                        pe.wait_ge(T["kT"], 2 * n + 1)
                    else:
                        pe.wait_ge(T["pTa"], 2 * k + 2)
                for c in range(4):
                    m = nc.tensor.matmul(bank[3 - t][:, 0:D], oT[:, t, c, :], wo_s[:, l, c, :],
                                         start=(c == 0), stop=(c == 3))
                m.then_inc(T["w_ps"], 1)

            def turn_qk(t):
                pe.wait_ge(T["qrot"], 2 * n + t + 1)
                if t == 0:
                    until(pe, T["pTb"], 2 * n)
                elif tail:
                    pe.wait_ge(T["oT"], 2 * n)
                else:
                    pe.wait_ge(T["qT"], 2 * n + 1)
                turn(qrot, t, 3, T["qT_ps"])
                pe.wait_ge(T["krot"], 2 * n + t + 1)
                if t == 0 and now:
                    pe.wait_ge(T["hT"], n1 + 1)
                elif t == 0:
                    pe.wait_ge(T["pTa"], 2 * n)
                elif tail:
                    pe.wait_ge(T["yn"], 2 * n)
                else:
                    pe.wait_ge(T["kT"], 2 * n + 1)
                turn(krot, t, 2, T["kT_ps"])

            if now:
                pe.wait_ge(T[f"h_in{p}"], 32 * half_count(n1))
                if behind:
                    until(pe, T["pTa"], 2 * n)
                else:
                    until(pe, T["yn"], 2 * n1)
                for t in range(TPB):
                    m = nc.tensor.transpose(bank[2][:, t * P:(t + 1) * P], hs[:, p, t, :], ident[:])
                m.then_inc(T["hT_ps"], 1)
            if tail:
                weigh(n - 1, 2, p)
                turn_p(n - 1, 3)
            if now:
                project_q(0)
            if tail:
                weigh(n - 1, 3, p)
            if behind:
                turn_qk(0)
            if now:
                project_kv(0)
            if tail:
                turn_o(n - 1, 1)
            if behind:
                scores(0)
                scores(1)
            if tail:
                out_project(n - 1, 1)
            if behind:
                turn_qk(1)
            if now:
                project_q(1)
            if behind:
                turn_p(n, 0)
            if now:
                project_kv(1)
            if behind:
                turn_p(n, 1)
                weigh(n, 0, 1 - p)
                scores(2)
                weigh(n, 1, 1 - p)
                scores(3)
                turn_o(n, 0)
                turn_p(n, 2)
                out_project(n, 0)

        def t_steps(eng, step):
            step(0, True, False, False)
            step(1, True, True, False)
            step(2, True, True, True)
            with eng.Fori(3, B - 2, 2) as i:
                step(i, True, True, True)
                step(i + 1, True, True, True, odd=False)
            step(B - 1, True, True, True)
            step(B, False, True, True)
            step(B + 1, False, False, True)

        M = B // 2
        A_BANK = (4, 5, 1)
        FIRST, REST = range(2), range(2, HC)

        def f_sync(sp, l, i, odd=False, load_next=True):
            p = par_of(i, odd)
            m = l * M + i
            until(sp, G["xn"], 1 * (m - 1))
            if not isinstance(m, int):
                apart(sp)
            until(sp, G["yb"], 1 * (m - 1))
            if not isinstance(m, int):
                apart(sp)
            for k in range(2):
                b = 2 * i + k
                tt = slice(TPB * k, TPB * k + TPB)
                for c, row in ((0, 1), (1, 0)):
                    sp.dma_start(f_h[:, p, tt, 64 * c:64 * c + 64],
                                 y_d[2 * l + 1][bass.ds(b, 1), row:row + N, 64 * c:64 * c + 64].rearrange(
                                     "b (t p) d -> p (b t) d", p=P)).then_inc(G[f"in{p}"], 16)
                sp.dma_start(f_y[:, p, tt, :], y_d[2 * l + 1][bass.ds(b, 1), 1:ROWS, :].rearrange(
                    "b (t p) d -> p (b t) d", p=P)).then_inc(G[f"in{p}"], 16)
            if l == L - 1 and isinstance(i, int) and i < 2:
                f_x1_in(sp, i, odd)

        def f_x1_in(sp, i, odd):
            p = par_of(i, odd)
            for k in range(2):
                sp.dma_start(f_x1[:, p, TPB * k:TPB * k + TPB, :],
                             x1_d[bass.ds(2 * i + k, 1)].rearrange("b (t p) d -> p (b t) d", p=P)
                             ).then_inc(G[f"x1_in{p}"], 16)

        def f_in_count(l, i):
            return 96 * (M // 2 * l) + 96 * half_count(i)

        def f_store(sp, l, i, odd=False):
            p = par_of(i, odd)
            m = l * M + i
            src, ready = (f_o, "o") if l == L - 1 else (f_yn, "yn")
            until(sp, G[ready], i + 1 if l == L - 1 else m + 1)
            for k in range(2):
                tt = slice(TPB * k, TPB * k + TPB)
                if l == L - 1:
                    dst = out[bass.ds(2 * i + k, 1)]
                else:
                    dst = y_d[2 * l + 2][bass.ds(2 * i + k, 1), 1:ROWS, :]
                sp.dma_start(dst.rearrange("b (t p) d -> p (b t) d", p=P), src[:, p, tt, :]
                             ).then_inc(G[f"out{p}"], 16)
            if l == L - 1 and not (isinstance(i, int) and i + 2 >= M):
                f_x1_in(sp, i + 2, odd)

        def f_pool(pool, l, i, odd=False):
            p = par_of(i, odd)
            m = l * M + i
            inv_std(pool, f_ve[:], f_rs[:], f_mv[:, :, 1], G["mv"], m + 1, G["ve"], G["rs"])

        def f_pool_bias(pool, l, i, odd=False):
            p = par_of(i, odd)
            m = l * M + i
            until(pool, G["yn"], m - 1)
            nc.gpsimd.tensor_tensor(f_yb[:, p], f_y[:, p], b2_s[:, l, :].unsqueeze(1).broadcast_to([P, FT, D]),
                                    ALU.add).then_inc(G["yb"], 1)

        def f_pool_end(pool, l, i, odd=False):
            if l == L - 1:
                p = par_of(i, odd)
                inv_std(pool, f_ve2[:], f_rs2[:], f_mv2[:, :, 1], G["mv2"], i + 1, G["ve2"], G["rs2"])
                pool.wait_ge(G["ln"], i + 1)
                pool.wait_ge(G[f"x1_in{p}"], 32 * half_count(i))
                until(pool, G[f"out{p}"], 32 * (M // 2 * l) + 32 * (half_count(i) - 1))
                nc.gpsimd.tensor_tensor(f_o[:, p], f_ln[:], f_x1[:, p], ALU.add).then_inc(G["o"], 1)

        def f_act(act, l, i, odd=False):
            m = l * M + i
            for c in range(HC):
                w = HW[c]
                act.wait_ge(G["g_ps"], HC * m + c + 1)
                until(act, G["u"], HC * (m - 1) + c + 1)
                nc.scalar.activation(f_g[0:w, c, :], bank[2 + c % 2][0:w, :], ACT.Gelu,
                                     bias=b1_s[0:w, l, 1, c:c + 1]).then_inc(G["g"], 1)

        def f_dve_stats(dve, l, i, odd=False):
            p = par_of(i, odd)
            m = l * M + i
            dve.wait_ge(G[f"in{p}"], f_in_count(l, i))
            until(dve, G["rs"], m)
            stats(dve, f_h[:, p], f_st, f_mv, FT, G["st"], FT * (m + 1), G["mv"])

        def f_dve_in(dve, l, i, odd=False):
            p = par_of(i, odd)
            m = l * M + i
            dve.wait_ge(G["rs"], m + 1)
            until(dve, G["hT_ps"], m)
            for t in range(FT):
                j = normal(f_xn, f_h[:, p], f_mv, f_rs, t)
            j.then_inc(G["xn"], 1)

        def f_dve_turned(dve, l, i, odd=False):
            p = par_of(i, odd)
            m = l * M + i
            dve.wait_ge(G["hT_ps"], m + 1)
            until(dve, G["a_ps"], HC * (m - 1))
            nc.vector.tensor_scalar(f_hT[:, p, :], bank[0][:], lngb[:, l, 0:1], lngb[:, l, 1:2], ALU.mult, ALU.add
                                    ).then_inc(G["hT"], 1)

        def f_dve_gate(dve, l, i, chunks, odd=False):
            p = par_of(i, odd)
            m = l * M + i
            until(dve, G["w_ps"], m - 1)
            for c in chunks:
                w = HW[c]
                dve.wait_ge(G["g"], HC * m + c + 1)
                dve.wait_ge(G["a_ps"], HC * m + c + 1)
                nc.vector.scalar_tensor_tensor(out=f_u[0:w, p, c, :], in0=bank[A_BANK[c]][0:w, :],
                                               scalar=b1_s[0:w, l, 0, c:c + 1], in1=f_g[0:w, c, :],
                                               op0=ALU.add, op1=ALU.mult).then_inc(G["u"], 1)

        def f_dve_out(dve, l, i, odd=False):
            p = par_of(i, odd)
            m = l * M + i
            dve.wait_ge(G["yb"], m + 1)
            dve.wait_ge(G["w_ps"], m + 1)
            if l < L - 1:
                until(dve, G[f"out{p}"], 32 * (half_count(i) - 1) + 32 * (M // 2 * l))
            elif isinstance(i, int) and i < 2:
                until(dve, G[f"out{p}"], 32 * (M // 2 * l))
            nc.vector.tensor_tensor(f_yn[:, p].rearrange("p t d -> p (t d)"), f_yb[:, p].rearrange("p t d -> p (t d)"),
                                    bank[6 + p][:], ALU.add).then_inc(G["yn"], 1)
            if l == L - 1:
                dve.wait_ge(G["yn"], m + 1)
                until(dve, G["rs2"], i)
                stats(dve, f_yn[:, p], f_st2, f_mv2, FT, G["st2"], FT * (i + 1), G["mv2"])

        def f_dve_last(dve, l, i, odd=False):
            if l == L - 1:
                p = par_of(i, odd)
                dve.wait_ge(G["rs2"], i + 1)
                until(dve, G["o"], i)
                for t in range(FT):
                    j = normal(f_ln, f_yn[:, p], f_mv2, f_rs2, t)
                j.then_inc(G["ln"], 1)

        def f_pe_turn(pe, l, i, odd=False):
            m = l * M + i
            pe.wait_ge(G["xn"], m + 1)
            until(pe, G["hT"], m)
            for t in range(FT):
                j = nc.tensor.transpose(bank[0][:, t * P:(t + 1) * P], f_xn[:, t, :], ident[:])
            j.then_inc(G["hT_ps"], 1)

        def f_pe_up(pe, l, i, chunks, odd=False):
            p = par_of(i, odd)
            m = l * M + i
            pe.wait_ge(G["hT"], m + 1)
            for c in chunks:
                w = HW[c]
                k = HC * m + c
                until(pe, G["g"], k - 1 if c else k)
                nc.tensor.matmul(bank[2 + c % 2][0:w, :], w1_s[:, l, HID + c * P:HID + c * P + w], f_hT[:, p, :],
                                 start=True, stop=True).then_inc(G["g_ps"], 1)
                until(pe, G["u"], k - HC + 1)
                nc.tensor.matmul(bank[A_BANK[c]][0:w, :], w1_s[:, l, c * P:c * P + w], f_hT[:, p, :],
                                 start=True, stop=True).then_inc(G["a_ps"], 1)

        def f_pe_down(pe, l, i, odd=False):
            p = par_of(i, odd)
            m = l * M + i
            pe.wait_ge(G["u"], HC * (m + 1))
            until(pe, G["yn"], m - 1)
            for t in range(FT):
                for c in range(HC):
                    j = nc.tensor.matmul(bank[6 + p][:, t * P:(t + 1) * P], f_u[0:HW[c], p, c, t * P:(t + 1) * P],
                                         w2_s[0:HW[c], l, c, :], start=(c == 0), stop=(c == HC - 1))
            j.then_inc(G["w_ps"], 1)

        def f_steps(eng, *parts):
            def step(i, odd):
                for f, d in parts:
                    k = i + d
                    if not (isinstance(k, int) and not 0 <= k < M):
                        f(k, odd=odd ^ (d % 2 == 1))
            for i in range(-3, 3):
                step(i, i % 2 == 1)
            with eng.Fori(3, M - 4, 2) as i:
                step(i, True)
                step(i + 1, False)
            for i in range(M - 3, M + 1):
                step(i, i % 2 == 1)

        def phase(eng, k):
            eng.wait_ge(phase_end, k)

        @block.sync
        def _(sp):
            setup_sync(sp)
            steps(sp, lambda *a, **k: a_sync(sp, *a, **k), lambda part: late_loads(sp, part))
            for p in range(2):
                sp.wait_ge(A[f"out{p}"], 16 * B)
            sp.wait_ge(zero_out, 16 * 2 * L)
            sp.sem_inc(phase_end, 1)
            for l in range(L):
                phase(sp, 2 * l + 1)

                t_steps(sp, lambda *a, **k: t_sync(sp, l, *a, **k))
                for p in range(2):
                    sp.wait_ge(T[f"out{p}"], 8 * B * (l + 1))
                sp.sem_inc(phase_end, 1)
                phase(sp, 2 * l + 2)

                f_steps(sp, (lambda i, **k: f_sync(sp, l, i, **k), 3), (lambda i, **k: f_store(sp, l, i, **k), -1))
                for p in range(2):
                    sp.wait_ge(G[f"out{p}"], 32 * (M // 2) * (l + 1))
                sp.sem_inc(phase_end, 1)

        @block.gpsimd
        def _(pool):
            setup_gpsimd(pool)
            setup_done(pool)
            steps(pool, lambda *a, **k: a_pool(pool, *a, **k))
            late_done(pool)
            for l in range(L):
                phase(pool, 2 * l + 1)
                t_steps(pool, lambda *a, **k: t_pool(pool, l, *a, **k))
                phase(pool, 2 * l + 2)

                f_steps(pool, (lambda i, **k: f_pool(pool, l, i, **k), 2), (lambda i, **k: f_pool_bias(pool, l, i, **k), 1),
                        (lambda i, **k: f_pool_end(pool, l, i, **k), -1))

        @block.scalar
        def _(act):
            setup_done(act)
            steps(act, lambda *a, **k: a_act(act, *a, **k))
            late_done(act)
            for l in range(L):
                phase(act, 2 * l + 1)
                t_steps(act, lambda *a, **k: t_act(act, l, *a, **k))
                phase(act, 2 * l + 2)
                f_steps(act, (lambda i, **k: f_act(act, l, i, **k), 0))

        @block.vector
        def _(dve):
            setup_vector(dve)
            setup_done(dve)
            steps(dve, lambda *a, **k: a_dve(dve, *a, **k))
            setup_late(dve)
            late_done(dve)
            for l in range(L):
                phase(dve, 2 * l + 1)
                t_steps(dve, lambda *a, **k: t_dve(dve, l, *a, **k))
                phase(dve, 2 * l + 2)

                f_steps(dve, (lambda i, **k: f_dve_gate(dve, l, i, FIRST, **k), 0),
                        (lambda i, **k: f_dve_stats(dve, l, i, **k), 2), (lambda i, **k: f_dve_turned(dve, l, i, **k), 1),
                        (lambda i, **k: f_dve_out(dve, l, i, **k), -1), (lambda i, **k: f_dve_in(dve, l, i, **k), 2),
                        (lambda i, **k: f_dve_gate(dve, l, i, REST, **k), 0),
                        (lambda i, **k: f_dve_last(dve, l, i, **k), -1))

        @block.tensor
        def _(pe):
            setup_tensor(pe)
            setup_done(pe)
            steps(pe, lambda *a, **k: a_pe(pe, *a, **k))
            late_done(pe)
            for l in range(L):
                phase(pe, 2 * l + 1)
                t_steps(pe, lambda *a, **k: t_pe(pe, l, *a, **k))
                phase(pe, 2 * l + 2)

                f_steps(pe, (lambda i, **k: f_pe_up(pe, l, i, FIRST, **k), 0), (lambda i, **k: f_pe_down(pe, l, i, **k), -1),
                        (lambda i, **k: f_pe_turn(pe, l, i, **k), 1), (lambda i, **k: f_pe_up(pe, l, i, REST, **k), 0))


_INS = ["L0_attn_x", "L0_attn_w_qkv", "L0_attn_w_out", "L0_attn_b_out", "L0_attn_random_features", "L0_ffn_wqkv",
        "L0_ffn_q_scale", "L0_ffn_k_scale", "L0_ffn_wo", "L0_ffn_ln_g", "L0_ffn_ln_b", "L0_ffn_w1", "L0_ffn_b1",
        "L0_ffn_w2", "L0_ffn_b2"]


def kernel(**inputs):
    import numpy as _np
    import concourse.bacc as _bacc
    from concourse import mybir as _mybir
    from concourse.bass_utils import run_bass_kernel_spmd as _run

    nc = _bacc.Bacc("TRN2", target_bir_lowering=False, num_devices=1)
    arrays, args = {}, []
    for name in _INS:
        a = _np.ascontiguousarray(inputs[name])
        arrays[f"in_{name}"] = a
        args.append(nc.dram_tensor(f"in_{name}", a.shape, _mybir.dt.from_np(a.dtype), kind="ExternalInput").ap())
    shape = inputs["L0_attn_x"].shape
    args.append(nc.dram_tensor("out_0", shape, _mybir.dt.float32, kind="ExternalOutput").ap())
    build(nc, *args)
    r = _run(nc, [arrays], core_ids=[0])
    return r.results[0]["out_0"]
```
